# Optimizing a Trainium2 kernel written in Bass

```python
import numpy as np
import jax
import jax.numpy as jnp

def _softmax(x, axis=-1):
    return jax.nn.softmax(x, axis=axis)

def _gelu(x):
    return jax.nn.gelu(x, approximate=True)

def _silu(x):
    return jax.nn.silu(x)

def _sigmoid(x):
    return jax.nn.sigmoid(x)

def _layernorm(x, axis=-1, eps=1e-05):
    m = jnp.mean(x, axis=axis, keepdims=True)
    v = jnp.var(x, axis=axis, keepdims=True)
    return (x - m) / jnp.sqrt(v + eps)

def _scatter_add(tgt, idx, src, axis=0):
    return tgt.at[idx].add(src)

def _segment_sum(src, seg, n):
    return jax.ops.segment_sum(src, seg, n)
kernel_name = 'mk_decoder_preln_d1_seqx_r2_480bf8'

def setup_inputs(seed: int=0):
    np.random.seed(seed)
    _w = jnp.asarray

    def _rec_inputs():
        import jax
        import jax.numpy as jnp
        _rk = jax.random.key(seed)
        x = -0.0002928 + 1 * jax.random.normal(jax.random.fold_in(_rk, 1), (8, 1024, 512), jnp.float32)
        _lenS = 1024 - jax.random.randint(jax.random.fold_in(_rk, 7), (8,), 0, max(1, 1024 // 4) + 1, jnp.int32)
        _lenS2 = 64 - jax.random.randint(jax.random.fold_in(_rk, 8), (8,), 0, max(1, 64 // 4) + 1, jnp.int32)
        _ctx_1024P = jax.random.normal(jax.random.fold_in(_rk, 11), (8, 16, 512), jnp.float32)
        _ctx_1024c = jax.random.dirichlet(jax.random.fold_in(_rk, 511), 0.3 * jnp.ones((16,), jnp.float32), (8, 64))
        _ctx_1024t = jnp.einsum('bsk,bkd->bsd', _ctx_1024c, _ctx_1024P)
        _ctx_1024t = _ctx_1024t * jax.lax.rsqrt(jnp.mean(jnp.square(_ctx_1024t)) + 1e-12) * 0.953939
        ctx_1024 = -1.39393e-06 + 0.999914 * (_ctx_1024t + 0.3 * jax.random.normal(jax.random.fold_in(_rk, 611), (8, 64, 512), jnp.float32))
        _validS = jnp.arange(1024)[None, :] < _lenS[:, None]
        _validS2 = jnp.arange(64)[None, :] < _lenS2[:, None]
        _causal = jnp.tril(jnp.ones((1024, 1024), dtype=bool))
        mask_BxS2_ik0 = jnp.where(jnp.broadcast_to(_validS2[:, :], (8, 64)), 0, 1).astype(jnp.int32)
        return (x, ctx_1024, mask_BxS2_ik0)
    x, ctx_1024, mask_BxS2_ik0 = _rec_inputs()

    def _L0_attn_setup():
        import jax, jax.numpy as jnp
        import numpy as np
        T, N, D, H = (128, 128, 512, 512)
        LR = 0.001

        def _recon(params, z):
            W1, b1, W2, b2 = params
            h = jax.nn.gelu(z @ W1.T + b1, approximate=False)
            return z + h @ W2.T + b2
        key = jax.random.key(seed)
        ks = jax.random.split(key, 6)
        sd = 1.0 / np.sqrt(D)
        sh = 1.0 / np.sqrt(H)
        s4 = 1.0 / np.sqrt(H // 4)
        return {'in_seq': jax.random.normal(ks[0], (T, N, D), jnp.float32), 't_k': jax.random.normal(ks[1], (H, D), jnp.float32) * sd, 't_v': jax.random.normal(ks[2], (H, D), jnp.float32) * sd, 't_q': jax.random.normal(ks[3], (H, D), jnp.float32) * sd, 'W1': jax.random.normal(ks[4], (H // 4, H), jnp.float32) * sh, 'b1': jnp.zeros((H // 4,), jnp.float32), 'W2': jax.random.normal(ks[5], (H, H // 4), jnp.float32) * s4, 'b2': jnp.zeros((H,), jnp.float32)}
    _L0_attn_all = _L0_attn_setup()
    _L0_attn_in = {k: v for k, v in _L0_attn_all.items() if k in ('t_k', 't_v', 't_q', 'W1', 'b1', 'W2', 'b2')}
    del _L0_attn_all

    def _L0_xattn_setup():
        import jax, jax.numpy as jnp
        import numpy as np
        B, SQ, SKV, D, H = (2, 1024, 1024, 512, 16)
        W = D // H

        def _heads(x):
            b, s, _ = x.shape
            return x.reshape(b, s, H, W).transpose(0, 2, 1, 3)
        key = jax.random.key(seed)
        ks = jax.random.split(key, 10)
        s = 1.0 / np.sqrt(D)
        return {'x_q': jax.random.normal(ks[0], (B, SQ, D), jnp.float32), 'x_k': jax.random.normal(ks[1], (B, SKV, D), jnp.float32), 'x_v': jax.random.normal(ks[2], (B, SKV, D), jnp.float32), 'mask': jax.random.randint(ks[3], (B, SKV), 0, 2, jnp.int32), 'Wq': jax.random.normal(ks[4], (D, D), jnp.float32) * s, 'bq': jnp.zeros((D,), jnp.float32), 'Wk': jax.random.normal(ks[5], (D, D), jnp.float32) * s, 'bk': jnp.zeros((D,), jnp.float32), 'Wv': jax.random.normal(ks[6], (D, D), jnp.float32) * s, 'bv': jnp.zeros((D,), jnp.float32)}
    _L0_xattn_all = _L0_xattn_setup()
    _L0_xattn_in = {k: v for k, v in _L0_xattn_all.items() if k in ('Wq', 'bq', 'Wk', 'bk', 'Wv', 'bv')}
    del _L0_xattn_all

    def _L0_ffn_setup():
        import jax, jax.numpy as jnp
        import numpy as np
        EMB = 512
        FF = 4 * EMB

        def _ternary(w):
            scale = jnp.maximum(jnp.mean(jnp.abs(w)), 1e-08)
            w_t = jnp.clip(jnp.round(w / scale), -1.0, 1.0)
            return w + jax.lax.stop_gradient(w_t - w)
        key = jax.random.key(seed)
        kx, k1, k2, kb1, kb2 = jax.random.split(key, 5)
        x = jax.random.normal(kx, (4, 1024, EMB), dtype=jnp.float32)
        lim1 = 1.0 / np.sqrt(EMB)
        lim2 = 1.0 / np.sqrt(FF)
        W1 = jax.random.uniform(k1, (FF, EMB), jnp.float32, -lim1, lim1)
        b1 = jax.random.uniform(kb1, (FF,), jnp.float32, -lim1, lim1)
        W2 = jax.random.uniform(k2, (EMB, FF), jnp.float32, -lim2, lim2)
        b2 = jax.random.uniform(kb2, (EMB,), jnp.float32, -lim2, lim2)
        return {'x': x, 'W1': W1, 'b1': b1, 'W2': W2, 'b2': b2}
    _L0_ffn_all = _L0_ffn_setup()
    _L0_ffn_in = {k: v for k, v in _L0_ffn_all.items() if k in ('W1', 'b1', 'W2', 'b2')}
    del _L0_ffn_all
    return {'x': x, 'ctx_1024': ctx_1024, 'mask_BxS2_ik0': mask_BxS2_ik0, 'L0_attn_t_k': _L0_attn_in['t_k'], 'L0_attn_t_v': _L0_attn_in['t_v'], 'L0_attn_t_q': _L0_attn_in['t_q'], 'L0_attn_W1': _L0_attn_in['W1'], 'L0_attn_b1': _L0_attn_in['b1'], 'L0_attn_W2': _L0_attn_in['W2'], 'L0_attn_b2': _L0_attn_in['b2'], 'L0_xattn_Wq': _L0_xattn_in['Wq'], 'L0_xattn_bq': _L0_xattn_in['bq'], 'L0_xattn_Wk': _L0_xattn_in['Wk'], 'L0_xattn_bk': _L0_xattn_in['bk'], 'L0_xattn_Wv': _L0_xattn_in['Wv'], 'L0_xattn_bv': _L0_xattn_in['bv'], 'L0_ffn_W1': _L0_ffn_in['W1'], 'L0_ffn_b1': _L0_ffn_in['b1'], 'L0_ffn_W2': _L0_ffn_in['W2'], 'L0_ffn_b2': _L0_ffn_in['b2']}

def reference(x, ctx_1024, mask_BxS2_ik0, L0_attn_t_k, L0_attn_t_v, L0_attn_t_q, L0_attn_W1, L0_attn_b1, L0_attn_W2, L0_attn_b2, L0_xattn_Wq, L0_xattn_bq, L0_xattn_Wk, L0_xattn_bk, L0_xattn_Wv, L0_xattn_bv, L0_ffn_W1, L0_ffn_b1, L0_ffn_W2, L0_ffn_b2):
    import jax
    import jax.numpy as jnp

    def _L0_attn_ref(in_seq, t_k, t_v, t_q, W1, b1, W2, b2):
        import jax, jax.numpy as jnp
        import numpy as np
        T, N, D, H = (128, 128, 512, 512)
        LR = 0.001

        def _recon(params, z):
            W1, b1, W2, b2 = params
            h = jax.nn.gelu(z @ W1.T + b1, approximate=False)
            return z + h @ W2.T + b2

        def loss_fn(params, z, y):
            return jnp.mean((_recon(params, z) - y) ** 2)

        def step(params, x):
            z = x @ t_k.T
            y = x @ t_v.T
            grads = jax.grad(loss_fn)(params, z, y)
            new_params = jax.tree_util.tree_map(lambda p, g: jax.lax.stop_gradient(p - LR * g), params, grads)
            out = _recon(new_params, x @ t_q.T)
            return (new_params, out)
        _, outs = jax.lax.scan(step, (W1, b1, W2, b2), in_seq)
        return outs

    def _L0_xattn_ref(x_q, x_k, x_v, mask, Wq, bq, Wk, bk, Wv, bv):
        import jax, jax.numpy as jnp
        import numpy as np
        B, SQ, SKV, D, H = (2, 1024, 1024, 512, 16)
        W = D // H

        def _heads(x):
            b, s, _ = x.shape
            return x.reshape(b, s, H, W).transpose(0, 2, 1, 3)
        q = _heads(x_q @ Wq.T + bq)
        k = _heads(x_k @ Wk.T + bk)
        v = _heads(x_v @ Wv.T + bv)
        scores = jnp.einsum('bhqw,bhkw->bhqk', q, k) / np.sqrt(W).astype(np.float32)
        m = mask[:, None, None, :].astype(scores.dtype)
        scores = scores - 10000.0 * (1.0 - m)
        p = jax.nn.softmax(scores, axis=-1)
        h = jnp.einsum('bhqk,bhkw->bhqw', p, v)
        return h.transpose(0, 2, 1, 3).reshape(x_q.shape[0], x_q.shape[1], D)

    def _L0_ffn_ref(x, W1, b1, W2, b2):
        import jax, jax.numpy as jnp
        import numpy as np
        EMB = 512
        FF = 4 * EMB

        def _ternary(w):
            scale = jnp.maximum(jnp.mean(jnp.abs(w)), 1e-08)
            w_t = jnp.clip(jnp.round(w / scale), -1.0, 1.0)
            return w + jax.lax.stop_gradient(w_t - w)
        h = jnp.einsum('bsd,fd->bsf', x, _ternary(W1)) + b1
        h = jax.nn.gelu(h, approximate=False)
        out = jnp.einsum('bsf,df->bsd', h, _ternary(W2)) + b2
        return out
    x = x + _L0_attn_ref(_layernorm(x, axis=-1), L0_attn_t_k, L0_attn_t_v, L0_attn_t_q, L0_attn_W1, L0_attn_b1, L0_attn_W2, L0_attn_b2)
    x = x + _L0_xattn_ref(_layernorm(x, axis=-1), ctx_1024, ctx_1024, mask_BxS2_ik0, L0_xattn_Wq, L0_xattn_bq, L0_xattn_Wk, L0_xattn_bk, L0_xattn_Wv, L0_xattn_bv)
    x = x + _L0_ffn_ref(_layernorm(x, axis=-1), L0_ffn_W1, L0_ffn_b1, L0_ffn_W2, L0_ffn_b2)
    return x

_drawn_inputs = setup_inputs


def setup_inputs(seed=0):
    import zlib

    import numpy as np

    out = dict(_drawn_inputs(seed))
    spreads = {'L0_attn_b1': (0.0, 0.1),
     'L0_attn_b2': (0.0, 0.1),
     'L0_xattn_bq': (0.0, 0.455),
     'L0_xattn_bk': (0.0, 2.0),
     'L0_xattn_bv': (0.0, 0.1)}
    factors = {'L0_attn_t_k': 64.0, 'L0_attn_t_v': 64.0, 'L0_ffn_b1': 45.128, 'L0_ffn_b2': 64.0}
    for name, (base, spread) in spreads.items():
        noise = np.random.default_rng([zlib.crc32(name.encode()), seed]).standard_normal(out[name].shape)
        drawn = base * np.exp(spread * noise) if base else spread * noise
        out[name] = jnp.asarray(drawn.astype(out[name].dtype))
    for name, factor in factors.items():
        out[name] = (out[name] * factor).astype(out[name].dtype)
    return out
```

```python
import math
from contextlib import ExitStack

import concourse.bass as bass
from concourse import mybir

F32, F16, BF16, F8, I32 = (mybir.dt.float32, mybir.dt.float16, mybir.dt.bfloat16, mybir.dt.float8e4, mybir.dt.int32)
ALU = mybir.AluOpType
ACT = mybir.ActivationFunctionType
AX = mybir.AxisListType

P = 128
B, N, D = 8, 1024, 512
HID = 128
HEADS, W, KEYS = 16, 32, 64
FF = 4 * D
C = D // P
G2, T4 = 2, 4
GT = T4 * P
TILES = G2 * T4
FCH = FF // P
PAIRS = HEADS // 2
WSCALE = 256.0
LR = 0.001
ETA = LR * 2.0 / (N * D)
EPS = 1e-5
MASKED = 10000.0
TINY = 1e-15
INV_SQRT_2PI = (2.0 * math.pi) ** -0.5
SQW = float(W) ** 0.5
HI, LO = 0, 1
PASSES = ((HI, HI), (HI, LO), (LO, HI))
NAT = 2 * HID + 2

RINGS = {"M": 4, "O": 2, "T": 2, "S": 3}
USES = {
    "K": {"M": 4}, "KQ": {"M": 4}, "DT": {"M": 4}, "TQT": {"M": 4}, "W1T": {"M": 1}, "AINIT": {"M": 2},
    "W2T0": {"M": 1}, "WQT": {"M": 4}, "WKT": {"M": 4}, "WVT": {"M": 4}, "CTXT": {"M": 4}, "KCTX": {"M": 4},
    "VCTX": {"M": 4}, "MEAN": {"M": 1}, "TERN": {"T": 8},
    "L1": {"S": 4}, "T1": {"T": 4}, "PRE": {"M": 1, "S": 1}, "DH": {"M": 1}, "HT": {"T": 4}, "S": {"M": 5},
    "U1": {"M": 4}, "U2": {"M": 1}, "U3": {"M": 2}, "A3P": {"M": 1, "S": 1}, "A3O": {"O": 4},
    "L2": {"S": 4}, "T2": {"T": 4}, "Q": {"M": 4, "S": 4}, "GUARD": {"O": 8}, "GT": {"T": 1},
    "ST": {"M": 8, "S": 8}, "PV": {"O": 8}, "L3": {"S": 4}, "T3": {"T": 4}, "F1": {"M": 16, "S": 16},
    "F2": {"O": 4},
}


def units(text):
    return [(w.rstrip("01") if w[-2:-1] == "." else w, int(w[-1]) if w[-2:-1] == "." else 0) for w in text.split()]


def schedule(text):
    return [(name.rstrip("."), g) for name, g in units(text)]


SETUP = schedule("K KQ DT TQT W1T AINIT W2T0 U3 CTXT WKT WVT WQT KCTX VCTX MEAN.0 TERN.0 MEAN.1 TERN.1")
FIRST = schedule("L1.0 L1.1 T1.0 T1.1 PRE.0 PRE.1 DH.0 DH.1 HT.0 HT.1 S U1 U2 U3 "
                 "A3P.0 A3O.0 L2.0 T2.0 A3P.1 A3O.1")
BODY = schedule("Q.0 L1.0 GUARD.0 GT.0 L1.1 ST.0 PV.0 L3.0 T1.0 T1.1 PRE.0 PRE.1 DH.0 DH.1 T3.0 HT.0 HT.1 S U1 "
                "F1.0 U2 U3 L2.1 T2.1 F2.0 Q.1 A3P.0 GUARD.1 GT.1 A3O.0 ST.1 PV.1 L3.1 A3P.1 T3.1 L2.0 "
                "F1.1 T2.0 F2.1 A3O.1")
LAST = schedule("Q.0 GUARD.0 GT.0 ST.0 PV.0 L3.0 T3.0 F1.0 L2.1 T2.1 F2.0 Q.1 GUARD.1 GT.1 ST.1 PV.1 L3.1 "
                "T3.1 F1.1 F2.1")
STREAM_X = {("L2", 1), ("T2", 1)} | {(u, g) for u in ("Q", "GUARD", "GT", "ST", "PV", "L3", "T3", "F1", "F2")
                                     for g in range(G2)}


class Use:

    def __init__(self, slot, before, full, done):
        self.slot, self.before, self.full, self.done = slot, before, full, done
        self.reused = not (isinstance(before, int) and before == 0)


class Phase:

    def __init__(self, order, base):
        self.order, self.base, self.place = order, base, {}
        self.total = {r: [0] * n for r, n in RINGS.items()}
        count = {r: 0 for r in RINGS}
        for unit in order:
            for ring, n in USES[unit[0]].items():
                for i in range(n):
                    slot = count[ring] % RINGS[ring]
                    self.place[unit, ring, i] = (slot, count[ring] if ring == "S" else self.total[ring][slot])
                    self.total[ring][slot] += 1
                    count[ring] += 1
        self.count = count
        self.turn = 0

    def start(self, ring, slot):
        if ring == "S":
            return self.turn * self.count["S"] + self.base["S"][0]
        return self.turn * self.total[ring][slot] + self.base[ring][slot]

    def after(self, turns):
        base = {r: [b + turns * t for b, t in zip(self.base[r], self.total[r])] for r in RINGS}
        base["S"] = [self.base["S"][0] + turns * self.count["S"]] * RINGS["S"]
        return base


def build(nc, x, ctx_in, mask, t_k, t_v, t_q, w1, b1, w2, b2, wq, bq, wk, bk, wv, bv, fw1, fb1, fw2, fb2, out):
    setup = Phase(SETUP, {r: [0] * n for r, n in RINGS.items()})
    first = Phase(FIRST, setup.after(1))
    body = Phase(BODY, first.after(1))
    last = Phase(LAST, body.after(B - 1))

    with ExitStack() as stack:
        def sb(name, shape, dt):
            return stack.enter_context(nc.sbuf_tensor(name, shape, dt))

        def sem(name):
            return stack.enter_context(nc.semaphore(name))

        k_scr = nc.dram_tensor("k_scr", (B, P, 2, C, KEYS), F16).ap()
        v_scr = nc.dram_tensor("v_scr", (B, KEYS, 2, D), F16).ap()
        mb_scr = nc.dram_tensor("mb_scr", (B, P, 1), F32).ap()
        mr_scr = nc.dram_tensor("mr_scr", (B, 1, KEYS), F16).ap()
        dn_scr = nc.dram_tensor("dn_scr", (P, C, D), F32).ap()
        dt_scr = nc.dram_tensor("dt_scr", (P, C, D), F32).ap()

        psT = stack.enter_context(nc.psum_tensor("psT", [P, 2, 1024], F16))
        psM = stack.enter_context(nc.psum_tensor("psM", [P, 4, 512], F32))
        psO = stack.enter_context(nc.psum_tensor("psO", [P, 2, 512], F32))

        id16, idbf, id32 = sb("id16", [P, P], F16), sb("idbf", [P, P], BF16), sb("id32", [P, P], F32)
        ones32 = sb("ones32", [P, P], F32)
        ones_row = sb("ones_row", [1, P], F16)
        neg_ind = sb("neg_ind", [HEADS, PAIRS * P], BF16)
        neghalf = sb("neghalf", [P, T4], F32)
        fw1T = sb("fw1T", [P, C, FF], F8)
        fw2T = sb("fw2T", [P, FCH, D], F8)
        tqT = sb("tqT", [P, 2, C, D], F16)
        wqT = sb("wqT", [P, 2, C, D], F16)
        kk = sb("kk", [P, C, D], F32)
        kq = sb("kq", [P, C, D], F32)
        dd = sb("dd", [P, C, D], F32)
        b1c = sb("b1c", [P, 1], F32)
        cc = sb("cc", [P, 1], F32)
        bqc, bkc, fb1c = sb("bqc", [P, C], F32), sb("bkc", [P, C], F32), sb("fb1c", [P, FCH], F32)
        b2b, fb2b = sb("b2b", [P, D], F32), sb("fb2b", [P, D], F32)

        A32, Aq32 = sb("A32", [P, C, HID], F32), sb("Aq32", [P, C, HID], F32)
        A16, Aq16 = sb("A16", [P, 2, C, HID], F16), sb("Aq16", [P, 2, C, HID], F16)
        P16, G16 = sb("P16", [P, 2, C, HID], F16), sb("G16", [P, 2, HID], F16)
        w2T32, w2T16 = sb("w2T32", [P, D], F32), sb("w2T16", [P, 2, D], F16)

        kbd = sb("kbd", [P, 2, C, 4 * KEYS], F16)
        vbd = sb("vbd", [P, 2, PAIRS, 2 * (W + 1)], F16)
        mbc = sb("mbc", [P, 1], F32)
        mrow = sb("mrow", [1, KEYS], F16)

        xin = sb("xin", [P, TILES, D], F32)
        x1 = sb("x1", [P, TILES, D], F32)
        xn1 = sb("xn1", [P, 2, TILES, D], F16)
        xT1 = sb("xT1", [P, 2 * C, N], F16)
        xnX = sb("xnX", [P, 2, T4, D], F16)
        xTX = sb("xTX", [P, 2 * C, GT], F16)
        arena = sb("arena", [P, 16384], F16)
        stage = sb("stage", [P, RINGS["S"], 512], F32)
        obuf = sb("obuf", [P, 2, 8, W], F32)
        rden = sb("rden", [P, 2, 8], F32)
        gm = sb("gm", [P, T4, HEADS], BF16)
        gT = sb("gT", [HEADS, GT], BF16)
        st = sb("st", [P, 3, T4, 6], F32)
        mv = sb("mv", [P, 3, T4, 2], F32)
        ve = sb("ve", [P, 3, T4], F32)
        rs = sb("rs", [P, 3, G2, T4], F32)
        nm = sb("nm", [P, 3, G2, T4], F32)
        mci = sb("mci", [P, B], I32)
        mx = sb("mx", [P, B], F32)
        mcf = sb("mcf", [P, B], F32)
        mr16 = sb("mr16", [1, B, KEYS], F16)
        asum = sb("asum", [P, 2], F32)
        thr = sb("thr", [P, 2, 3], F32)

        def part(buf, start, shape, dt, rows=P):
            size = 1
            for s in shape:
                size *= s
            nbytes = size * (4 if dt in (F32, I32) else 2)
            v = buf[0:rows, start // 2:(start + nbytes) // 2]
            if dt != F16:
                v = v.bitcast(dt)
            if len(shape) == 2:
                v = v.rearrange("p (a c) -> p a c", a=shape[0])
            if len(shape) == 3:
                v = v.rearrange("p (a e c) -> p a e c", a=shape[0], e=shape[1])
            return v

        nat = part(arena, 0, [TILES, 2, NAT], F16)
        o = TILES * 2 * NAT * 2
        hT = part(arena, o, [G2, 2, GT], F16)
        dpT = part(arena, o + 4096, [G2, 2, GT], F16)
        gp = part(arena, o + 8192, [G2, GT], F32)
        s12 = part(arena, o + 12288, [C, NAT], F32)
        o += 12288 + C * NAT * 4
        s3 = part(arena, o, [132], F32)
        sxb = part(arena, o + 528, [C, P], F32)
        tb = part(arena, o + 528, [D], F32)
        s4b = part(arena, o + 528 + 2048, [P], F32)
        tw = part(arena, o + 528 + 2048 + 512, [D], F32)
        assert o + 528 + 2048 + 512 + 2048 <= 32768
        un = part(arena, o - C * NAT * 4, [G2, GT], F32)
        ee = part(arena, o - C * NAT * 4 + 4096, [G2, GT], F32)
        es = part(arena, 0, [2, PAIRS, GT], F16)
        qs = part(arena, 24576, [2, C, GT], F16)
        hF = part(arena, 0, [FCH, 2, GT], F16)
        h2 = obuf[:, :, :, :].rearrange("p a h w -> p (a h w)").bitcast(F16).rearrange("p (a t) -> p a t", a=2)
        w2n = part(xnX[:, :, :, :].rearrange("p a t d -> p (a t d)"), 0, [C, HID], F32)

        xn1f = xn1[:, :, :, :].rearrange("p a t d -> p (a t d)")
        xT1f = xT1[:, :, :].rearrange("p a d -> p (a d)")
        xnXf = xnX[:, :, :, :].rearrange("p a t d -> p (a t d)")
        xTXf = xTX[:, :, :].rearrange("p a d -> p (a d)")
        x1f = x1[:, :, :].rearrange("p a d -> p (a d)")
        tk, tq = part(xn1f, 0, [C, D], F32), part(xn1f, 8192, [C, D], F32)
        dn = part(xT1f, 0, [C, D], F32)
        w1s, w1T = part(xT1f, 8192, [D], F32), part(xT1f, 10240, [C, HID], F32)
        wqs, wks = part(arena, 0, [C, D], F32), part(arena, 8192, [C, D], F32)
        wvs, ctxs = part(arena, 16384, [C, D], F32), part(arena, 24576, [C, D], F32)
        wkT, wvT = x1[:, 0:C, :], x1[:, C:2 * C, :]
        ctxT = part(xTXf, 0, [C, D], F32)
        mi = part(xnXf, 4096, [B * KEYS], I32)
        kTs = part(xnXf, 0, [2, C, D], F16)
        vs = part(arena, 24576, [C, 2, D], F16)
        bvb, v32 = stage[:, 0, :], stage[:, 1, :]
        ffs = part(arena, 0, [FF * D // P], F32)
        junk = xn1f
        tern = x1f.bitcast(F16)[:, 0:FF * D // P]

        full = {r: [sem(f"{r}{i}_filled") for i in range(n)] for r, n in RINGS.items() if r != "S"}
        done = {r: [sem(f"{r}{i}_emptied") for i in range(n)] for r, n in RINGS.items() if r != "S"}
        staged = sem("xhat_staged")
        hi_done = sem("hi_done")
        split = sem("split_done")
        consts, idents = sem("consts"), sem("idents")
        ld = {n: sem(f"load_{n}") for n in ("tk", "tq", "tv", "w1", "w2", "small", "wq", "wk", "wv", "ctx",
                                            "mask", "fw")}
        x_loaded = [sem(f"x_loaded{g}") for g in range(G2)]
        scr_stored = sem("scratch_stored")
        ctx_loaded = sem("ctx_loaded")
        dd_loaded = sem("dd_loaded")
        out_stored = [sem(f"out_stored{t}") for t in range(TILES)]
        d_ready = sem("d_ready")
        wt_hi = sem("weight_hi")
        init = sem("state_init")
        kv_hi = sem("kv_hi")
        v_split = sem("v_split")
        mask_step = sem("mask_step")
        abs_done, thr_step, tern_step = sem("abs_done"), sem("thr_step"), sem("tern_step")
        bn = [sem(f"ln{k}_bn") for k in (1, 2, 3)]
        stats = [sem(f"ln{k}_stats") for k in (1, 2, 3)]
        vep = [sem(f"ln{k}_var_eps") for k in (1, 2, 3)]
        rstd = [sem(f"ln{k}_rstd") for k in (1, 2, 3)]
        nmr = [sem(f"ln{k}_shift") for k in (1, 2, 3)]
        u_step = sem("u_step")
        e_step = sem("exp_step")
        h_staged = sem("h_staged")
        gp_step = sem("gp_step")
        gp_ready, dp_hi, dp_split = sem("gp_ready"), sem("dp_hi"), sem("dp_split")
        ones_set = sem("ones_set")
        bc_ready = sem("sums_broadcast")
        u1 = sem("update_step")
        u3 = sem("pg_hi")
        xa_done = sem("x_plus_b2")
        o_done = sem("attn_added")
        xf_done = sem("x_plus_fb2")
        rd = sem("denominators")
        passed = sem("passed")
        U1_STEPS = 10

        def use(ph, unit, ring, i):
            slot, nth = ph.place[unit, ring, i]
            before = ph.start(ring, slot) + nth
            if ring == "S":
                return Use(slot, before, None, split)
            return Use(slot, before, full[ring][slot], done[ring][slot])

        def held(eng, waits):
            for sm, n in waits:
                eng.wait_ge(sm, n)
            eng.sem_inc(passed, 1)

        def run(eng, unit_programs):
            for ph, b in ((setup, 0), (first, 0)):
                for name, g in ph.order:
                    if name in unit_programs:
                        unit_programs[name](ph, b, g)
            with eng.Fori(1, B) as b:
                body.turn = b - 1
                if "START" in unit_programs:
                    unit_programs["START"](body, b, 0)
                for name, g in BODY:
                    if name in unit_programs:
                        unit_programs[name](body, b - 1 if (name, g) in STREAM_X else b, g)
            if "START" in unit_programs:
                unit_programs["START"](last, B, 0)
            for name, g in LAST:
                if name in unit_programs:
                    unit_programs[name](last, B - 1, g)

        block = stack.enter_context(nc.Block())

        @block.sync
        def _(sp):
            rows = "(j p) d -> p j d"
            sp.dma_start(tk, t_k.rearrange(rows, p=P)).then_inc(ld["tk"], 16)
            sp.dma_start(tq, t_q.rearrange(rows, p=P)).then_inc(ld["tq"], 16)
            sp.dma_start(dn, t_v.rearrange(rows, p=P)).then_inc(ld["tv"], 16)
            sp.dma_start(w1s, w1).then_inc(ld["w1"], 16)
            sp.dma_start(w2n, w2.rearrange("(j p) h -> p j h", p=P)).then_inc(ld["w2"], 16)
            small = [(b1c[:, :], b1.rearrange("(p a) -> p a", a=1)), (b2b[:, :], b2.partition_broadcast(P)),
                     (fb2b[:, :], fb2.partition_broadcast(P)), (bvb, bv.partition_broadcast(P)),
                     (bqc[:, :], bq.rearrange("(m p) -> p m", p=P)), (bkc[:, :], bk.rearrange("(m p) -> p m", p=P)),
                     (fb1c[:, :], fb1.rearrange("(m p) -> p m", p=P))]
            for dst, src in small:
                sp.dma_start(dst, src, allow_slow_non_contiguous=True).then_inc(ld["small"], 16)
            sp.dma_start(ctxs, ctx_in.rearrange("b k d -> (b k) d").rearrange(rows, p=P)).then_inc(ld["ctx"], 16)
            sp.dma_start(wks, wk.rearrange(rows, p=P)).then_inc(ld["wk"], 16)
            sp.dma_start(wvs, wv.rearrange(rows, p=P)).then_inc(ld["wv"], 16)
            sp.dma_start(wqs, wq.rearrange(rows, p=P)).then_inc(ld["wq"], 16)
            sp.dma_start(mi, mask.rearrange("b k -> (b k)").partition_broadcast(P)).then_inc(ld["mask"], 16)
            for j in range(2):
                sp.dma_start(mci[j * KEYS:(j + 1) * KEYS, :], mask.rearrange("b k -> k b"),
                             allow_slow_non_contiguous=True).then_inc(ld["mask"], 16)
            for g in range(G2):
                sp.dma_start(xin[:, g * T4:(g + 1) * T4, :],
                             x[0, g * GT:(g + 1) * GT, :].rearrange("(t p) d -> p t d", p=P)).then_inc(x_loaded[g], 16)
            stores = 0
            sp.wait_ge(mask_step, 7)
            sp.dma_start(mb_scr.rearrange("b p a -> p (b a)"), mcf[:, :], allow_slow_non_contiguous=True).then_inc(scr_stored, 16)
            sp.dma_start(mr_scr.rearrange("b a k -> a b k"), mr16[:, :, :]).then_inc(scr_stored, 16)
            sp.wait_ge(d_ready, 1)
            sp.dma_start(dn_scr, dn).then_inc(scr_stored, 16)
            for c in range(C):
                u = use(setup, ("DT", 0), "M", c)
                sp.wait_ge(u.done, u.before + 1)
            sp.dma_start(dt_scr, dd[:, :, :]).then_inc(scr_stored, 16)
            for m in range(C):
                u = use(setup, ("KCTX", 0), "M", m)
                sp.wait_ge(u.done, u.before + 1)
            for b in range(B):
                sp.dma_start(k_scr[b], kTs[:, :, :, b * KEYS:(b + 1) * KEYS]).then_inc(scr_stored, 16)
            sp.wait_ge(v_split, C)
            for b in range(B):
                half = (b % 2) * KEYS
                sp.dma_start(v_scr[b], vs[half:half + KEYS, b // 2, :, :]).then_inc(scr_stored, 16)
            stores = 16 * (4 + 2 * B)
            sp.wait_ge(scr_stored, stores)
            u = use(setup, ("WQT", 0), "M", C - 1)
            sp.wait_ge(u.full, u.before + 1)
            sp.dma_start(ffs.rearrange("p (m d) -> p m d", d=D), fw1.rearrange("(m p) d -> p m d", p=P)).then_inc(ld["fw"], 16)
            sp.wait_ge(tern_step, 2)
            sp.wait_ge(abs_done, 1)
            sp.dma_start(ffs.rearrange("p (m f) -> p m f", f=FF), fw2.rearrange("(m p) f -> p m f", p=P)).then_inc(ld["fw"], 16)

            def load_start(ph, b, g):
                for s in range(2):
                    sp.wait_ge(done["O"][s], ph.start("O", s))
                for hh in range(4):
                    sp.dma_start(kbd[hh * W:(hh + 1) * W, :, :, hh * KEYS:(hh + 1) * KEYS],
                                 k_scr[b - 1, hh * W:(hh + 1) * W, :, :, :]).then_inc(ctx_loaded, 16)
                for j in range(2):
                    for hl in range(2):
                        src = v_scr[b - 1, :, hl, :].rearrange("k (q e w) -> k q e w", e=2, w=W)[:, :, j, :]
                        sp.dma_start(vbd[j * KEYS:(j + 1) * KEYS, hl, :, j * (W + 1):j * (W + 1) + W],
                                     src).then_inc(ctx_loaded, 16)
                sp.dma_start(mbc[:, :], mb_scr[b - 1]).then_inc(ctx_loaded, 16)
                sp.dma_start(mrow[:, :], mr_scr[b - 1]).then_inc(ctx_loaded, 16)
                if ph is body:
                    for gg in range(G2):
                        sp.dma_start(xin[:, gg * T4:(gg + 1) * T4, :],
                                     x[b, gg * GT:(gg + 1) * GT, :].rearrange("(t p) d -> p t d", p=P)
                                     ).then_inc(x_loaded[gg], 16)
                    for s in range(4):
                        sp.wait_ge(done["M"][s], ph.start("M", s))
                    sp.dma_start(dd[:, :, :], dt_scr).then_inc(dd_loaded, 16)

            def load_d(ph, b, g):
                u = use(ph, ("U1", 0), "M", 1)
                sp.wait_ge(u.full, u.before + 1)
                sp.dma_start(dd[:, :, :], dn_scr).then_inc(dd_loaded, 16)

            def store_out(ph, c, g):
                for t in range(T4):
                    u = use(ph, ("F2", g), "O", t)
                    sp.wait_ge(u.done, u.before + 1)
                    sp.dma_start(out[c, g * GT + t * P:g * GT + (t + 1) * P, :],
                                 x1[:, g * T4 + t, :]).then_inc(out_stored[g * T4 + t], 16)

            sp.wait_ge(consts, 10)
            run(sp, {"START": load_start, "U1": load_d, "F2": store_out})
            for t in range(TILES):
                sp.wait_ge(out_stored[t], 16 * B)

        @block.tensor
        def _(pe):
            mm = nc.tensor.matmul

            def acquire(u):
                if u.reused:
                    pe.wait_ge(u.done, u.before)

            def transposed(name, src, ready, ident=None):
                def unit(ph, b, g):
                    pe.wait_ge(idents, 6)
                    pe.wait_ge(*ready)
                    for c in range(C):
                        u = use(ph, (name, 0), "M", c)
                        acquire(u)
                        for j in range(C):
                            i = nc.tensor.transpose(psM[:, u.slot, j * P:(j + 1) * P],
                                                    src[:, j, c * P:(c + 1) * P], id32[:, :])
                        i.then_inc(u.full, 1)
                return unit

            def gram(name, right, ready):
                def unit(ph, b, g):
                    pe.wait_ge(ld["tk"], 16)
                    pe.wait_ge(*ready)
                    for c in range(C):
                        u = use(ph, (name, 0), "M", c)
                        acquire(u)
                        for j in range(C):
                            i = mm(psM[:, u.slot, :], tk[:, j, c * P:(c + 1) * P], right[:, j, :],
                                   start=(j == 0), stop=(j == C - 1))
                        i.then_inc(u.full, 1)
                return unit

            def w1_transposed(ph, b, g):
                pe.wait_ge(ld["w1"], 16)
                u = use(ph, ("W1T", 0), "M", 0)
                acquire(u)
                for j in range(C):
                    i = nc.tensor.transpose(psM[:, u.slot, j * P:(j + 1) * P], w1s[:, j * P:(j + 1) * P], id32[:, :])
                i.then_inc(u.full, 1)

            def chunked(u, left, right, parts):
                acquire(u)
                for c in range(C):
                    for j in range(parts):
                        i = mm(psM[:, u.slot, c * P:(c + 1) * P], left[:, j, c * P:(c + 1) * P], right(j),
                               start=(c == 0 and j == 0), stop=(j == parts - 1), skip_group_check=True)
                i.then_inc(u.full, 1)

            def a_init(ph, b, g):
                u = use(ph, ("W1T", 0), "M", 0)
                pe.wait_ge(u.done, u.before + 1)
                chunked(use(ph, ("AINIT", 0), "M", 0), tk, lambda j: w1T[:, j, :], C)
                chunked(use(ph, ("AINIT", 0), "M", 1), tq, lambda j: w1T[:, j, :], C)

            def w2_transposed(ph, b, g):
                pe.wait_ge(ld["w2"], 16)
                u = use(ph, ("W2T0", 0), "M", 0)
                acquire(u)
                for j in range(C):
                    i = nc.tensor.transpose(psM[:, u.slot, j * P:(j + 1) * P], w2n[:, j, :], id32[:, :])
                i.then_inc(u.full, 1)

            def keys(ph, b, g):
                for n in ("CTXT", "WKT"):
                    for c in range(C):
                        u = use(ph, (n, 0), "M", c)
                        pe.wait_ge(u.done, u.before + 1)
                for m in range(C):
                    u = use(ph, ("KCTX", 0), "M", m)
                    acquire(u)
                    for c in range(C):
                        i = mm(psM[:, u.slot, :], wkT[:, c, m * P:(m + 1) * P], ctxT[:, c, :],
                               start=(c == 0), stop=(c == C - 1))
                    i.then_inc(u.full, 1)

            def values(ph, b, g):
                for c in range(C):
                    u = use(ph, ("WVT", 0), "M", c)
                    pe.wait_ge(u.done, u.before + 1)
                for r in range(C):
                    u = use(ph, ("VCTX", 0), "M", r)
                    acquire(u)
                    for c in range(C):
                        i = mm(psM[:, u.slot, :], ctxT[:, c, r * P:(r + 1) * P], wvT[:, c, :],
                               start=(c == 0), stop=(c == C - 1))
                    i.then_inc(u.full, 1)

            def mean(ph, b, g):
                u = use(ph, ("MEAN", g), "M", 0)
                acquire(u)
                pe.wait_ge(consts, 10)
                pe.wait_ge(abs_done, g + 1)
                mm(psM[:, u.slot, 0:1], ones32[:, :], asum[:, g:g + 1], start=True, stop=True).then_inc(u.full, 1)

            def ternary(ph, b, g):
                pe.wait_ge(tern_step, 2 * (g + 1))
                w = tern.rearrange("p (m d) -> p m d", d=D) if g == 0 else tern.rearrange("p (m f) -> p m f", f=FF)
                for pair in range(FCH // 2):
                    u = use(ph, ("TERN", g), "T", pair)
                    acquire(u)
                    for k in range(8):
                        if g == 0:
                            dc, fc = k // 2, 2 * pair + k % 2
                            src = w[:, fc, dc * P:(dc + 1) * P]
                        else:
                            fc, dc = 2 * pair + k // 4, k % 4
                            src = w[:, dc, fc * P:(fc + 1) * P]
                        i = nc.tensor.transpose(psT[:, u.slot, k * P:(k + 1) * P], src, id16[:, :])
                    i.then_inc(u.full, 1)

            def tile_transposes(ln, name, src):
                def unit(ph, b, g):
                    for t in range(T4):
                        u = use(ph, (name, g), "T", t)
                        acquire(u)
                        s = use(ph, (ln, g), "S", t)
                        pe.wait_ge(split, s.before + 1)
                        for k in range(2 * C):
                            i = nc.tensor.transpose(psT[:, u.slot, k * P:(k + 1) * P],
                                                    src(g, t, k // C)[:, (k % C) * P:(k % C + 1) * P], id16[:, :])
                        i.then_inc(u.full, 1)
                return unit

            def triple(dst, lhs, rhs, chunks, opened=False, closes=True):
                n = 0
                for c in range(chunks):
                    for l, r in PASSES:
                        n += 1
                        i = mm(dst, lhs(l, c), rhs(r, c), start=(n == 1 and not opened),
                               stop=(closes and n == 3 * chunks))
                return i

            def in_sbuf(ph, unit, n):
                for t in range(n - 2, n):
                    u = use(ph, unit, "T", t)
                    pe.wait_ge(u.done, u.before + 1)

            def pre(ph, b, g):
                if ph is first:
                    pe.wait_ge(init, 9)
                else:
                    pe.wait_ge(u1, b * U1_STEPS)
                in_sbuf(ph, ("T1", g), T4)
                u = use(ph, ("PRE", g), "M", 0)
                acquire(u)
                triple(psM[:, u.slot, :], lambda l, c: A16[:, l, c, :],
                       lambda r, c: xT1[:, r * C + c, g * GT:(g + 1) * GT], C).then_inc(u.full, 1)

            def dh(ph, b, g):
                if g == 0:
                    for s in range(4):
                        pe.wait_ge(done["M"][s], ph.start("M", s))
                u = use(ph, ("DH", g), "M", 0)
                acquire(u)
                triple(psM[:, u.slot, :], lambda l, c: P16[:, l, c, :],
                       lambda r, c: xT1[:, r * C + c, g * GT:(g + 1) * GT], C, closes=False)
                s = use(ph, ("PRE", g), "S", 0)
                pe.wait_ge(split, s.before + 1)
                triple(psM[:, u.slot, :], lambda l, c: G16[:, l, :], lambda r, c: hT[:, g, r, :], 1,
                       opened=True).then_inc(u.full, 1)

            def h_transposes(ph, b, g):
                pe.wait_ge(dp_split, 2 * b + g + 1)
                for t in range(T4):
                    u = use(ph, ("HT", g), "T", t)
                    acquire(u)
                    for k, (src, hl) in enumerate(((dpT, HI), (hT, HI), (dpT, LO), (hT, LO))):
                        i = nc.tensor.transpose(psT[:, u.slot, k * P:(k + 1) * P],
                                                src[:, g, hl, t * P:(t + 1) * P], id16[:, :])
                    i.then_inc(u.full, 1)

            def sums(ph, b, g):
                in_sbuf(ph, ("HT", 1), T4)
                pe.wait_ge(ones_set, b + 1)
                u = use(ph, ("S", 0), "M", 0)
                acquire(u)
                for t in range(TILES):
                    h_hi, h_lo = nat[:, t, HI, HID:2 * HID], nat[:, t, LO, HID:2 * HID]
                    h_one = nat[:, t, HI, HID:2 * HID + 1]
                    mm(psM[:, u.slot, 0:HID + 1], h_hi, h_one, start=(t == 0), stop=False, skip_group_check=True)
                    mm(psM[:, u.slot, 0:HID + 1], h_lo, h_one, start=False, stop=False, skip_group_check=True)
                    mm(psM[:, u.slot, 0:HID], h_hi, h_lo, start=False, stop=False, skip_group_check=True)
                for t in range(TILES):
                    for hl in range(2):
                        i = mm(psM[:, u.slot, HID + 2:HID + 3], nat[:, t, hl, 0:HID],
                               nat[:, t, HI, 2 * HID:2 * HID + 1], start=False,
                               stop=(t == TILES - 1 and hl == 1), skip_group_check=True)
                i.then_inc(u.full, 1)
                for c in range(C):
                    u = use(ph, ("S", 0), "M", 1 + c)
                    acquire(u)
                    for t in range(TILES):
                        x_hi, x_lo = (xn1[:, hl, t, c * P:(c + 1) * P] for hl in range(2))
                        mm(psM[:, u.slot, 0:2 * HID + 1], x_hi, nat[:, t, HI, 0:2 * HID + 1], start=(t == 0),
                           stop=False, skip_group_check=True)
                        mm(psM[:, u.slot, 0:2 * HID], x_hi, nat[:, t, LO, 0:2 * HID], start=False, stop=False,
                           skip_group_check=True)
                        i = mm(psM[:, u.slot, 0:2 * HID + 1], x_lo, nat[:, t, HI, 0:2 * HID + 1], start=False,
                               stop=(t == TILES - 1), skip_group_check=True)
                    i.then_inc(u.full, 1)

            def update(ph, b, g):
                if ph is not first:
                    pe.wait_ge(dd_loaded, 32 * b)
                for k in range(5):
                    u = use(ph, ("S", 0), "M", k)
                    pe.wait_ge(u.done, u.before + 1)
                u = use(ph, ("U1", 0), "M", 0)
                acquire(u)
                for c in range(C):
                    mm(psM[:, u.slot, :], s12[:, c, HID:2 * HID], dd[:, c, :], start=(c == 0), stop=False)
                mm(psM[:, u.slot, :], s3[:, 0:HID], w2T32[:, :], start=False, stop=True).then_inc(u.full, 1)
                pe.wait_ge(bc_ready, 2 * b + 2)
                u = use(ph, ("U1", 0), "M", 1)
                acquire(u)
                for c in range(C):
                    mm(psM[:, u.slot, :], sxb[:, c, :], dd[:, c, :], start=(c == 0), stop=False)
                mm(psM[:, u.slot, :], s4b, w2T32[:, :], start=False, stop=True).then_inc(u.full, 1)
                chunked(use(ph, ("U1", 0), "M", 2), kk, lambda j: s12[:, j, 0:HID], C)
                chunked(use(ph, ("U1", 0), "M", 3), kq, lambda j: s12[:, j, 0:HID], C)

            def new_w2(ph, b, g):
                pe.wait_ge(u1, b * U1_STEPS + 1)
                u = use(ph, ("U2", 0), "M", 0)
                acquire(u)
                for j in range(C):
                    i = nc.tensor.transpose(psM[:, u.slot, j * P:(j + 1) * P], w2T32[:, j * P:(j + 1) * P], id32[:, :])
                i.then_inc(u.full, 1)

            def new_pg(ph, b, g):
                if ph is setup:
                    pe.wait_ge(d_ready, 1)
                    left = dn
                else:
                    left = dd
                    u = use(ph, ("U2", 0), "M", 0)
                    pe.wait_ge(u.done, u.before + 1)
                    pe.wait_ge(dd_loaded, 32 * b + 16)
                chunked(use(ph, ("U3", 0), "M", 0), left, lambda j: w2n[:, j, :], C)
                u = use(ph, ("U3", 0), "M", 1)
                acquire(u)
                for j in range(C):
                    i = mm(psM[:, u.slot, 0:HID], w2n[:, j, :], w2n[:, j, :], start=(j == 0), stop=(j == C - 1))
                i.then_inc(u.full, 1)

            def pre2(ph, b, g):
                pe.wait_ge(u1, (b + 1) * U1_STEPS)
                u = use(ph, ("A3P", g), "M", 0)
                acquire(u)
                triple(psM[:, u.slot, :], lambda l, c: Aq16[:, l, c, :],
                       lambda r, c: xT1[:, r * C + c, g * GT:(g + 1) * GT], C).then_inc(u.full, 1)

            def mlp_out(ph, b, g):
                for t in range(T4):
                    u = use(ph, ("A3O", g), "O", t)
                    acquire(u)
                    tok = slice(g * GT + t * P, g * GT + (t + 1) * P)
                    triple(psO[:, u.slot, :], lambda l, c: xT1[:, l * C + c, tok], lambda r, c: tqT[:, r, c, :], C,
                           closes=False)
                    if t == 0:
                        s = use(ph, ("A3P", g), "S", 0)
                        pe.wait_ge(split, s.before + 1)
                    triple(psO[:, u.slot, :], lambda l, c: h2[:, l, t * P:(t + 1) * P], lambda r, c: w2T16[:, r, :],
                           1, opened=True).then_inc(u.full, 1)

            def queries(ph, c_, g):
                if g == 0:
                    for s in range(2):
                        pe.wait_ge(done["T"][s], ph.start("T", s))
                else:
                    in_sbuf(ph, ("T2", 1), T4)
                for m in range(C):
                    u = use(ph, ("Q", g), "M", m)
                    acquire(u)
                    triple(psM[:, u.slot, :], lambda l, c: wqT[:, l, c, m * P:(m + 1) * P],
                           lambda r, c: xTX[:, r * C + c, :], C).then_inc(u.full, 1)

            def guard(ph, c_, g):
                if g == 0:
                    pe.wait_ge(ctx_loaded, 160 * c_ + 160)
                s = use(ph, ("Q", g), "S", C - 1)
                pe.wait_ge(split, s.before + 1)
                for t in range(T4):
                    for i in range(2):
                        u = use(ph, ("GUARD", g), "O", 2 * t + i)
                        acquire(u)
                        for k in range(2):
                            m = 2 * i + k
                            mm(psO[:, u.slot, k * 256:(k + 1) * 256], qs[:, HI, m, t * P:(t + 1) * P],
                               kbd[:, HI, m, :], start=(k == 0), stop=False, skip_group_check=True)
                        mm(psO[:, u.slot, :].rearrange("p (h k) -> p h k", k=KEYS), ones_row[:, :],
                           mrow[:, :].rearrange("p (a k) -> p a k", a=1).broadcast_to([1, 8, KEYS]), start=False, stop=True,
                           skip_group_check=True).then_inc(u.full, 1)

            def guard_transposes(ph, c_, g):
                for k in range(6, 8):
                    u = use(ph, ("GUARD", g), "O", k)
                    pe.wait_ge(u.done, u.before + 1)
                u = use(ph, ("GT", g), "T", 0)
                acquire(u)
                for t in range(T4):
                    i = nc.tensor.transpose(psT[0:HEADS, u.slot, t * P:(t + 1) * P].bitcast(BF16), gm[:, t, :], idbf[:, :])
                i.then_inc(u.full, 1)

            def scores(ph, c_, g):
                u = use(ph, ("GT", g), "T", 0)
                pe.wait_ge(u.done, u.before + 1)
                for q in range(PAIRS):
                    m, half = q // 2, slice((q % 2) * P, (q % 2 + 1) * P)
                    u = use(ph, ("ST", g), "M", q)
                    acquire(u)
                    triple(psM[:, u.slot, :], lambda l, c: kbd[:, l, m, half], lambda r, c: qs[:, r, m, :], 1,
                           closes=False)
                    mm(psM[:, u.slot, :], neg_ind[:, q * P:(q + 1) * P], gT[:, :], start=False,
                       stop=True).then_inc(u.full, 1)

            def weighted_values(ph, c_, g):
                for t in range(T4):
                    for i in range(2):
                        u = use(ph, ("PV", g), "O", 2 * t + i)
                        acquire(u)
                        n = 0
                        for k in range(4):
                            q = 4 * i + k
                            if t == 0:
                                s = use(ph, ("ST", g), "S", q)
                                pe.wait_ge(split, s.before + 1)
                            for l, r in PASSES:
                                ins = mm(psO[:, u.slot, k * 66:(k + 1) * 66], es[:, l, q, t * P:(t + 1) * P],
                                         vbd[:, r, q, :], start=(n == 0), stop=(n == 11), skip_group_check=True)
                                n += 1
                        ins.then_inc(u.full, 1)

            def ffn1(ph, c_, g):
                for f in range(FCH):
                    u = use(ph, ("F1", g), "M", f)
                    waits = [(u.done, u.before), (done["T"][0], setup.total["T"][0])]
                    if f == 0:
                        for t in range(T4 - 2, T4):
                            tr = use(ph, ("T3", g), "T", t)
                            waits.append((tr.done, tr.before + 1))
                    held(pe, waits)
                    for c in range(C):
                        for hl in range(2):
                            i = mm(psM[:, u.slot, :], fw1T[:, c, f * P:(f + 1) * P], xTX[:, hl * C + c, :],
                                   start=(c == 0 and hl == 0), stop=(c == C - 1 and hl == 1))
                    i.then_inc(u.full, 1)

            def ffn2(ph, c_, g):
                for t in range(T4):
                    u = use(ph, ("F2", g), "O", t)
                    for f in range(FCH):
                        waits = [(u.done, u.before), (done["T"][1], setup.total["T"][1])] if f == 0 else []
                        if t == 0:
                            s = use(ph, ("F1", g), "S", f)
                            waits.append((split, s.before + 1))
                        if waits:
                            held(pe, waits)
                        for hl in range(2):
                            i = mm(psO[:, u.slot, :], hF[:, f, hl, t * P:(t + 1) * P], fw2T[:, f, :],
                                   start=(f == 0 and hl == 0), stop=(f == FCH - 1 and hl == 1))
                    i.then_inc(u.full, 1)

            run(pe, {
                "K": gram("K", tk, (ld["tk"], 16)), "KQ": gram("KQ", tq, (ld["tq"], 16)),
                "DT": transposed("DT", dn, (d_ready, 1)), "TQT": transposed("TQT", tq, (ld["tq"], 16)),
                "WQT": transposed("WQT", wqs, (ld["wq"], 16)), "WKT": transposed("WKT", wks, (ld["wk"], 16)),
                "WVT": transposed("WVT", wvs, (ld["wv"], 16)), "CTXT": transposed("CTXT", ctxs, (ld["ctx"], 16)),
                "W1T": w1_transposed, "AINIT": a_init, "W2T0": w2_transposed, "KCTX": keys, "VCTX": values,
                "MEAN": mean, "TERN": ternary,
                "T1": tile_transposes("L1", "T1", lambda g, t, hl: xn1[:, hl, g * T4 + t, :]),
                "T2": tile_transposes("L2", "T2", lambda g, t, hl: xnX[:, hl, t, :]),
                "T3": tile_transposes("L3", "T3", lambda g, t, hl: xnX[:, hl, t, :]),
                "PRE": pre, "DH": dh, "HT": h_transposes, "S": sums, "U1": update, "U2": new_w2, "U3": new_pg,
                "A3P": pre2, "A3O": mlp_out, "Q": queries, "GUARD": guard, "GT": guard_transposes, "ST": scores,
                "PV": weighted_values, "F1": ffn1, "F2": ffn2,
            })

        @block.scalar
        def _(act):
            activation = nc.scalar.activation

            def copied(name, dst):
                def unit(ph, b, g):
                    for c in range(C):
                        u = use(ph, (name, 0), "M", c)
                        act.wait_ge(u.full, u.before + 1)
                        activation(dst[:, c, :], psM[:, u.slot, :], ACT.Copy).then_inc(u.done, 1)
                return unit

            def weight_hi(name, dst):
                def unit(ph, b, g):
                    for c in range(C):
                        u = use(ph, (name, 0), "M", c)
                        act.wait_ge(u.full, u.before + 1)
                        activation(dst[:, HI, c, :], psM[:, u.slot, :], ACT.Copy, scale=WSCALE).then_inc(wt_hi, 1)
                return unit

            def one_block(name, dst):
                def unit(ph, b, g):
                    u = use(ph, (name, 0), "M", 0)
                    act.wait_ge(u.full, u.before + 1)
                    activation(dst, psM[:, u.slot, :].rearrange("p (j h) -> p j h", j=C), ACT.Copy).then_inc(u.done, 1)
                return unit

            def magnitudes(ph, b, g):
                act.wait_ge(ld["fw"], 16 * (g + 1))
                if g == 0:
                    u = use(ph, ("VCTX", 0), "M", C - 1)
                    act.wait_ge(u.full, u.before + 1)
                activation(junk, ffs, ACT.Abs, accum_out=asum[:, g:g + 1]).then_inc(abs_done, 1)

            def ternary(ph, b, g):
                for pair in range(FCH // 2):
                    u = use(ph, ("TERN", g), "T", pair)
                    act.wait_ge(u.full, u.before + 1)
                    if g == 0:
                        dst = fw1T[:, :, pair * 2 * P:(pair + 1) * 2 * P]
                        src = psT[:, u.slot, :].rearrange("p (c f) -> p c f", c=C)
                    else:
                        dst = fw2T[:, 2 * pair:2 * pair + 2, :]
                        src = psT[:, u.slot, :].rearrange("p (c f) -> p c f", c=2)
                    activation(dst, src, ACT.Copy, saturate=False).then_inc(u.done, 1)

            def stage_free(ph, unit, i):
                s = use(ph, unit, "S", i)
                if ph.place[unit, "S", i][1] < RINGS["S"]:
                    if ph is not first:
                        act.wait_ge(split, ph.start("S", 0))
                else:
                    act.wait_ge(split, s.before - RINGS["S"] + 1)
                return stage[:, s.slot, :]

            def normalized(k, name, src):
                def unit(ph, b, g):
                    act.wait_ge(nmr[k], 2 * b + g + 1)
                    for t in range(T4):
                        dst = stage_free(ph, (name, g), t)
                        activation(dst, src[:, g * T4 + t, :], ACT.Identity, bias=nm[:, k, g, t:t + 1],
                                   scale=rs[:, k, g, t:t + 1]).then_inc(staged, 1)
                return unit

            def collect(name, dst):
                def unit(ph, b, g):
                    for t in range(T4):
                        u = use(ph, (name, g), "T", t)
                        act.wait_ge(u.full, u.before + 1)
                        activation(dst(g, t), psT[:, u.slot, :].rearrange("p (a d) -> p a d", d=P),
                                   ACT.Copy).then_inc(u.done, 1)
                return unit

            def hidden(ph, b, g):
                act.wait_ge(u_step, 6 * b + 3 * g + 3)
                activation(ee[:, g, :], un[:, g, :], ACT.Square).then_inc(e_step, 1)
                act.wait_ge(e_step, 4 * b + 2 * g + 1)
                activation(ee[:, g, :], ee[:, g, :], ACT.Exp, scale=-0.5).then_inc(e_step, 1)
                for k in range(G2 if g == G2 - 1 else 0):
                    dst = stage_free(ph, ("PRE", k), 0)
                    activation(dst, un[:, k, :], ACT.Gelu).then_inc(h_staged, 1)

            def token_major(ph, b, g):
                for t in range(T4):
                    u = use(ph, ("HT", g), "T", t)
                    act.wait_ge(u.full, u.before + 1)
                    activation(nat[:, g * T4 + t, :, 0:2 * HID],
                               psT[:, u.slot, 0:4 * P].rearrange("p (a d) -> p a d", a=2), ACT.Copy).then_inc(u.done, 1)

            def new_hidden(ph, b, g):
                u = use(ph, ("A3P", g), "M", 0)
                act.wait_ge(u.full, u.before + 1)
                dst = stage_free(ph, ("A3P", g), 0)
                activation(dst, psM[:, u.slot, :], ACT.Gelu, bias=b1c[:, :], scale=1.0 / WSCALE).then_inc(u.done, 1)

            def queries(ph, c_, g):
                for m in range(C):
                    u = use(ph, ("Q", g), "M", m)
                    act.wait_ge(u.full, u.before + 1)
                    dst = stage_free(ph, ("Q", g), m)
                    activation(dst, psM[:, u.slot, :], ACT.Identity, bias=bqc[:, m:m + 1],
                               scale=1.0 / WSCALE).then_inc(u.done, 1)

            def guard_rows(ph, c_, g):
                u = use(ph, ("GT", g), "T", 0)
                act.wait_ge(u.full, u.before + 1)
                activation(gT[:, :], psT[0:HEADS, u.slot, 0:GT].bitcast(BF16), ACT.Copy).then_inc(u.done, 1)

            def exponentials(ph, c_, g):
                for q in range(PAIRS):
                    u = use(ph, ("ST", g), "M", q)
                    act.wait_ge(u.full, u.before + 1)
                    dst = stage_free(ph, ("ST", g), q)
                    activation(dst, psM[:, u.slot, :], ACT.Exp, bias=mbc[:, :], scale=1.0 / SQW).then_inc(u.done, 1)

            def ffn_hidden(ph, c_, g):
                for f in range(FCH):
                    u = use(ph, ("F1", g), "M", f)
                    act.wait_ge(u.full, u.before + 1)
                    dst = stage_free(ph, ("F1", g), f)
                    activation(dst, psM[:, u.slot, :], ACT.Gelu, bias=fb1c[:, f:f + 1]).then_inc(u.done, 1)

            act.wait_ge(ld["small"], 112)
            run(act, {
                "K": copied("K", kk), "KQ": copied("KQ", kq), "DT": copied("DT", dd), "TQT": weight_hi("TQT", tqT),
                "W1T": one_block("W1T", w1T), "WQT": weight_hi("WQT", wqT), "WKT": copied("WKT", wkT),
                "WVT": copied("WVT", wvT), "CTXT": copied("CTXT", ctxT), "MEAN": magnitudes, "TERN": ternary,
                "L1": normalized(0, "L1", xin), "L2": normalized(1, "L2", x1), "L3": normalized(2, "L3", x1),
                "T1": collect("T1", lambda g, t: xT1[:, :, g * GT + t * P:g * GT + (t + 1) * P]),
                "T2": collect("T2", lambda g, t: xTX[:, :, t * P:(t + 1) * P]),
                "T3": collect("T3", lambda g, t: xTX[:, :, t * P:(t + 1) * P]),
                "PRE": hidden, "HT": token_major, "U2": one_block("U2", w2n), "A3P": new_hidden, "Q": queries,
                "GT": guard_rows, "ST": exponentials, "F1": ffn_hidden,
            })

        @block.gpsimd
        def _(pool):
            for m in (id16, idbf, id32):
                nc.gpsimd.memset(m[:, :], 0.0).then_inc(idents, 1)
            pool.wait_ge(idents, 3)
            for m in (id16, idbf, id32):
                nc.gpsimd.affine_select(out=m[:, :], in_=m[:, :], compare_op=ALU.not_equal, fill=1.0, base=0,
                                        pattern=[[-1, P]], channel_multiplier=1).then_inc(idents, 1)
            nc.gpsimd.memset(ones32[:, :], 1.0).then_inc(consts, 1)
            nc.gpsimd.memset(ones_row[:, :], 1.0).then_inc(consts, 1)
            nc.gpsimd.memset(neghalf[:, :], -0.5).then_inc(consts, 1)
            nc.gpsimd.memset(neg_ind[:, :], -1.0).then_inc(consts, 1)
            nc.gpsimd.memset(kbd[:, :, :, :], 0.0).then_inc(consts, 1)
            nc.gpsimd.memset(vbd[:, :, :, :], 0.0).then_inc(consts, 1)
            pool.wait_ge(consts, 6)
            for j in range(2):
                one = j * (W + 1) + W
                nc.gpsimd.memset(vbd[j * KEYS:(j + 1) * KEYS, HI, :, one:one + 1], 1.0).then_inc(consts, 1)
            nc.gpsimd.affine_select(out=neg_ind[:, :], in_=neg_ind[:, :], compare_op=ALU.is_ge, fill=0.0, base=0,
                                    pattern=[[1, PAIRS * P]], channel_multiplier=-KEYS).then_inc(consts, 1)
            pool.wait_ge(consts, 9)
            nc.gpsimd.affine_select(out=neg_ind[:, :], in_=neg_ind[:, :], compare_op=ALU.is_ge, fill=0.0,
                                    base=KEYS - 1, pattern=[[-1, PAIRS * P]], channel_multiplier=KEYS).then_inc(consts, 1)
            pool.wait_ge(ld["small"], 112)
            pool.wait_ge(consts, 10)

            def rsqrt(k):
                def unit(ph, b, g):
                    held(pool, [(stats[k], 2 * b + g + 1)])
                    nc.gpsimd.tensor_scalar(ve[:, k, :], mv[:, k, :, 1], EPS, None, ALU.add).then_inc(vep[k], 1)
                    pool.wait_ge(vep[k], 2 * b + g + 1)
                    nc.gpsimd.tensor_tensor(rs[:, k, g, :], ve[:, k, :], neghalf[:, :], ALU.pow).then_inc(rstd[k], 1)
                return unit

            def add_b2(ph, b, g):
                if g == 0:
                    pool.wait_ge(u1, b * U1_STEPS + 2)
                for t in range(T4):
                    xt = xin[:, g * T4 + t, :]
                    nc.gpsimd.tensor_tensor(xt, xt, b2b[:, :], ALU.add).then_inc(xa_done, 1)

            def add_attention(ph, c_, g):
                for t in range(T4):
                    for i in range(2):
                        u = use(ph, ("PV", g), "O", 2 * t + i)
                        pool.wait_ge(u.done, u.before + 1)
                        xt = x1[:, g * T4 + t, i * 256:(i + 1) * 256]
                        nc.gpsimd.tensor_tensor(xt, xt, obuf[:, i, :, :].rearrange("p h w -> p (h w)"),
                                                ALU.add).then_inc(o_done, 1)

            def add_fb2(ph, c_, g):
                for t in range(T4):
                    s = use(ph, ("L3", g), "S", t)
                    pool.wait_ge(hi_done, s.before + 1)
                    xt = x1[:, g * T4 + t, :]
                    nc.gpsimd.tensor_tensor(xt, xt, fb2b[:, :], ALU.add).then_inc(xf_done, 1)

            run(pool, {"L1": rsqrt(0), "L2": rsqrt(1), "L3": rsqrt(2), "A3P": add_b2, "PV": add_attention,
                       "F1": add_fb2})

        @block.vector
        def _(dve):
            v = nc.vector

            def d_matrix(ph, b, g):
                dve.wait_ge(ld["tk"], 16)
                dve.wait_ge(ld["tv"], 16)
                v.tensor_tensor(dn, tk, dn, ALU.subtract).then_inc(d_ready, 1)
                dve.wait_ge(ld["mask"], 48)
                mf = stage[:, 2, :]
                v.tensor_copy(mf, mi).then_inc(mask_step, 1)
                v.tensor_copy(mcf[:, :], mci[:, :]).then_inc(mask_step, 1)
                dve.wait_ge(mask_step, 2)
                mfb = mf.rearrange("p (b k) -> p b k", b=B)
                v.tensor_reduce(mx[:, :], mfb, AX.X, ALU.max).then_inc(mask_step, 1)
                dve.wait_ge(mask_step, 3)
                v.tensor_tensor(mcf[:, :], mcf[:, :], mx[:, :], ALU.subtract).then_inc(mask_step, 1)
                v.tensor_tensor(mfb[0:1], mfb[0:1], mx[0:1, :].rearrange("p (b a) -> p b a", a=1).broadcast_to([1, B, KEYS]),
                                ALU.subtract).then_inc(mask_step, 1)
                dve.wait_ge(mask_step, 5)
                v.tensor_scalar(mcf[:, :], mcf[:, :], MASKED, None, ALU.mult).then_inc(mask_step, 1)
                v.tensor_scalar(mr16[:, :, :], mfb[0:1], MASKED * SQW, -60000.0, ALU.mult, ALU.max).then_inc(mask_step, 1)

            weights_seen = [0]

            def weight_lo(name, dst):
                def unit(ph, b, g):
                    for c in range(C):
                        u = use(ph, (name, 0), "M", c)
                        weights_seen[0] += 1
                        dve.wait_ge(wt_hi, weights_seen[0])
                        v.scalar_tensor_tensor(out=dst[:, LO, c, :], in0=psM[:, u.slot, :], scalar=WSCALE,
                                               in1=dst[:, HI, c, :], op0=ALU.mult, op1=ALU.subtract).then_inc(u.done, 1)
                return unit

            def flat(ap):
                return ap.rearrange("p c h -> p (c h)")

            def a_init(ph, b, g):
                dve.wait_ge(ld["small"], 112)
                step = 0
                for k, (f32, f16, scale) in enumerate(((A32, A16, 1.0), (Aq32, Aq16, WSCALE))):
                    u = use(ph, ("AINIT", 0), "M", k)
                    dve.wait_ge(u.full, u.before + 1)
                    v.tensor_copy(flat(f32[:, :, :]), psM[:, u.slot, :]).then_inc(u.done, 1)
                    dve.wait_ge(u.done, u.before + 1)
                    v.tensor_scalar(f16[:, HI], f32[:, :, :], scale, None, ALU.mult).then_inc(init, 1)
                    dve.wait_ge(init, step + 1)
                    v.scalar_tensor_tensor(out=f16[:, LO], in0=f32[:, :, :], scalar=scale, in1=f16[:, HI],
                                           op0=ALU.mult, op1=ALU.subtract).then_inc(init, 1)
                    step += 2

            def w2_init(ph, b, g):
                u = use(ph, ("W2T0", 0), "M", 0)
                dve.wait_ge(u.full, u.before + 1)
                v.tensor_copy(w2T32[:, :], psM[:, u.slot, :]).then_inc(u.done, 1)
                dve.wait_ge(u.done, u.before + 1)
                v.tensor_scalar(w2T16[:, HI], w2T32[:, :], WSCALE, None, ALU.mult).then_inc(init, 1)
                dve.wait_ge(init, 5)
                v.scalar_tensor_tensor(out=w2T16[:, LO], in0=w2T32[:, :], scalar=WSCALE, in1=w2T16[:, HI],
                                       op0=ALU.mult, op1=ALU.subtract).then_inc(init, 1)
                v.tensor_tensor_reduce(out=obuf[:, :, :, :].rearrange("p a h w -> p (a h w)"), in0=w2T32[:, :],
                                       in1=b2b[:, :], scale=1.0, scalar=0.0, op0=ALU.mult, op1=ALU.add,
                                       accum_out=cc[:, :]).then_inc(init, 1)

            def new_pg(ph, b, g):
                at = 0 if ph is setup else 2 * b + 2
                for k, (dst, cols) in enumerate(((P16, C * HID), (G16, HID))):
                    u = use(ph, ("U3", 0), "M", k)
                    dve.wait_ge(u.full, u.before + 1)
                    hi = dst[:, HI] if k else flat(dst[:, HI])
                    lo = dst[:, LO] if k else flat(dst[:, LO])
                    v.tensor_copy(hi, psM[:, u.slot, 0:cols]).then_inc(u3, 1)
                    dve.wait_ge(u3, at + k + 1)
                    v.tensor_tensor(lo, psM[:, u.slot, 0:cols], hi, ALU.subtract).then_inc(u.done, 1)
                if ph is setup:
                    for k in range(2):
                        u = use(ph, ("U3", 0), "M", k)
                        dve.wait_ge(u.done, u.before + 1)
                    v.memset(nm[:, :, :, :], 0.0).then_inc(init, 1)
                    v.memset(rden[:, :, :], 0.0).then_inc(init, 1)

            def keys(ph, b, g):
                for m in range(C):
                    u = use(ph, ("KCTX", 0), "M", m)
                    dve.wait_ge(u.full, u.before + 1)
                    v.tensor_scalar(kTs[:, HI, m, :], psM[:, u.slot, :], bkc[:, m:m + 1], None, ALU.add).then_inc(kv_hi, 1)
                    dve.wait_ge(kv_hi, m + 1)
                    v.scalar_tensor_tensor(out=kTs[:, LO, m, :], in0=psM[:, u.slot, :], scalar=bkc[:, m:m + 1],
                                           in1=kTs[:, HI, m, :], op0=ALU.add, op1=ALU.subtract).then_inc(u.done, 1)

            def values(ph, b, g):
                for r in range(C):
                    u = use(ph, ("VCTX", 0), "M", r)
                    dve.wait_ge(u.full, u.before + 1)
                    if r:
                        dve.wait_ge(v_split, r)
                    v.tensor_tensor(v32, psM[:, u.slot, :], bvb, ALU.add).then_inc(u.done, 1)
                    dve.wait_ge(u.done, u.before + 1)
                    v.tensor_copy(vs[:, r, HI, :], v32).then_inc(kv_hi, 1)
                    dve.wait_ge(kv_hi, C + r + 1)
                    v.tensor_tensor(vs[:, r, LO, :], v32, vs[:, r, HI, :], ALU.subtract).then_inc(v_split, 1)

            def ternary(ph, b, g):
                u = use(ph, ("MEAN", g), "M", 0)
                dve.wait_ge(u.full, u.before + 1)
                v.tensor_scalar(thr[:, g, 0:1], psM[:, u.slot, 0:1], 1.0 / (FF * D), 1e-8, ALU.mult,
                                ALU.max).then_inc(u.done, 1)
                dve.wait_ge(u.done, u.before + 1)
                v.tensor_scalar(thr[:, g, 1:2], thr[:, g, 0:1], 0.5, None, ALU.mult).then_inc(thr_step, 1)
                v.tensor_scalar(thr[:, g, 2:3], thr[:, g, 0:1], -0.5, None, ALU.mult).then_inc(thr_step, 1)
                dve.wait_ge(thr_step, 2 * g + 2)
                if g == 1:
                    for k in range(6, 8):
                        u = use(ph, ("TERN", 0), "T", k)
                        dve.wait_ge(u.full, u.before + 1)
                v.tensor_scalar(tern, ffs, thr[:, g, 2:3], None, ALU.is_lt).then_inc(tern_step, 1)
                dve.wait_ge(tern_step, 2 * g + 1)
                v.scalar_tensor_tensor(out=tern, in0=ffs, scalar=thr[:, g, 1:2], in1=tern, op0=ALU.is_gt,
                                       op1=ALU.subtract).then_inc(tern_step, 1)

            def split_stage(s, hi, lo):
                src = stage[:, s.slot, :]
                v.tensor_copy(hi, src).then_inc(hi_done, 1)
                dve.wait_ge(hi_done, s.before + 1)
                v.tensor_tensor(lo, src, hi, ALU.subtract).then_inc(split, 1)

            def layernorm(k, name, src, dst):
                def unit(ph, b, g):
                    if name == "L1":
                        dve.wait_ge(x_loaded[g], 16 * b + 16)
                    elif name == "L3":
                        dve.wait_ge(o_done, 16 * b + 8 * g + 8)
                    elif g == 0:
                        for t in range(2, 4):
                            u = use(ph, ("A3O", 0), "O", t)
                            dve.wait_ge(u.done, u.before + 1)
                    else:
                        for s in range(2):
                            dve.wait_ge(done["O"][s], ph.start("O", s))
                    for t in range(T4):
                        i = v.bn_stats(st[:, k, t, :], src[:, g * T4 + t, :])
                    i.then_inc(bn[k], 1)
                    held(dve, [(bn[k], 2 * b + g + 1)])
                    for t in range(T4):
                        i = v.bn_aggr(mv[:, k, t, :], st[:, k, t, :])
                    i.then_inc(stats[k], 1)
                    dve.wait_ge(rstd[k], 2 * b + g + 1)
                    v.scalar_tensor_tensor(out=nm[:, k, g, :], in0=mv[:, k, :, 0], scalar=-1.0, in1=rs[:, k, g, :],
                                           op0=ALU.mult, op1=ALU.mult).then_inc(nmr[k], 1)
                    if name == "L2" and g == 0 and ph is body:
                        u = use(ph, ("T3", 1), "T", T4 - 1)
                        dve.wait_ge(u.full, u.before + 1)
                    for t in range(T4):
                        dve.wait_ge(staged, staged_before(ph, (name, g)) + t + 1)
                        split_stage(use(ph, (name, g), "S", t), dst(g, t, HI), dst(g, t, LO))
                return unit

            LN_ORDER = {id(ph): [u for u in ph.order if u[0] in ("L1", "L2", "L3")] for ph in (first, body, last)}

            def staged_before(ph, unit):
                n = T4 * LN_ORDER[id(ph)].index(unit)
                if ph is first:
                    return n
                n += T4 * len(LN_ORDER[id(first)])
                if ph is body:
                    return body.turn * (T4 * len(LN_ORDER[id(body)])) + n
                return n + (B - 1) * T4 * len(LN_ORDER[id(body)])

            def hidden(ph, b, g):
                u = use(ph, ("PRE", g), "M", 0)
                dve.wait_ge(u.full, u.before + 1)
                v.tensor_scalar(un[:, g, :], psM[:, u.slot, :], b1c[:, :], None, ALU.add).then_inc(u.done, 1)
                dve.wait_ge(u.done, u.before + 1)
                v.tensor_tensor(ee[:, g, :], un[:, g, :], un[:, g, :], ALU.mult).then_inc(u_step, 1)
                dve.wait_ge(u_step, 6 * b + 3 * g + 1)
                v.tensor_scalar(ee[:, g, :], ee[:, g, :], TINY * TINY, 4 * TINY, ALU.is_le, ALU.mult).then_inc(u_step, 1)
                dve.wait_ge(u_step, 6 * b + 3 * g + 2)
                v.tensor_tensor(un[:, g, :], ee[:, g, :], un[:, g, :], ALU.add).then_inc(u_step, 1)
                for k in range(G2 if g == G2 - 1 else 0):
                    at = 6 * b + 3 * k
                    dve.wait_ge(u_step, 6 * b + 3 * k + 3)
                    v.reciprocal(gp[:, k, :], un[:, k, :]).then_inc(gp_step, 1)
                    s = use(ph, ("PRE", k), "S", 0)
                    h = stage[:, s.slot, :]
                    dve.wait_ge(h_staged, 2 * b + k + 1)
                    v.tensor_copy(hT[:, k, HI, :], h).then_inc(hi_done, 1)
                    dve.wait_ge(gp_step, at + 1)
                    v.tensor_tensor(gp[:, k, :], h, gp[:, k, :], ALU.mult).then_inc(gp_step, 1)
                    dve.wait_ge(hi_done, s.before + 1)
                    v.tensor_tensor(hT[:, k, LO, :], h, hT[:, k, HI, :], ALU.subtract).then_inc(split, 1)
                    dve.wait_ge(e_step, 4 * b + 2 * k + 2)
                    v.scalar_tensor_tensor(out=ee[:, k, :], in0=ee[:, k, :], scalar=INV_SQRT_2PI, in1=un[:, k, :],
                                           op0=ALU.mult, op1=ALU.mult).then_inc(gp_step, 1)
                    dve.wait_ge(gp_step, at + 3)
                    v.tensor_tensor(gp[:, k, :], gp[:, k, :], ee[:, k, :], ALU.add).then_inc(gp_ready, 1)

            def hidden_gradient(ph, b, g):
                if g == 0:
                    v.memset(nat[:, :, HI, 2 * HID:2 * HID + 2], 1.0).then_inc(ones_set, 1)
                    if ph is body:
                        dve.wait_ge(u1, b * U1_STEPS)
                dve.wait_ge(gp_ready, 2 * b + g + 1)
                u = use(ph, ("DH", g), "M", 0)
                dve.wait_ge(u.full, u.before + 1)
                v.scalar_tensor_tensor(out=gp[:, g, :], in0=psM[:, u.slot, :], scalar=cc[:, :], in1=gp[:, g, :], op0=ALU.add,
                                       op1=ALU.mult).then_inc(u.done, 1)
                dve.wait_ge(u.done, u.before + 1)
                v.tensor_copy(dpT[:, g, HI, :], gp[:, g, :]).then_inc(dp_hi, 1)
                dve.wait_ge(dp_hi, 2 * b + g + 1)
                v.tensor_tensor(dpT[:, g, LO, :], gp[:, g, :], dpT[:, g, HI, :], ALU.subtract).then_inc(dp_split, 1)

            def sums(ph, b, g):
                u = use(ph, ("S", 0), "M", 0)
                dve.wait_ge(u.full, u.before + 1)
                v.tensor_copy(s3[:, 0:HID + 1], psM[:, u.slot, 0:HID + 1])
                v.tensor_copy(s3[:, HID + 2:HID + 3], psM[:, u.slot, HID + 2:HID + 3]).then_inc(u.done, 1)
                dve.wait_ge(u.done, u.before + 1)
                v.tensor_copy(s4b, s3[:, HID:HID + 1].broadcast_to([P, P])).then_inc(bc_ready, 1)
                for c in range(C):
                    u = use(ph, ("S", 0), "M", 1 + c)
                    dve.wait_ge(u.full, u.before + 1)
                    v.tensor_copy(s12[:, c, 0:2 * HID + 1], psM[:, u.slot, 0:2 * HID + 1]).then_inc(u.done, 1)
                dve.wait_ge(u.done, u.before + 1)
                v.tensor_copy(sxb, s12[:, :, 2 * HID:2 * HID + 1].broadcast_to([P, C, P])).then_inc(bc_ready, 1)

            def update(ph, b, g):
                at = b * U1_STEPS
                m = [use(ph, ("U1", 0), "M", k) for k in range(4)]
                dve.wait_ge(m[0].full, m[0].before + 1)
                v.scalar_tensor_tensor(out=tw, in0=b2b[:, :], scalar=s3[:, HID:HID + 1], in1=psM[:, m[0].slot, :],
                                       op0=ALU.mult, op1=ALU.add).then_inc(m[0].done, 1)
                dve.wait_ge(m[1].full, m[1].before + 1)
                v.scalar_tensor_tensor(out=tb, in0=b2b[:, :], scalar=float(N), in1=psM[:, m[1].slot, :],
                                       op0=ALU.mult, op1=ALU.add).then_inc(m[1].done, 1)
                dve.wait_ge(m[0].done, m[0].before + 1)
                v.scalar_tensor_tensor(out=w2T32[:, :], in0=tw, scalar=-ETA, in1=w2T32[:, :], op0=ALU.mult,
                                       op1=ALU.add).then_inc(u1, 1)
                dve.wait_ge(m[1].done, m[1].before + 1)
                v.scalar_tensor_tensor(out=b2b[:, :], in0=tb, scalar=-ETA, in1=b2b[:, :], op0=ALU.mult,
                                       op1=ALU.add).then_inc(u1, 1)
                v.scalar_tensor_tensor(out=b1c[:, :], in0=s3[:, HID + 2:HID + 3], scalar=-ETA, in1=b1c[:, :],
                                       op0=ALU.mult, op1=ALU.add).then_inc(u1, 1)
                dve.wait_ge(u1, at + 2)
                v.tensor_scalar(w2T16[:, HI], w2T32[:, :], WSCALE, None, ALU.mult).then_inc(u1, 1)
                v.tensor_tensor_reduce(out=tw, in0=w2T32[:, :], in1=b2b[:, :], scale=1.0, scalar=0.0, op0=ALU.mult,
                                       op1=ALU.add, accum_out=cc[:, :]).then_inc(u1, 1)
                dve.wait_ge(u1, at + 4)
                v.scalar_tensor_tensor(out=w2T16[:, LO], in0=w2T32[:, :], scalar=WSCALE, in1=w2T16[:, HI],
                                       op0=ALU.mult, op1=ALU.subtract).then_inc(u1, 1)
                for k, (f32, f16, scale) in enumerate(((A32, A16, 1.0), (Aq32, Aq16, WSCALE))):
                    r = m[2 + k]
                    dve.wait_ge(r.full, r.before + 1)
                    v.scalar_tensor_tensor(out=flat(f32[:, :, :]), in0=psM[:, r.slot, :], scalar=-ETA,
                                           in1=flat(f32[:, :, :]), op0=ALU.mult, op1=ALU.add).then_inc(r.done, 1)
                    dve.wait_ge(r.done, r.before + 1)
                    v.tensor_scalar(f16[:, HI], f32[:, :, :], scale, None, ALU.mult).then_inc(u1, 1)
                    dve.wait_ge(u1, at + 7 + 2 * k)
                    v.scalar_tensor_tensor(out=f16[:, LO], in0=f32[:, :, :], scalar=scale, in1=f16[:, HI],
                                           op0=ALU.mult, op1=ALU.subtract).then_inc(u1, 1)

            def new_hidden(ph, b, g):
                u = use(ph, ("A3P", g), "M", 0)
                dve.wait_ge(u.done, u.before + 1)
                split_stage(use(ph, ("A3P", g), "S", 0), h2[:, HI, :], h2[:, LO, :])

            def add_mlp(ph, b, g):
                for t in range(T4):
                    tile = g * T4 + t
                    u = use(ph, ("A3O", g), "O", t)
                    dve.wait_ge(u.full, u.before + 1)
                    dve.wait_ge(xa_done, TILES * b + tile + 1)
                    if ph is body:
                        dve.wait_ge(out_stored[tile], 16 * b)
                    v.scalar_tensor_tensor(out=x1[:, tile, :], in0=psO[:, u.slot, :], scalar=1.0 / (WSCALE * 1.0),
                                           in1=xin[:, tile, :], op0=ALU.mult, op1=ALU.add).then_inc(u.done, 1)

            def queries(ph, c_, g):
                for m in range(C):
                    u = use(ph, ("Q", g), "M", m)
                    dve.wait_ge(u.done, u.before + 1)
                    split_stage(use(ph, ("Q", g), "S", m), qs[:, HI, m, :], qs[:, LO, m, :])

            def guard(ph, c_, g):
                for k in range(2 * T4):
                    u = use(ph, ("GUARD", g), "O", k)
                    dve.wait_ge(u.full, u.before + 1)
                    v.tensor_reduce(gm[:, k // 2, (k % 2) * 8:(k % 2) * 8 + 8],
                                    psO[:, u.slot, :].rearrange("p (h k) -> p h k", k=KEYS), AX.X,
                                    ALU.max).then_inc(u.done, 1)

            def exponentials(ph, c_, g):
                for q in range(PAIRS):
                    u = use(ph, ("ST", g), "M", q)
                    dve.wait_ge(u.done, u.before + 1)
                    split_stage(use(ph, ("ST", g), "S", q), es[:, HI, q, :], es[:, LO, q, :])

            def normalize(ph, c_, g):
                for k in range(2 * T4):
                    u = use(ph, ("PV", g), "O", k)
                    i = k % 2
                    dve.wait_ge(u.full, u.before + 1)
                    heads = psO[:, u.slot, 0:8 * (W + 1)].rearrange("p (h w) -> p h w", w=W + 1)
                    v.reciprocal(rden[:, i, :], heads[:, :, W]).then_inc(rd, 1)
                    dve.wait_ge(rd, 16 * c_ + 8 * g + k + 1)
                    if k >= 2:
                        dve.wait_ge(o_done, 16 * c_ + 8 * g + k - 1)
                    v.tensor_tensor(obuf[:, i, :, :], heads[:, :, 0:W],
                                    rden[:, i, :].rearrange("p (h a) -> p h a", a=1).broadcast_to([P, 8, W]),
                                    ALU.mult).then_inc(u.done, 1)

            def ffn_hidden(ph, c_, g):
                for f in range(FCH):
                    u = use(ph, ("F1", g), "M", f)
                    dve.wait_ge(u.done, u.before + 1)
                    split_stage(use(ph, ("F1", g), "S", f), hF[:, f, HI, :], hF[:, f, LO, :])

            def add_ffn(ph, c_, g):
                for t in range(T4):
                    tile = g * T4 + t
                    u = use(ph, ("F2", g), "O", t)
                    dve.wait_ge(u.full, u.before + 1)
                    dve.wait_ge(xf_done, TILES * c_ + tile + 1)
                    v.tensor_tensor(x1[:, tile, :], psO[:, u.slot, :], x1[:, tile, :], ALU.add).then_inc(u.done, 1)

            run(dve, {
                "K": d_matrix, "TQT": weight_lo("TQT", tqT), "AINIT": a_init, "W2T0": w2_init, "U3": new_pg,
                "WQT": weight_lo("WQT", wqT), "KCTX": keys, "VCTX": values, "TERN": ternary,
                "L1": layernorm(0, "L1", xin, lambda g, t, hl: xn1[:, hl, g * T4 + t, :]),
                "L2": layernorm(1, "L2", x1, lambda g, t, hl: xnX[:, hl, t, :]),
                "L3": layernorm(2, "L3", x1, lambda g, t, hl: xnX[:, hl, t, :]),
                "PRE": hidden, "DH": hidden_gradient, "S": sums, "U1": update, "A3P": new_hidden, "A3O": add_mlp,
                "Q": queries, "GUARD": guard, "ST": exponentials, "PV": normalize, "F1": ffn_hidden, "F2": add_ffn,
            })


_INS = ["x", "ctx_1024", "mask_BxS2_ik0", "L0_attn_t_k", "L0_attn_t_v", "L0_attn_t_q", "L0_attn_W1", "L0_attn_b1",
        "L0_attn_W2", "L0_attn_b2", "L0_xattn_Wq", "L0_xattn_bq", "L0_xattn_Wk", "L0_xattn_bk", "L0_xattn_Wv",
        "L0_xattn_bv", "L0_ffn_W1", "L0_ffn_b1", "L0_ffn_W2", "L0_ffn_b2"]


def kernel(**inputs):
    import numpy as _np
    import concourse.bacc as _bacc
    from concourse import mybir as _mybir
    from concourse.bass_utils import run_bass_kernel_spmd as _run

    nc = _bacc.Bacc("TRN2", target_bir_lowering=False, num_devices=1)
    arrays, args = {}, []
    for name in _INS:
        a = _np.ascontiguousarray(inputs[name])
        arrays[f"in_{name}_dram"] = a
        args.append(nc.dram_tensor(f"in_{name}_dram", a.shape, _mybir.dt.from_np(a.dtype), kind="ExternalInput").ap())
    args.append(nc.dram_tensor("out_0_dram", (B, N, D), F32, kind="ExternalOutput").ap())
    build(nc, *args)
    r = _run(nc, [arrays], core_ids=[0])
    return r.results[0]["out_0_dram"]
```

```python
import math
from contextlib import ExitStack

import concourse.bass as bass
from concourse import mybir

F32, F16, BF16, F8, I32 = (mybir.dt.float32, mybir.dt.float16, mybir.dt.bfloat16, mybir.dt.float8e4, mybir.dt.int32)
ALU = mybir.AluOpType
ACT = mybir.ActivationFunctionType
AX = mybir.AxisListType

P = 128
B, N, D = 8, 1024, 512
HID = 128
HEADS, W, KEYS = 16, 32, 64
FF = 4 * D
C = D // P
G2, T4 = 2, 4
GT = T4 * P
TILES = G2 * T4
FCH = FF // P
PAIRS = HEADS // 2
WSCALE = 256.0
LR = 0.001
ETA = LR * 2.0 / (N * D)
EPS = 1e-5
MASKED = 10000.0
TINY = 1e-15
INV_SQRT_2PI = (2.0 * math.pi) ** -0.5
SQW = float(W) ** 0.5
HI, LO = 0, 1
PASSES = ((HI, HI), (HI, LO), (LO, HI))
NAT = 2 * HID + 2
HALF = FF * D // P // 2
HT_AT = TILES * 2 * NAT * 2
DPT_AT = HT_AT + 4096
GP_AT = DPT_AT + 4096
S3_AT = HT_AT + 2560
HF_AT = (GP_AT + C * NAT * 4 + 63) // 64 * 64
ARENA = HF_AT + FCH // 2 * 2 * GT * 2

RINGS = {"M": 4, "O": 2, "T": 2, "S": 3}
USES = {
    "D": {}, "K": {"M": 4}, "KQ": {"M": 4}, "DT": {"M": 4}, "TQT": {"M": 4}, "W1T": {"M": 1}, "AINIT": {"M": 2},
    "W2T0": {"M": 1}, "WQT": {"M": 4}, "WKT": {"M": 4}, "WVT": {"M": 4}, "CTXT": {"M": 4}, "KCTX": {"M": 4},
    "VCTX": {"M": 4}, "FW": {}, "MEAN": {"M": 1}, "TERa": {"T": 4}, "TERb": {"T": 4},
    "X0": {}, "X1": {}, "KV": {},
    "L1a": {}, "L1b": {"S": 4}, "T1": {"T": 4}, "PRE": {"M": 1}, "PRG": {"S": 2}, "DH": {"M": 2}, "HT": {"T": 8},
    "S": {"M": 5}, "U1": {"M": 4}, "U2": {"M": 1}, "U3": {"M": 2},
    "A3P": {"M": 1, "S": 1}, "A3Oa": {"O": 2}, "A3Ob": {"O": 2},
    "L2a": {}, "L2b": {"S": 4}, "T2": {"T": 4}, "Q": {"M": 4, "S": 4}, "GUARD": {"O": 8}, "GT": {"T": 1},
    "ST": {"M": 8, "S": 8}, "PV": {"O": 8}, "L3a": {}, "L3b": {"S": 4}, "T3": {"T": 4},
}
USES |= {"F1" + k: {"M": 4, "S": 4} for k in "abcd"} | {"F2" + k: {"O": 2} for k in "abcd"}


def schedule(text):
    return [(name, int(g or 0)) for name, _, g in (word.partition(".") for word in text.split())]


SETUP = schedule("D W1T AINIT W2T0 U3 L1a.0 L1b.0 CTXT WKT WVT WQT L1a.1 L1b.1 KCTX VCTX DT TQT KV")
FIRST = schedule("T1.0 T1.1 PRE.0 PRE.1 PRG K KQ FW.0 DH HT MEAN.0 TERa.0 S TERb.0 FW.1 U1 U2 U3 "
                 "A3P.0 A3Oa.0 A3Ob.0 L2a.0 MEAN.1 L2b.0 TERa.1 T2.0 Q.0 TERb.1 GUARD.0 GT.0 ST.0 PV.0 "
                 "L3a.0 L3b.0 T3.0")
BODY = schedule("X0 F1a.0 F1b.0 L1a.0 L1b.0 A3P.1 F2a.0 T1.0 A3Oa.1 A3Ob.1 X1 L2a.1 F2b.0 PRE.0 L1a.1 F1c.0 L1b.1 "
                "L2b.1 F1d.0 T1.1 PRE.1 PRG F2c.0 DH F2d.0 HT S U1 T2.1 U2 Q.1 U3 A3P.0 GUARD.1 A3Oa.0 GT.1 A3Ob.0 "
                "ST.1 L2a.0 L2b.0 PV.1 KV T2.0 L3a.1 L3b.1 Q.0 T3.1 F1a.1 GUARD.0 F1b.1 GT.0 F2a.1 ST.0 F2b.1 "
                "PV.0 F1c.1 L3a.0 F1d.1 L3b.0 F2c.1 T3.0 F2d.1")
LAST = schedule("F1a.0 F1b.0 A3P.1 F2a.0 A3Oa.1 A3Ob.1 L2a.1 F2b.0 L2b.1 F1c.0 T2.1 F1d.0 Q.1 F2c.0 GUARD.1 GT.1 "
                "F2d.0 ST.1 PV.1 L3a.1 L3b.1 T3.1 F1a.1 F1b.1 F2a.1 F2b.1 F1c.1 F1d.1 F2c.1 F2d.1")
BEHIND = {u for u in BODY if u[0][:2] in ("F1", "F2")}
BEHIND |= {u for u in BODY if u[1] == 1 and u[0] in ("A3P", "A3Oa", "A3Ob", "L2a", "L2b", "T2", "Q", "GUARD", "GT", "ST",
                                                     "PV", "L3a", "L3b", "T3")}


class Use:

    def __init__(self, slot, before, full, done):
        self.slot, self.before, self.full, self.done = slot, before, full, done
        self.reused = not (isinstance(before, int) and before == 0)


class Phase:

    def __init__(self, order, base):
        self.order, self.base, self.place = order, base, {}
        self.total = {r: [0] * n for r, n in RINGS.items()}
        count = {r: 0 for r in RINGS}
        for unit in order:
            for ring, n in USES[unit[0]].items():
                for i in range(n):
                    slot = count[ring] % RINGS[ring]
                    self.place[unit, ring, i] = (slot, count[ring] if ring == "S" else self.total[ring][slot])
                    self.total[ring][slot] += 1
                    count[ring] += 1
        self.count = count
        self.turn = 0

    def start(self, ring, slot):
        if ring == "S":
            return self.turn * self.count["S"] + self.base["S"][0]
        return self.turn * self.total[ring][slot] + self.base[ring][slot]

    def after(self, turns):
        base = {r: [b + turns * t for b, t in zip(self.base[r], self.total[r])] for r in RINGS}
        base["S"] = [self.base["S"][0] + turns * self.count["S"]] * RINGS["S"]
        return base


def build(nc, x, ctx_in, mask, t_k, t_v, t_q, w1, b1, w2, b2, wq, bq, wk, bk, wv, bv, fw1, fb1, fw2, fb2, out):
    setup = Phase(SETUP, {r: [0] * n for r, n in RINGS.items()})
    first = Phase(FIRST, setup.after(1))
    body = Phase(BODY, first.after(1))
    last = Phase(LAST, body.after(B - 1))

    with ExitStack() as stack:
        def sb(name, shape, dt):
            return stack.enter_context(nc.sbuf_tensor(name, shape, dt))

        def sem(name):
            return stack.enter_context(nc.semaphore(name))

        k_scr = nc.dram_tensor("k_scr", (B, P, 2, C, KEYS), F16).ap()
        v_scr = nc.dram_tensor("v_scr", (B, KEYS, 2, D), F16).ap()
        mb_scr = nc.dram_tensor("mb_scr", (B, P, 1), F32).ap()
        mr_scr = nc.dram_tensor("mr_scr", (B, 1, KEYS), F16).ap()
        dn_scr = nc.dram_tensor("dn_scr", (P, C, D), F32).ap()
        dt_scr = nc.dram_tensor("dt_scr", (P, C, D), F32).ap()

        psT = stack.enter_context(nc.psum_tensor("psT", [P, 2, 1024], F16))
        psM = stack.enter_context(nc.psum_tensor("psM", [P, 4, 512], F32))
        psO = stack.enter_context(nc.psum_tensor("psO", [P, 2, 512], F32))

        id16, idbf, id32 = sb("id16", [P, P], F16), sb("idbf", [P, P], BF16), sb("id32", [P, P], F32)
        ones_row = sb("ones_row", [1, P], F16)
        neg_ind = sb("neg_ind", [HEADS, PAIRS * P], BF16)
        neghalf, minus1, eps = (sb(n, [P, T4], F32) for n in ("neghalf", "minus1", "eps"))
        fw1T = sb("fw1T", [P, C, FF], F8)
        fw2T = sb("fw2T", [P, FCH, D], F8)
        tqT = sb("tqT", [P, 2, C, D], F16)
        wqT = sb("wqT", [P, 2, C, D], F16)
        kk = sb("kk", [P, C, D], F32)
        kq = sb("kq", [P, C, D], F32)
        dd = sb("dd", [P, C, D], F32)
        b1c = sb("b1c", [P, 1], F32)
        cc = sb("cc", [P, 1], F32)
        bqc, bkc, fb1c = sb("bqc", [P, C], F32), sb("bkc", [P, C], F32), sb("fb1c", [P, FCH], F32)
        b2b, fb2b = sb("b2b", [P, D], F32), sb("fb2b", [P, D], F32)

        A32, Aq32 = sb("A32", [P, C, HID], F32), sb("Aq32", [P, C, HID], F32)
        A16, Aq16 = sb("A16", [P, 2, C, HID], F16), sb("Aq16", [P, 2, C, HID], F16)
        P16, G16 = sb("P16", [P, 2, C, HID], F16), sb("G16", [P, 2, HID], F16)
        w2T32, w2T16 = sb("w2T32", [P, D], F32), sb("w2T16", [P, 2, D], F16)

        kbd = sb("kbd", [P, 2, C, 4 * KEYS], F16)
        vbd = sb("vbd", [P, 2, PAIRS, 2 * (W + 1)], F16)
        mbc = sb("mbc", [P, 1], F32)
        mrow = sb("mrow", [1, KEYS], F16)

        xin = sb("xin", [P, TILES, D], F32)
        x1 = sb("x1", [P, TILES, D], F32)
        xn1 = sb("xn1", [P, 2, TILES, D], F16)
        xT1 = sb("xT1", [P, 2 * C, N], F16)
        xnX = sb("xnX", [P, 2, T4, D], F16)
        xTF = sb("xTF", [P, 2 * C, GT], F16)
        arena = sb("arena", [P, ARENA // 2], F16)
        stage = sb("stage", [P, RINGS["S"], 512], F32)
        rden = sb("rden", [P, 2, 8], F32)
        gm = sb("gm", [P, T4, HEADS], BF16)
        st = sb("st", [P, 3, T4, 6], F32)
        mv = sb("mv", [P, 3, T4, 2], F32)
        ve = sb("ve", [P, 3, T4], F32)
        rs = sb("rs", [P, 3, G2, T4], F32)
        nm = sb("nm", [P, 3, G2, T4], F32)
        mci = sb("mci", [P, B], I32)
        mx = sb("mx", [P, B], F32)
        mcf = sb("mcf", [P, B], F32)
        asum = sb("asum", [P, 2, 2], F32)
        thr = sb("thr", [P, 2, 3], F32)

        def part(buf, start, shape, dt, rows=P):
            size = 1
            for s in shape:
                size *= s
            nbytes = size * (4 if dt in (F32, I32) else 2)
            v = buf[0:rows, start // 2:(start + nbytes) // 2]
            if dt != F16:
                v = v.bitcast(dt)
            if len(shape) == 2:
                v = v.rearrange("p (a c) -> p a c", a=shape[0])
            if len(shape) == 3:
                v = v.rearrange("p (a e c) -> p a e c", a=shape[0], e=shape[1])
            return v

        xn1f = xn1[:, :, :, :].rearrange("p a t d -> p (a t d)")
        xT1f = xT1[:, :, :].rearrange("p a d -> p (a d)")
        xnXf = xnX[:, :, :, :].rearrange("p a t d -> p (a t d)")
        xTFf = xTF[:, :, :].rearrange("p a d -> p (a d)")
        x1f = x1[:, :, :].rearrange("p a d -> p (a d)")
        fw1f = fw1T[:, :, :].rearrange("p a d -> p (a d)").bitcast(F32)
        fw2f = fw2T[:, :, :].rearrange("p a d -> p (a d)").bitcast(F32)

        un, ee = part(arena, 0, [G2, GT], F32), part(arena, 4096, [G2, GT], F32)
        nat = part(arena, 0, [TILES, 2, NAT], F16)
        hT, dpT = part(arena, HT_AT, [G2, 2, GT], F16), part(arena, DPT_AT, [G2, 2, GT], F16)
        sxb, s4b = part(arena, HT_AT, [C, P], F32), part(arena, HT_AT + 2048, [P], F32)
        tb, tw = part(arena, DPT_AT, [D], F32), part(arena, DPT_AT + 2048, [D], F32)
        gp = part(arena, GP_AT, [G2, GT], F32)
        s12 = part(arena, GP_AT, [C, NAT], F32)
        w2n = part(arena, GP_AT, [C, HID], F32)
        h2 = part(arena, GP_AT, [2, GT], F16)
        s3 = part(arena, S3_AT, [132], F32)
        xTQ, qs = part(arena, 0, [2 * C, GT], F16), part(arena, 8192, [2, C, GT], F16)
        gT = part(arena, 0, [GT], BF16, rows=HEADS)
        obuf = part(arena, GP_AT + 2048, [2, 8, W], F32)
        es = part(xn1f, 0, [2, PAIRS, GT], F16)
        hF = part(arena, HF_AT, [FCH // 2, 2, GT], F16)

        tk, tq = part(x1f.bitcast(F16), 0, [C, D], F32), part(x1f.bitcast(F16), 8192, [C, D], F32)
        dn = part(xT1f, 0, [C, D], F32)
        w1s, w1T = part(xT1f, 8192, [D], F32), part(xT1f, 10240, [C, HID], F32)
        bvb, v32 = part(xT1f, 12288, [D], F32), part(xT1f, 14336, [D], F32)
        wqs, wks = part(arena, 0, [C, D], F32), part(arena, 8192, [C, D], F32)
        wvs, ctxs = part(arena, 16384, [C, D], F32), part(arena, 24576, [C, D], F32)
        wkT, wvT = (f.rearrange("p (c d) -> p c d", c=C) for f in (fw1f, fw2f))
        ctxT = part(xTFf, 0, [C, D], F32)
        w2s = part(xnXf, 0, [C, HID], F32)
        cjunk = part(xn1f, 14336, [D], F32)
        mr16 = part(xnXf, 2048, [B, KEYS], F16, rows=1)
        mi, mf = part(xnXf, 4096, [B * KEYS], I32), part(xnXf, 6144, [B * KEYS], F32)
        kTs = part(xnXf, 0, [2, C, D], F16)
        vs = part(arena, 24576, [C, 2, D], F16)
        ffs = [[part(arena, HF_AT, [HALF], F32), x1f], [part(arena, HF_AT, [HALF], F32), part(xn1f, 0, [HALF], F32)]]
        ones32 = part(xnXf, 0, [P], F32)
        tern = part(xTFf, 0, [HALF], F16)

        full = {r: [sem(f"{r}{i}_filled") for i in range(n)] for r, n in RINGS.items() if r != "S"}
        done = {r: [sem(f"{r}{i}_emptied") for i in range(n)] for r, n in RINGS.items() if r != "S"}
        staged = sem("xhat_staged")
        hi_done = sem("hi_done")
        split = sem("split_done")
        consts, idents = sem("consts"), sem("idents")
        ld = {n: sem(f"load_{n}") for n in ("tk", "tq", "tv", "w1", "w2", "small", "wq", "wk", "wv", "ctx",
                                            "mask", "fw1_0", "fw1_1", "fw2_0", "fw2_1")}
        x_loaded = [sem(f"x_loaded{g}") for g in range(G2)]
        scr_stored = sem("scratch_stored")
        ctx_loaded = sem("ctx_loaded")
        dd_loaded = sem("dd_loaded")
        out_stored = [sem(f"out_stored{t}") for t in range(TILES)]
        d_ready = sem("d_ready")
        wt_hi = sem("weight_hi")
        init = sem("state_init")
        kv_hi = sem("kv_hi")
        v_split = sem("v_split")
        mask_step = sem("mask_step")
        abs_done, thr_step, tern_step = sem("abs_done"), sem("thr_step"), sem("tern_step")
        bn = [sem(f"ln{k}_bn") for k in (1, 2, 3)]
        stats = [sem(f"ln{k}_stats") for k in (1, 2, 3)]
        lnp = [sem(f"ln{k}_steps") for k in (1, 2, 3)]
        u_step = sem("u_step")
        e_step = sem("exp_step")
        h_staged = sem("h_staged")
        gp_step = sem("gp_step")
        gp_ready, dp_hi, dp_split = sem("gp_ready"), sem("dp_hi"), sem("dp_split")
        ones_set = sem("ones_set")
        bc_ready = sem("sums_broadcast")
        u1 = sem("update_step")
        u3 = sem("pg_hi")
        xa_done = sem("x_plus_b2")
        o_done = sem("attn_added")
        xf_done = sem("x_plus_fb2")
        rd = sem("denominators")
        passed = sem("passed")
        U1_STEPS, LN_STEPS, CONSTS = 10, 4, 11
        STORED = 16 * (4 + 2 * B)

        def use(ph, unit, ring, i):
            slot, nth = ph.place[unit, ring, i]
            before = ph.start(ring, slot) + nth
            if ring == "S":
                return Use(slot, before, None, split)
            return Use(slot, before, full[ring][slot], done[ring][slot])

        def held(eng, waits):
            for sm, n in waits:
                eng.wait_ge(sm, n)
            eng.sem_inc(passed, 1)

        def run(eng, unit_programs):
            for ph, b in ((setup, 0), (first, 0)):
                for name, g in ph.order:
                    if name in unit_programs:
                        unit_programs[name](ph, b, g)
            with eng.Fori(1, B) as b:
                body.turn = b - 1
                for unit in BODY:
                    if unit[0] in unit_programs:
                        unit_programs[unit[0]](body, b - 1 if unit in BEHIND else b, unit[1])
            for name, g in LAST:
                if name in unit_programs:
                    unit_programs[name](last, B - 1, g)

        block = stack.enter_context(nc.Block())

        @block.sync
        def _(sp):
            rows = "(j p) d -> p j d"
            for t in range(T4, TILES):
                sp.sem_inc(out_stored[t], 16)
            sp.dma_start(tk, t_k.rearrange(rows, p=P)).then_inc(ld["tk"], 16)
            sp.dma_start(w1s, w1).then_inc(ld["w1"], 16)
            sp.dma_start(dn, t_v.rearrange(rows, p=P)).then_inc(ld["tv"], 16)
            sp.dma_start(w2s, w2.rearrange("(j p) h -> p j h", p=P)).then_inc(ld["w2"], 16)
            small = [(b1c[:, :], b1.rearrange("(p a) -> p a", a=1)), (b2b[:, :], b2.partition_broadcast(P)),
                     (fb2b[:, :], fb2.partition_broadcast(P)), (bvb, bv.partition_broadcast(P)),
                     (bqc[:, :], bq.rearrange("(m p) -> p m", p=P)), (bkc[:, :], bk.rearrange("(m p) -> p m", p=P)),
                     (fb1c[:, :], fb1.rearrange("(m p) -> p m", p=P))]
            for dst, src in small:
                sp.dma_start(dst, src, allow_slow_non_contiguous=True).then_inc(ld["small"], 16)
            sp.dma_start(mi, mask.rearrange("b k -> (b k)").partition_broadcast(P)).then_inc(ld["mask"], 16)
            for j in range(2):
                sp.dma_start(mci[j * KEYS:(j + 1) * KEYS, :], mask.rearrange("b k -> k b"),
                             allow_slow_non_contiguous=True).then_inc(ld["mask"], 16)
            sp.dma_start(tq, t_q.rearrange(rows, p=P)).then_inc(ld["tq"], 16)

            def load_x(b, g):
                sp.dma_start(xin[:, g * T4:(g + 1) * T4, :],
                             x[b, g * GT:(g + 1) * GT, :].rearrange("(t p) d -> p t d", p=P)).then_inc(x_loaded[g], 16)

            load_x(0, 0)
            sp.dma_start(ctxs, ctx_in.rearrange("b k d -> (b k) d").rearrange(rows, p=P)).then_inc(ld["ctx"], 16)
            sp.dma_start(wks, wk.rearrange(rows, p=P)).then_inc(ld["wk"], 16)
            sp.dma_start(wvs, wv.rearrange(rows, p=P)).then_inc(ld["wv"], 16)
            sp.dma_start(wqs, wq.rearrange(rows, p=P)).then_inc(ld["wq"], 16)
            load_x(0, 1)
            sp.wait_ge(mask_step, 7)
            sp.dma_start(mb_scr.rearrange("b p a -> p (b a)"), mcf[:, :], allow_slow_non_contiguous=True).then_inc(scr_stored, 16)
            sp.dma_start(mr_scr.rearrange("b a k -> a b k"), mr16[:, :, :]).then_inc(scr_stored, 16)
            sp.wait_ge(d_ready, 1)
            sp.dma_start(dn_scr, dn).then_inc(scr_stored, 16)
            for m in range(C):
                u = use(setup, ("KCTX", 0), "M", m)
                sp.wait_ge(u.done, u.before + 1)
            for b in range(B):
                sp.dma_start(k_scr[b], kTs[:, :, :, b * KEYS:(b + 1) * KEYS]).then_inc(scr_stored, 16)
            sp.wait_ge(v_split, C)
            for b in range(B):
                half = (b % 2) * KEYS
                sp.dma_start(v_scr[b], vs[half:half + KEYS, b // 2, :, :]).then_inc(scr_stored, 16)
            for c in range(C):
                u = use(setup, ("DT", 0), "M", c)
                sp.wait_ge(u.done, u.before + 1)
            sp.dma_start(dt_scr, dd[:, :, :]).then_inc(scr_stored, 16)

            def load_keys(ph, b, g):
                if ph is setup:
                    sp.wait_ge(scr_stored, STORED)
                    sp.wait_ge(consts, CONSTS)
                else:
                    for k in range(6, 8):
                        u = use(ph, ("PV", 1), "O", k)
                        sp.wait_ge(u.full, u.before + 1)
                    u = use(ph, ("ST", 1), "M", PAIRS - 1)
                    sp.wait_ge(u.done, u.before + 1)
                for hh in range(4):
                    sp.dma_start(kbd[hh * W:(hh + 1) * W, :, :, hh * KEYS:(hh + 1) * KEYS],
                                 k_scr[b, hh * W:(hh + 1) * W, :, :, :]).then_inc(ctx_loaded, 16)
                for j in range(2):
                    for hl in range(2):
                        src = v_scr[b, :, hl, :].rearrange("k (q e w) -> k q e w", e=2, w=W)[:, :, j, :]
                        sp.dma_start(vbd[j * KEYS:(j + 1) * KEYS, hl, :, j * (W + 1):j * (W + 1) + W],
                                     src).then_inc(ctx_loaded, 16)
                sp.dma_start(mbc[:, :], mb_scr[b]).then_inc(ctx_loaded, 16)
                sp.dma_start(mrow[:, :], mr_scr[b]).then_inc(ctx_loaded, 16)

            def load_ffn(ph, b, g):
                w = (fw1 if g == 0 else fw2).rearrange("(m p) d -> p m d", p=P)
                m, d = (FCH, D) if g == 0 else (C, FF)
                for half in range(2):
                    if g == 0 and half == 0:
                        for n in ("WVT", "CTXT"):
                            u = use(setup, (n, 0), "M", C - 1)
                            sp.wait_ge(u.full, u.before + 1)
                    elif g == 0:
                        u = use(ph, ("KQ", 0), "M", C - 1)
                        sp.wait_ge(u.full, u.before + 1)
                    elif half == 0:
                        sp.wait_ge(tern_step, 4)
                    else:
                        u = use(ph, ("S", 0), "M", C)
                        sp.wait_ge(u.full, u.before + 1)
                    sp.dma_start(ffs[g][half].rearrange("p (m d) -> p m d", d=d),
                                 w[:, half * m // 2:(half + 1) * m // 2, :]).then_inc(ld[f"fw{g + 1}_{half}"], 16)

            def load_group0(ph, b, g):
                for s in range(2):
                    sp.wait_ge(done["O"][s], ph.start("O", s))
                load_x(b, 0)

            def load_group1(ph, b, g):
                for t in range(2):
                    u = use(ph, ("A3Ob", 1), "O", t)
                    sp.wait_ge(u.done, u.before + 1)
                load_x(b, 1)

            def load_d(ph, b, g):
                u = use(ph, ("U1", 0), "M", 1)
                sp.wait_ge(u.full, u.before + 1)
                sp.dma_start(dd[:, :, :], dn_scr).then_inc(dd_loaded, 16)

            def load_dt(ph, b, g):
                if ph is not setup:
                    u = use(ph, ("U3", 0), "M", 0)
                    sp.wait_ge(u.full, u.before + 1)
                    sp.dma_start(dd[:, :, :], dt_scr).then_inc(dd_loaded, 16)

            def store_out(tiles):
                def unit(ph, c, g):
                    for k, t in enumerate(tiles):
                        u = use(ph, ("F2c" if t < 2 else "F2d", g), "O", k)
                        sp.wait_ge(u.done, u.before + 1)
                        sp.dma_start(out[c, g * GT + t * P:g * GT + (t + 1) * P, :],
                                     x1[:, g * T4 + t, :]).then_inc(out_stored[g * T4 + t], 16)
                return unit

            run(sp, {"KV": load_keys, "FW": load_ffn, "X0": load_group0, "X1": load_group1, "U1": load_d,
                     "U3": load_dt, "F2c": store_out((0, 1)), "F2d": store_out((2, 3))})
            for t in range(TILES):
                sp.wait_ge(out_stored[t], 16 * B + (16 if t >= T4 else 0))

        @block.tensor
        def _(pe):
            mm = nc.tensor.matmul

            def acquire(u):
                if u.reused:
                    pe.wait_ge(u.done, u.before)

            def transposed(name, src, ready, ident=None):
                def unit(ph, b, g):
                    pe.wait_ge(idents, 6)
                    pe.wait_ge(*ready)
                    for c in range(C):
                        u = use(ph, (name, 0), "M", c)
                        acquire(u)
                        for j in range(C):
                            i = nc.tensor.transpose(psM[:, u.slot, j * P:(j + 1) * P],
                                                    src[:, j, c * P:(c + 1) * P], id32[:, :])
                        i.then_inc(u.full, 1)
                return unit

            def gram(name, right, ready):
                def unit(ph, b, g):
                    pe.wait_ge(ld["tk"], 16)
                    pe.wait_ge(*ready)
                    for c in range(C):
                        u = use(ph, (name, 0), "M", c)
                        acquire(u)
                        for j in range(C):
                            i = mm(psM[:, u.slot, :], tk[:, j, c * P:(c + 1) * P], right[:, j, :],
                                   start=(j == 0), stop=(j == C - 1))
                        i.then_inc(u.full, 1)
                return unit

            def w1_transposed(ph, b, g):
                pe.wait_ge(idents, 6)
                pe.wait_ge(ld["w1"], 16)
                u = use(ph, ("W1T", 0), "M", 0)
                acquire(u)
                for j in range(C):
                    i = nc.tensor.transpose(psM[:, u.slot, j * P:(j + 1) * P], w1s[:, j * P:(j + 1) * P], id32[:, :])
                i.then_inc(u.full, 1)

            def chunked(u, left, right, parts):
                acquire(u)
                for c in range(C):
                    for j in range(parts):
                        i = mm(psM[:, u.slot, c * P:(c + 1) * P], left[:, j, c * P:(c + 1) * P], right(j),
                               start=(c == 0 and j == 0), stop=(j == parts - 1), skip_group_check=True)
                i.then_inc(u.full, 1)

            def a_init(ph, b, g):
                u = use(ph, ("W1T", 0), "M", 0)
                pe.wait_ge(u.done, u.before + 1)
                pe.wait_ge(ld["tk"], 16)
                chunked(use(ph, ("AINIT", 0), "M", 0), tk, lambda j: w1T[:, j, :], C)
                pe.wait_ge(ld["tq"], 16)
                chunked(use(ph, ("AINIT", 0), "M", 1), tq, lambda j: w1T[:, j, :], C)

            def w2_transposed(ph, b, g):
                pe.wait_ge(idents, 6)
                pe.wait_ge(ld["w2"], 16)
                u = use(ph, ("W2T0", 0), "M", 0)
                acquire(u)
                for j in range(C):
                    i = nc.tensor.transpose(psM[:, u.slot, j * P:(j + 1) * P], w2s[:, j, :], id32[:, :])
                i.then_inc(u.full, 1)

            def keys(ph, b, g):
                for n in ("CTXT", "WKT"):
                    for c in range(C):
                        u = use(ph, (n, 0), "M", c)
                        pe.wait_ge(u.done, u.before + 1)
                for m in range(C):
                    u = use(ph, ("KCTX", 0), "M", m)
                    acquire(u)
                    for c in range(C):
                        i = mm(psM[:, u.slot, :], wkT[:, c, m * P:(m + 1) * P], ctxT[:, c, :],
                               start=(c == 0), stop=(c == C - 1))
                    i.then_inc(u.full, 1)

            def values(ph, b, g):
                for c in range(C):
                    u = use(ph, ("WVT", 0), "M", c)
                    pe.wait_ge(u.done, u.before + 1)
                for r in range(C):
                    u = use(ph, ("VCTX", 0), "M", r)
                    acquire(u)
                    for c in range(C):
                        i = mm(psM[:, u.slot, :], ctxT[:, c, r * P:(r + 1) * P], wvT[:, c, :],
                               start=(c == 0), stop=(c == C - 1))
                    i.then_inc(u.full, 1)

            def mean(ph, b, g):
                u = use(ph, ("MEAN", g), "M", 0)
                acquire(u)
                pe.wait_ge(consts, CONSTS + 1)
                pe.wait_ge(abs_done, 2 * g + 2)
                mm(psM[:, u.slot, 0:1], ones32, asum[:, g, 0:1], start=True, stop=False)
                mm(psM[:, u.slot, 0:1], ones32, asum[:, g, 1:2], start=False, stop=True).then_inc(u.full, 1)

            def ternary(name, half):
                def unit(ph, b, g):
                    pe.wait_ge(tern_step, 4 * g + 2 * half + 2)
                    for k in range(4):
                        u = use(ph, (name, g), "T", k)
                        acquire(u)
                        for j in range(8):
                            if g == 0:
                                dc, fc = j // 2, 2 * k + j % 2
                                src = tern[:, fc * D + dc * P:fc * D + (dc + 1) * P]
                            else:
                                fc, dc = 4 * k + j // 2, j % 2
                                src = tern[:, dc * FF + fc * P:dc * FF + (fc + 1) * P]
                            i = nc.tensor.transpose(psT[:, u.slot, j * P:(j + 1) * P], src, id16[:, :])
                        i.then_inc(u.full, 1)
                return unit

            def tile_transposes(ln, name, src):
                def unit(ph, b, g):
                    for t in range(T4):
                        u = use(ph, (name, g), "T", t)
                        acquire(u)
                        s = use(setup if ph is first and ln == "L1b" else ph, (ln, g), "S", t)
                        pe.wait_ge(split, s.before + 1)
                        for k in range(2 * C):
                            i = nc.tensor.transpose(psT[:, u.slot, k * P:(k + 1) * P],
                                                    src(g, t, k // C)[:, (k % C) * P:(k % C + 1) * P], id16[:, :])
                        i.then_inc(u.full, 1)
                return unit

            def triple(dst, lhs, rhs, chunks, opened=False, closes=True):
                n = 0
                for c in range(chunks):
                    for l, r in PASSES:
                        n += 1
                        i = mm(dst, lhs(l, c), rhs(r, c), start=(n == 1 and not opened),
                               stop=(closes and n == 3 * chunks))
                return i

            def in_sbuf(ph, unit, n):
                for t in range(n - 2, n):
                    u = use(ph, unit, "T", t)
                    pe.wait_ge(u.done, u.before + 1)

            def pre(ph, b, g):
                if ph is first:
                    pe.wait_ge(init, 7)
                else:
                    pe.wait_ge(u1, b * U1_STEPS)
                in_sbuf(ph, ("T1", g), T4)
                u = use(ph, ("PRE", g), "M", 0)
                acquire(u)
                triple(psM[:, u.slot, :], lambda l, c: A16[:, l, c, :],
                       lambda r, c: xT1[:, r * C + c, g * GT:(g + 1) * GT], C).then_inc(u.full, 1)

            def dh(ph, b, g):
                if ph is body:
                    for s in range(4):
                        pe.wait_ge(done["M"][s], ph.start("M", s))
                us = [use(ph, ("DH", 0), "M", k) for k in range(G2)]
                for k, u in enumerate(us):
                    acquire(u)
                    triple(psM[:, u.slot, :], lambda l, c: P16[:, l, c, :],
                           lambda r, c: xT1[:, r * C + c, k * GT:(k + 1) * GT], C, closes=False)
                for k, u in enumerate(us):
                    s = use(ph, ("PRG", 0), "S", k)
                    pe.wait_ge(split, s.before + 1)
                    triple(psM[:, u.slot, :], lambda l, c: G16[:, l, :], lambda r, c: hT[:, k, r, :], 1,
                           opened=True).then_inc(u.full, 1)

            def h_transposes(ph, b, g):
                for t in range(TILES):
                    if t % T4 == 0:
                        pe.wait_ge(dp_split, 2 * b + t // T4 + 1)
                    u = use(ph, ("HT", 0), "T", t)
                    acquire(u)
                    for k, (src, hl) in enumerate(((dpT, HI), (hT, HI), (dpT, LO), (hT, LO))):
                        i = nc.tensor.transpose(psT[:, u.slot, k * P:(k + 1) * P],
                                                src[:, t // T4, hl, t % T4 * P:(t % T4 + 1) * P], id16[:, :])
                    i.then_inc(u.full, 1)

            def sums(ph, b, g):
                in_sbuf(ph, ("HT", 0), TILES)
                pe.wait_ge(ones_set, b + 1)
                u = use(ph, ("S", 0), "M", 0)
                acquire(u)
                for t in range(TILES):
                    h_hi, h_lo = nat[:, t, HI, HID:2 * HID], nat[:, t, LO, HID:2 * HID]
                    h_one = nat[:, t, HI, HID:2 * HID + 1]
                    mm(psM[:, u.slot, 0:HID + 1], h_hi, h_one, start=(t == 0), stop=False, skip_group_check=True)
                    mm(psM[:, u.slot, 0:HID + 1], h_lo, h_one, start=False, stop=False, skip_group_check=True)
                    mm(psM[:, u.slot, 0:HID], h_hi, h_lo, start=False, stop=False, skip_group_check=True)
                for t in range(TILES):
                    for hl in range(2):
                        i = mm(psM[:, u.slot, HID + 2:HID + 3], nat[:, t, hl, 0:HID],
                               nat[:, t, HI, 2 * HID:2 * HID + 1], start=False,
                               stop=(t == TILES - 1 and hl == 1), skip_group_check=True)
                i.then_inc(u.full, 1)
                for c in range(C):
                    u = use(ph, ("S", 0), "M", 1 + c)
                    acquire(u)
                    for t in range(TILES):
                        x_hi, x_lo = (xn1[:, hl, t, c * P:(c + 1) * P] for hl in range(2))
                        mm(psM[:, u.slot, 0:2 * HID + 1], x_hi, nat[:, t, HI, 0:2 * HID + 1], start=(t == 0),
                           stop=False, skip_group_check=True)
                        mm(psM[:, u.slot, 0:2 * HID], x_hi, nat[:, t, LO, 0:2 * HID], start=False, stop=False,
                           skip_group_check=True)
                        i = mm(psM[:, u.slot, 0:2 * HID + 1], x_lo, nat[:, t, HI, 0:2 * HID + 1], start=False,
                               stop=(t == TILES - 1), skip_group_check=True)
                    i.then_inc(u.full, 1)

            def update(ph, b, g):
                if ph is not first:
                    pe.wait_ge(dd_loaded, 32 * b)
                u = use(ph, ("U1", 0), "M", 0)
                acquire(u)
                r = use(ph, ("S", 0), "M", 0)
                pe.wait_ge(r.done, r.before + 1)
                for c in range(C):
                    r = use(ph, ("S", 0), "M", 1 + c)
                    pe.wait_ge(r.done, r.before + 1)
                    mm(psM[:, u.slot, :], s12[:, c, HID:2 * HID], dd[:, c, :], start=(c == 0), stop=False)
                mm(psM[:, u.slot, :], s3[:, 0:HID], w2T32[:, :], start=False, stop=True).then_inc(u.full, 1)
                pe.wait_ge(bc_ready, 2 * b + 2)
                u = use(ph, ("U1", 0), "M", 1)
                acquire(u)
                for c in range(C):
                    mm(psM[:, u.slot, :], sxb[:, c, :], dd[:, c, :], start=(c == 0), stop=False)
                mm(psM[:, u.slot, :], s4b, w2T32[:, :], start=False, stop=True).then_inc(u.full, 1)
                chunked(use(ph, ("U1", 0), "M", 2), kk, lambda j: s12[:, j, 0:HID], C)
                chunked(use(ph, ("U1", 0), "M", 3), kq, lambda j: s12[:, j, 0:HID], C)

            def new_w2(ph, b, g):
                pe.wait_ge(u1, b * U1_STEPS + 1)
                u = use(ph, ("U2", 0), "M", 0)
                acquire(u)
                for j in range(C):
                    i = nc.tensor.transpose(psM[:, u.slot, j * P:(j + 1) * P], w2T32[:, j * P:(j + 1) * P], id32[:, :])
                i.then_inc(u.full, 1)

            def new_pg(ph, b, g):
                if ph is setup:
                    pe.wait_ge(d_ready, 1)
                    left, new = dn, w2s
                else:
                    left, new = dd, w2n
                    u = use(ph, ("U2", 0), "M", 0)
                    pe.wait_ge(u.done, u.before + 1)
                    pe.wait_ge(dd_loaded, 32 * b + 16)
                chunked(use(ph, ("U3", 0), "M", 0), left, lambda j: new[:, j, :], C)
                u = use(ph, ("U3", 0), "M", 1)
                acquire(u)
                for j in range(C):
                    i = mm(psM[:, u.slot, 0:HID], new[:, j, :], new[:, j, :], start=(j == 0), stop=(j == C - 1))
                i.then_inc(u.full, 1)

            def pre2(ph, b, g):
                pe.wait_ge(u1, (b + 1) * U1_STEPS)
                u = use(ph, ("A3P", g), "M", 0)
                acquire(u)
                triple(psM[:, u.slot, :], lambda l, c: Aq16[:, l, c, :],
                       lambda r, c: xT1[:, r * C + c, g * GT:(g + 1) * GT], C).then_inc(u.full, 1)

            def mlp_out(name, first_tile):
                def unit(ph, b, g):
                    for k in range(2):
                        t = first_tile + k
                        u = use(ph, (name, g), "O", k)
                        acquire(u)
                        tok = slice(g * GT + t * P, g * GT + (t + 1) * P)
                        triple(psO[:, u.slot, :], lambda l, c: xT1[:, l * C + c, tok], lambda r, c: tqT[:, r, c, :], C,
                               closes=False)
                        if t == 0:
                            s = use(ph, ("A3P", g), "S", 0)
                            pe.wait_ge(split, s.before + 1)
                        triple(psO[:, u.slot, :], lambda l, c: h2[:, l, t * P:(t + 1) * P],
                               lambda r, c: w2T16[:, r, :], 1, opened=True).then_inc(u.full, 1)
                return unit

            def queries(ph, c_, g):
                in_sbuf(ph, ("T2", g), T4)
                for m in range(C):
                    u = use(ph, ("Q", g), "M", m)
                    acquire(u)
                    triple(psM[:, u.slot, :], lambda l, c: wqT[:, l, c, m * P:(m + 1) * P],
                           lambda r, c: xTQ[:, r * C + c, :], C).then_inc(u.full, 1)

            def guard(ph, c_, g):
                if g == 0:
                    pe.wait_ge(ctx_loaded, 160 * c_ + 160)
                s = use(ph, ("Q", g), "S", C - 1)
                pe.wait_ge(split, s.before + 1)
                for t in range(T4):
                    for i in range(2):
                        u = use(ph, ("GUARD", g), "O", 2 * t + i)
                        acquire(u)
                        for k in range(2):
                            m = 2 * i + k
                            mm(psO[:, u.slot, k * 256:(k + 1) * 256], qs[:, HI, m, t * P:(t + 1) * P],
                               kbd[:, HI, m, :], start=(k == 0), stop=False, skip_group_check=True)
                        mm(psO[:, u.slot, :].rearrange("p (h k) -> p h k", k=KEYS), ones_row[:, :],
                           mrow[:, :].rearrange("p (a k) -> p a k", a=1).broadcast_to([1, 8, KEYS]), start=False, stop=True,
                           skip_group_check=True).then_inc(u.full, 1)

            def guard_transposes(ph, c_, g):
                for k in range(6, 8):
                    u = use(ph, ("GUARD", g), "O", k)
                    pe.wait_ge(u.done, u.before + 1)
                u = use(ph, ("GT", g), "T", 0)
                acquire(u)
                for t in range(T4):
                    i = nc.tensor.transpose(psT[0:HEADS, u.slot, t * P:(t + 1) * P].bitcast(BF16), gm[:, t, :], idbf[:, :])
                i.then_inc(u.full, 1)

            def scores(ph, c_, g):
                u = use(ph, ("GT", g), "T", 0)
                pe.wait_ge(u.done, u.before + 1)
                for q in range(PAIRS):
                    m, half = q // 2, slice((q % 2) * P, (q % 2 + 1) * P)
                    u = use(ph, ("ST", g), "M", q)
                    acquire(u)
                    triple(psM[:, u.slot, :], lambda l, c: kbd[:, l, m, half], lambda r, c: qs[:, r, m, :], 1,
                           closes=False)
                    mm(psM[:, u.slot, :], neg_ind[:, q * P:(q + 1) * P], gT, start=False,
                       stop=True).then_inc(u.full, 1)

            def weighted_values(ph, c_, g):
                for t in range(T4):
                    for i in range(2):
                        u = use(ph, ("PV", g), "O", 2 * t + i)
                        acquire(u)
                        n = 0
                        for k in range(4):
                            q = 4 * i + k
                            if t == 0:
                                s = use(ph, ("ST", g), "S", q)
                                pe.wait_ge(split, s.before + 1)
                            for l, r in PASSES:
                                ins = mm(psO[:, u.slot, k * 66:(k + 1) * 66], es[:, l, q, t * P:(t + 1) * P],
                                         vbd[:, r, q, :], start=(n == 0), stop=(n == 11), skip_group_check=True)
                                n += 1
                        ins.then_inc(u.full, 1)

            def ffn1(name, first_chunk):
                def unit(ph, c_, g):
                    for k in range(4):
                        f = first_chunk + k
                        u = use(ph, (name, g), "M", k)
                        waits = [(u.done, u.before)]
                        if f == 0 and g == 0:
                            waits += [(done["T"][s], ph.start("T", s)) for s in range(2)]
                        elif f == 0:
                            for t in range(T4 - 2, T4):
                                tr = use(ph, ("T3", g), "T", t)
                                waits.append((tr.done, tr.before + 1))
                        held(pe, waits)
                        for c in range(C):
                            for hl in range(2):
                                i = mm(psM[:, u.slot, :], fw1T[:, c, f * P:(f + 1) * P], xTF[:, hl * C + c, :],
                                       start=(c == 0 and hl == 0), stop=(c == C - 1 and hl == 1))
                        i.then_inc(u.full, 1)
                return unit

            def ffn2(name, half, first_tile):
                def unit(ph, c_, g):
                    for k in range(2):
                        t = first_tile + k
                        u = use(ph, (name, g), "O", k)
                        for f in range(FCH // 2):
                            waits = [(u.done, u.before)] if f == 0 else []
                            if t == 0:
                                chunk = ("F1" + "abcd"[2 * half + f // 4], g)
                                s = use(ph, chunk, "S", f % 4)
                                waits.append((split, s.before + 1))
                            if waits:
                                held(pe, waits)
                            for hl in range(2):
                                i = mm(psO[:, u.slot, :], hF[:, f, hl, t * P:(t + 1) * P],
                                       fw2T[:, half * FCH // 2 + f, :], start=(f == 0 and hl == 0),
                                       stop=(f == FCH // 2 - 1 and hl == 1))
                        i.then_inc(u.full, 1)
                return unit

            run(pe, {
                "K": gram("K", tk, (ld["tk"], 16)), "KQ": gram("KQ", tq, (ld["tq"], 16)),
                "DT": transposed("DT", dn, (d_ready, 1)), "TQT": transposed("TQT", tq, (ld["tq"], 16)),
                "WQT": transposed("WQT", wqs, (ld["wq"], 16)), "WKT": transposed("WKT", wks, (ld["wk"], 16)),
                "WVT": transposed("WVT", wvs, (ld["wv"], 16)), "CTXT": transposed("CTXT", ctxs, (ld["ctx"], 16)),
                "W1T": w1_transposed, "AINIT": a_init, "W2T0": w2_transposed, "KCTX": keys, "VCTX": values,
                "MEAN": mean, "TERa": ternary("TERa", 0), "TERb": ternary("TERb", 1),
                "T1": tile_transposes("L1b", "T1", lambda g, t, hl: xn1[:, hl, g * T4 + t, :]),
                "T2": tile_transposes("L2b", "T2", lambda g, t, hl: xnX[:, hl, t, :]),
                "T3": tile_transposes("L3b", "T3", lambda g, t, hl: xnX[:, hl, t, :]),
                "PRE": pre, "DH": dh, "HT": h_transposes, "S": sums, "U1": update, "U2": new_w2, "U3": new_pg,
                "A3P": pre2, "A3Oa": mlp_out("A3Oa", 0), "A3Ob": mlp_out("A3Ob", 2), "Q": queries, "GUARD": guard,
                "GT": guard_transposes, "ST": scores, "PV": weighted_values,
                "F1a": ffn1("F1a", 0), "F1b": ffn1("F1b", 4), "F1c": ffn1("F1c", 8), "F1d": ffn1("F1d", 12),
                "F2a": ffn2("F2a", 0, 0), "F2b": ffn2("F2b", 0, 2), "F2c": ffn2("F2c", 1, 0), "F2d": ffn2("F2d", 1, 2),
            })

        @block.scalar
        def _(act):
            activation = nc.scalar.activation

            def copied(name, dst):
                def unit(ph, b, g):
                    for c in range(C):
                        u = use(ph, (name, 0), "M", c)
                        act.wait_ge(u.full, u.before + 1)
                        activation(dst[:, c, :], psM[:, u.slot, :], ACT.Copy).then_inc(u.done, 1)
                return unit

            def weight_hi(name, dst):
                def unit(ph, b, g):
                    for c in range(C):
                        u = use(ph, (name, 0), "M", c)
                        act.wait_ge(u.full, u.before + 1)
                        activation(dst[:, HI, c, :], psM[:, u.slot, :], ACT.Copy, scale=WSCALE).then_inc(wt_hi, 1)
                return unit

            def one_block(name, dst):
                def unit(ph, b, g):
                    u = use(ph, (name, 0), "M", 0)
                    act.wait_ge(u.full, u.before + 1)
                    activation(dst, psM[:, u.slot, :].rearrange("p (j h) -> p j h", j=C), ACT.Copy).then_inc(u.done, 1)
                return unit

            def magnitudes(ph, b, g):
                if g == 0:
                    u = use(setup, ("VCTX", 0), "M", C - 1)
                else:
                    u = use(ph, ("TERb", 0), "T", 3)
                act.wait_ge(u.full, u.before + 1)
                for half in range(2):
                    act.wait_ge(ld[f"fw{g + 1}_{half}"], 16)
                    if g + half:
                        act.wait_ge(abs_done, 2 * g + half)
                    activation(tern, ffs[g][half], ACT.Abs, accum_out=asum[:, g, half:half + 1]).then_inc(abs_done, 1)

            def ternary(name, half):
                def unit(ph, b, g):
                    for k in range(4):
                        u = use(ph, (name, g), "T", k)
                        act.wait_ge(u.full, u.before + 1)
                        if g == 0:
                            f = half * FF // 2 + k * 2 * P
                            dst = fw1T[:, :, f:f + 2 * P]
                            src = psT[:, u.slot, :].rearrange("p (c f) -> p c f", c=C)
                        else:
                            dst = fw2T[:, 4 * k:4 * k + 4, half * D // 2:(half + 1) * D // 2]
                            src = psT[:, u.slot, :].rearrange("p (c f) -> p c f", c=4)
                        activation(dst, src, ACT.Copy, saturate=False).then_inc(u.done, 1)
                return unit

            def stage_free(ph, unit, i):
                s = use(ph, unit, "S", i)
                if not (isinstance(s.before, int) and s.before < RINGS["S"]):
                    act.wait_ge(split, s.before - (RINGS["S"] - 1))
                return stage[:, s.slot, :]

            def normalized(k, name, src):
                def unit(ph, b, g):
                    act.wait_ge(lnp[k], LN_STEPS * (2 * b + g + 1))
                    for t in range(T4):
                        dst = stage_free(ph, (name, g), t)
                        activation(dst, src[:, g * T4 + t, :], ACT.Identity, bias=nm[:, k, g, t:t + 1],
                                   scale=rs[:, k, g, t:t + 1]).then_inc(staged, 1)
                return unit

            def collect(name, dst):
                def unit(ph, b, g):
                    if ph is first and name == "T1":
                        act.wait_ge(scr_stored, STORED)
                    for t in range(T4):
                        u = use(ph, (name, g), "T", t)
                        act.wait_ge(u.full, u.before + 1)
                        activation(dst(g, t), psT[:, u.slot, :].rearrange("p (a d) -> p a d", d=P),
                                   ACT.Copy).then_inc(u.done, 1)
                return unit

            def hidden(ph, b, g):
                for k in range(G2):
                    act.wait_ge(u_step, 6 * b + 3 * k + 3)
                    activation(ee[:, k, :], un[:, k, :], ACT.Square).then_inc(e_step, 1)
                for k in range(G2):
                    act.wait_ge(e_step, 4 * b + k + 1)
                    activation(ee[:, k, :], ee[:, k, :], ACT.Exp, scale=-0.5).then_inc(e_step, 1)
                for k in range(G2):
                    dst = stage_free(ph, ("PRG", 0), k)
                    activation(dst, un[:, k, :], ACT.Gelu).then_inc(h_staged, 1)

            def token_major(ph, b, g):
                for t in range(TILES):
                    u = use(ph, ("HT", 0), "T", t)
                    act.wait_ge(u.full, u.before + 1)
                    activation(nat[:, t, :, 0:2 * HID], psT[:, u.slot, 0:4 * P].rearrange("p (a d) -> p a d", a=2),
                               ACT.Copy).then_inc(u.done, 1)

            def new_hidden(ph, b, g):
                u = use(ph, ("A3P", g), "M", 0)
                act.wait_ge(u.full, u.before + 1)
                dst = stage_free(ph, ("A3P", g), 0)
                activation(dst, psM[:, u.slot, :], ACT.Gelu, bias=b1c[:, :], scale=1.0 / WSCALE).then_inc(u.done, 1)

            def queries(ph, c_, g):
                for m in range(C):
                    u = use(ph, ("Q", g), "M", m)
                    act.wait_ge(u.full, u.before + 1)
                    dst = stage_free(ph, ("Q", g), m)
                    activation(dst, psM[:, u.slot, :], ACT.Identity, bias=bqc[:, m:m + 1],
                               scale=1.0 / WSCALE).then_inc(u.done, 1)

            def guard_rows(ph, c_, g):
                u = use(ph, ("GT", g), "T", 0)
                act.wait_ge(u.full, u.before + 1)
                activation(gT, psT[0:HEADS, u.slot, 0:GT].bitcast(BF16), ACT.Copy).then_inc(u.done, 1)

            def exponentials(ph, c_, g):
                for q in range(PAIRS):
                    u = use(ph, ("ST", g), "M", q)
                    act.wait_ge(u.full, u.before + 1)
                    dst = stage_free(ph, ("ST", g), q)
                    activation(dst, psM[:, u.slot, :], ACT.Exp, bias=mbc[:, :], scale=1.0 / SQW).then_inc(u.done, 1)

            def ffn_hidden(name, first_chunk):
                def unit(ph, c_, g):
                    for k in range(4):
                        f = first_chunk + k
                        u = use(ph, (name, g), "M", k)
                        act.wait_ge(u.full, u.before + 1)
                        dst = stage_free(ph, (name, g), k)
                        activation(dst, psM[:, u.slot, :], ACT.Gelu, bias=fb1c[:, f:f + 1]).then_inc(u.done, 1)
                return unit

            act.wait_ge(ld["small"], 112)
            run(act, {
                "K": copied("K", kk), "KQ": copied("KQ", kq), "DT": copied("DT", dd), "TQT": weight_hi("TQT", tqT),
                "W1T": one_block("W1T", w1T), "WQT": weight_hi("WQT", wqT), "WKT": copied("WKT", wkT),
                "WVT": copied("WVT", wvT), "CTXT": copied("CTXT", ctxT), "MEAN": magnitudes,
                "TERa": ternary("TERa", 0), "TERb": ternary("TERb", 1),
                "L1b": normalized(0, "L1b", xin), "L2b": normalized(1, "L2b", x1), "L3b": normalized(2, "L3b", x1),
                "T1": collect("T1", lambda g, t: xT1[:, :, g * GT + t * P:g * GT + (t + 1) * P]),
                "T2": collect("T2", lambda g, t: xTQ[:, :, t * P:(t + 1) * P]),
                "T3": collect("T3", lambda g, t: xTF[:, :, t * P:(t + 1) * P]),
                "PRG": hidden, "HT": token_major, "U2": one_block("U2", w2n), "A3P": new_hidden, "Q": queries,
                "GT": guard_rows, "ST": exponentials,
                "F1a": ffn_hidden("F1a", 0), "F1b": ffn_hidden("F1b", 4), "F1c": ffn_hidden("F1c", 8),
                "F1d": ffn_hidden("F1d", 12),
            })

        @block.gpsimd
        def _(pool):
            for m in (id16, idbf, id32):
                nc.gpsimd.memset(m[:, :], 0.0).then_inc(idents, 1)
            pool.wait_ge(idents, 3)
            for m in (id16, idbf, id32):
                nc.gpsimd.affine_select(out=m[:, :], in_=m[:, :], compare_op=ALU.not_equal, fill=1.0, base=0,
                                        pattern=[[-1, P]], channel_multiplier=1).then_inc(idents, 1)
            nc.gpsimd.memset(ones_row[:, :], 1.0).then_inc(consts, 1)
            nc.gpsimd.memset(neghalf[:, :], -0.5).then_inc(consts, 1)
            nc.gpsimd.memset(minus1[:, :], -1.0).then_inc(consts, 1)
            nc.gpsimd.memset(eps[:, :], EPS).then_inc(consts, 1)
            nc.gpsimd.memset(neg_ind[:, :], -1.0).then_inc(consts, 1)
            nc.gpsimd.memset(kbd[:, :, :, :], 0.0).then_inc(consts, 1)
            nc.gpsimd.memset(vbd[:, :, :, :], 0.0).then_inc(consts, 1)
            pool.wait_ge(consts, 7)
            for j in range(2):
                one = j * (W + 1) + W
                nc.gpsimd.memset(vbd[j * KEYS:(j + 1) * KEYS, HI, :, one:one + 1], 1.0).then_inc(consts, 1)
            nc.gpsimd.affine_select(out=neg_ind[:, :], in_=neg_ind[:, :], compare_op=ALU.is_ge, fill=0.0, base=0,
                                    pattern=[[1, PAIRS * P]], channel_multiplier=-KEYS).then_inc(consts, 1)
            pool.wait_ge(consts, 10)
            nc.gpsimd.affine_select(out=neg_ind[:, :], in_=neg_ind[:, :], compare_op=ALU.is_ge, fill=0.0,
                                    base=KEYS - 1, pattern=[[-1, PAIRS * P]], channel_multiplier=KEYS).then_inc(consts, 1)
            pool.wait_ge(ld["small"], 112)
            pool.wait_ge(consts, CONSTS)

            def rsqrt(k):
                def unit(ph, b, g):
                    tt, at = nc.gpsimd.tensor_tensor, LN_STEPS * (2 * b + g)
                    pool.wait_ge(stats[k], 2 * b + g + 1)
                    tt(ve[:, k, :], mv[:, k, :, 1], eps[:, :], ALU.add).then_inc(lnp[k], 1)
                    tt(nm[:, k, g, :], mv[:, k, :, 0], minus1[:, :], ALU.mult).then_inc(lnp[k], 1)
                    pool.wait_ge(lnp[k], at + 1)
                    tt(rs[:, k, g, :], ve[:, k, :], neghalf[:, :], ALU.pow).then_inc(lnp[k], 1)
                    pool.wait_ge(lnp[k], at + 3)
                    tt(nm[:, k, g, :], nm[:, k, g, :], rs[:, k, g, :], ALU.mult).then_inc(lnp[k], 1)
                return unit

            def ones(ph, b, g):
                if g == 0:
                    pool.wait_ge(scr_stored, STORED)
                    nc.gpsimd.memset(ones32, 1.0).then_inc(consts, 1)

            def add_b2(ph, b, g):
                if g == 0:
                    pool.wait_ge(u1, b * U1_STEPS + 2)
                for t in range(T4):
                    xt = xin[:, g * T4 + t, :]
                    nc.gpsimd.tensor_tensor(xt, xt, b2b[:, :], ALU.add).then_inc(xa_done, 1)

            def add_attention(ph, c_, g):
                for t in range(T4):
                    for i in range(2):
                        u = use(ph, ("PV", g), "O", 2 * t + i)
                        pool.wait_ge(u.done, u.before + 1)
                        xt = x1[:, g * T4 + t, i * 256:(i + 1) * 256]
                        nc.gpsimd.tensor_tensor(xt, xt, obuf[:, i, :, :].rearrange("p h w -> p (h w)"),
                                                ALU.add).then_inc(o_done, 1)

            def add_fb2(ph, c_, g):
                for t in range(T4):
                    s = use(ph, ("L3b", g), "S", t)
                    pool.wait_ge(hi_done, s.before + 1)
                    xt = x1[:, g * T4 + t, :]
                    nc.gpsimd.tensor_tensor(xt, xt, fb2b[:, :], ALU.add).then_inc(xf_done, 1)

            run(pool, {"FW": ones, "L1a": rsqrt(0), "L2a": rsqrt(1), "L3a": rsqrt(2), "A3P": add_b2, "PV": add_attention,
                       "T3": add_fb2})

        @block.vector
        def _(dve):
            v = nc.vector

            def d_and_masks(ph, b, g):
                dve.wait_ge(ld["tk"], 16)
                dve.wait_ge(ld["tv"], 16)
                v.tensor_tensor(dn, tk, dn, ALU.subtract).then_inc(d_ready, 1)
                dve.wait_ge(ld["mask"], 48)
                v.tensor_copy(mf, mi).then_inc(mask_step, 1)
                v.tensor_copy(mcf[:, :], mci[:, :]).then_inc(mask_step, 1)
                dve.wait_ge(mask_step, 2)
                mfb = mf.rearrange("p (b k) -> p b k", b=B)
                v.tensor_reduce(mx[:, :], mfb, AX.X, ALU.max).then_inc(mask_step, 1)
                dve.wait_ge(mask_step, 3)
                v.tensor_tensor(mcf[:, :], mcf[:, :], mx[:, :], ALU.subtract).then_inc(mask_step, 1)
                v.tensor_tensor(mfb[0:1], mfb[0:1], mx[0:1, :].rearrange("p (b a) -> p b a", a=1).broadcast_to([1, B, KEYS]),
                                ALU.subtract).then_inc(mask_step, 1)
                dve.wait_ge(mask_step, 5)
                v.tensor_scalar(mcf[:, :], mcf[:, :], MASKED, None, ALU.mult).then_inc(mask_step, 1)
                v.tensor_scalar(mr16[:, :, :], mfb[0:1], MASKED * SQW, -60000.0, ALU.mult, ALU.max).then_inc(mask_step, 1)

            weights_seen = [0]

            def weight_lo(name, dst):
                def unit(ph, b, g):
                    for c in range(C):
                        u = use(ph, (name, 0), "M", c)
                        weights_seen[0] += 1
                        dve.wait_ge(wt_hi, weights_seen[0])
                        v.scalar_tensor_tensor(out=dst[:, LO, c, :], in0=psM[:, u.slot, :], scalar=WSCALE,
                                               in1=dst[:, HI, c, :], op0=ALU.mult, op1=ALU.subtract).then_inc(u.done, 1)
                return unit

            def flat(ap):
                return ap.rearrange("p c h -> p (c h)")

            def a_init(ph, b, g):
                dve.wait_ge(ld["small"], 112)
                step = 0
                for k, (f32, f16, scale) in enumerate(((A32, A16, 1.0), (Aq32, Aq16, WSCALE))):
                    u = use(ph, ("AINIT", 0), "M", k)
                    dve.wait_ge(u.full, u.before + 1)
                    v.tensor_copy(flat(f32[:, :, :]), psM[:, u.slot, :]).then_inc(u.done, 1)
                    dve.wait_ge(u.done, u.before + 1)
                    v.tensor_scalar(f16[:, HI], f32[:, :, :], scale, None, ALU.mult).then_inc(init, 1)
                    dve.wait_ge(init, step + 1)
                    v.scalar_tensor_tensor(out=f16[:, LO], in0=f32[:, :, :], scalar=scale, in1=f16[:, HI],
                                           op0=ALU.mult, op1=ALU.subtract).then_inc(init, 1)
                    step += 2

            def w2_init(ph, b, g):
                u = use(ph, ("W2T0", 0), "M", 0)
                dve.wait_ge(u.full, u.before + 1)
                v.tensor_copy(w2T32[:, :], psM[:, u.slot, :]).then_inc(u.done, 1)
                dve.wait_ge(u.done, u.before + 1)
                v.tensor_scalar(w2T16[:, HI], w2T32[:, :], WSCALE, None, ALU.mult).then_inc(init, 1)
                dve.wait_ge(init, 5)
                v.scalar_tensor_tensor(out=w2T16[:, LO], in0=w2T32[:, :], scalar=WSCALE, in1=w2T16[:, HI],
                                       op0=ALU.mult, op1=ALU.subtract).then_inc(init, 1)
                v.tensor_tensor_reduce(out=cjunk, in0=w2T32[:, :],
                                       in1=b2b[:, :], scale=1.0, scalar=0.0, op0=ALU.mult, op1=ALU.add,
                                       accum_out=cc[:, :]).then_inc(init, 1)

            def new_pg(ph, b, g):
                at = 0 if ph is setup else 2 * b + 2
                for k, (dst, cols) in enumerate(((P16, C * HID), (G16, HID))):
                    u = use(ph, ("U3", 0), "M", k)
                    dve.wait_ge(u.full, u.before + 1)
                    hi = dst[:, HI] if k else flat(dst[:, HI])
                    lo = dst[:, LO] if k else flat(dst[:, LO])
                    v.tensor_copy(hi, psM[:, u.slot, 0:cols]).then_inc(u3, 1)
                    dve.wait_ge(u3, at + k + 1)
                    v.tensor_tensor(lo, psM[:, u.slot, 0:cols], hi, ALU.subtract).then_inc(u.done, 1)
                if ph is setup:
                    for k in range(2):
                        u = use(ph, ("U3", 0), "M", k)
                        dve.wait_ge(u.done, u.before + 1)

            def keys(ph, b, g):
                dve.wait_ge(scr_stored, 48)
                for m in range(C):
                    u = use(ph, ("KCTX", 0), "M", m)
                    dve.wait_ge(u.full, u.before + 1)
                    v.tensor_scalar(kTs[:, HI, m, :], psM[:, u.slot, :], bkc[:, m:m + 1], None, ALU.add).then_inc(kv_hi, 1)
                    dve.wait_ge(kv_hi, m + 1)
                    v.scalar_tensor_tensor(out=kTs[:, LO, m, :], in0=psM[:, u.slot, :], scalar=bkc[:, m:m + 1],
                                           in1=kTs[:, HI, m, :], op0=ALU.add, op1=ALU.subtract).then_inc(u.done, 1)

            def values(ph, b, g):
                for r in range(C):
                    u = use(ph, ("VCTX", 0), "M", r)
                    dve.wait_ge(u.full, u.before + 1)
                    if r:
                        dve.wait_ge(v_split, r)
                    v.tensor_tensor(v32, psM[:, u.slot, :], bvb, ALU.add).then_inc(u.done, 1)
                    dve.wait_ge(u.done, u.before + 1)
                    v.tensor_copy(vs[:, r, HI, :], v32).then_inc(kv_hi, 1)
                    dve.wait_ge(kv_hi, C + r + 1)
                    v.tensor_tensor(vs[:, r, LO, :], v32, vs[:, r, HI, :], ALU.subtract).then_inc(v_split, 1)

            def threshold(ph, b, g):
                u = use(ph, ("MEAN", g), "M", 0)
                dve.wait_ge(u.full, u.before + 1)
                v.tensor_scalar(thr[:, g, 0:1], psM[:, u.slot, 0:1], 1.0 / (FF * D), 1e-8, ALU.mult,
                                ALU.max).then_inc(u.done, 1)
                dve.wait_ge(u.done, u.before + 1)
                v.tensor_scalar(thr[:, g, 1:2], thr[:, g, 0:1], 0.5, None, ALU.mult).then_inc(thr_step, 1)
                v.tensor_scalar(thr[:, g, 2:3], thr[:, g, 0:1], -0.5, None, ALU.mult).then_inc(thr_step, 1)

            def ternary(name, half):
                def unit(ph, b, g):
                    w, at = ffs[g][half], 4 * g + 2 * half
                    dve.wait_ge(thr_step, 2 * g + 2)
                    if half:
                        for k in range(2, 4):
                            u = use(ph, ("TERa", g), "T", k)
                            dve.wait_ge(u.full, u.before + 1)
                    v.tensor_scalar(tern, w, thr[:, g, 2:3], None, ALU.is_lt).then_inc(tern_step, 1)
                    dve.wait_ge(tern_step, at + 1)
                    v.scalar_tensor_tensor(out=tern, in0=w, scalar=thr[:, g, 1:2], in1=tern, op0=ALU.is_gt,
                                           op1=ALU.subtract).then_inc(tern_step, 1)
                return unit

            def split_stage(s, hi, lo):
                src = stage[:, s.slot, :]
                v.tensor_copy(hi, src).then_inc(hi_done, 1)
                dve.wait_ge(hi_done, s.before + 1)
                v.tensor_tensor(lo, src, hi, ALU.subtract).then_inc(split, 1)

            def moments(k, name, src):
                def unit(ph, b, g):
                    if name == "L1a":
                        dve.wait_ge(x_loaded[g], 16 * b + 16)
                    elif name == "L3a":
                        dve.wait_ge(o_done, 16 * b + 8 * g + 8)
                    else:
                        for t in range(2):
                            u = use(ph, ("A3Ob", g), "O", t)
                            dve.wait_ge(u.done, u.before + 1)
                    for t in range(T4):
                        i = v.bn_stats(st[:, k, t, :], src[:, g * T4 + t, :])
                    i.then_inc(bn[k], 1)
                    held(dve, [(bn[k], 2 * b + g + 1)])
                    for t in range(T4):
                        i = v.bn_aggr(mv[:, k, t, :], st[:, k, t, :])
                    i.then_inc(stats[k], 1)
                return unit

            def normalized(name, dst):
                def unit(ph, b, g):
                    if ph is first and name == "L2b":
                        dve.wait_ge(scr_stored, STORED)
                    for t in range(T4):
                        dve.wait_ge(staged, staged_before(ph, (name, g)) + t + 1)
                        split_stage(use(ph, (name, g), "S", t), dst(g, t, HI), dst(g, t, LO))
                return unit

            LN_ORDER = [(ph, [u for u in ph.order if u[0] in ("L1b", "L2b", "L3b")])
                        for ph in (setup, first, body, last)]

            def staged_before(ph, unit):
                n = 0
                for p, order in LN_ORDER:
                    if p is ph:
                        turns = p.turn if p is body else 0
                        return turns * (T4 * len(order)) + n + T4 * order.index(unit)
                    n += T4 * len(order) * (B - 1 if p is body else 1)

            def hidden(ph, b, g):
                u = use(ph, ("PRE", g), "M", 0)
                dve.wait_ge(u.full, u.before + 1)
                v.tensor_scalar(un[:, g, :], psM[:, u.slot, :], b1c[:, :], None, ALU.add).then_inc(u.done, 1)
                dve.wait_ge(u.done, u.before + 1)
                v.tensor_tensor(ee[:, g, :], un[:, g, :], un[:, g, :], ALU.mult).then_inc(u_step, 1)
                dve.wait_ge(u_step, 6 * b + 3 * g + 1)
                v.tensor_scalar(ee[:, g, :], ee[:, g, :], TINY * TINY, 4 * TINY, ALU.is_le, ALU.mult).then_inc(u_step, 1)
                dve.wait_ge(u_step, 6 * b + 3 * g + 2)
                v.tensor_tensor(un[:, g, :], ee[:, g, :], un[:, g, :], ALU.add).then_inc(u_step, 1)

            def gelu_and_slope(ph, b, g):
                for k in range(G2):
                    at = 6 * b + 3 * k
                    dve.wait_ge(u_step, 6 * b + 3 * k + 3)
                    v.reciprocal(gp[:, k, :], un[:, k, :]).then_inc(gp_step, 1)
                    s = use(ph, ("PRG", 0), "S", k)
                    h = stage[:, s.slot, :]
                    dve.wait_ge(h_staged, 2 * b + k + 1)
                    v.tensor_copy(hT[:, k, HI, :], h).then_inc(hi_done, 1)
                    dve.wait_ge(gp_step, at + 1)
                    v.tensor_tensor(gp[:, k, :], h, gp[:, k, :], ALU.mult).then_inc(gp_step, 1)
                    dve.wait_ge(hi_done, s.before + 1)
                    v.tensor_tensor(hT[:, k, LO, :], h, hT[:, k, HI, :], ALU.subtract).then_inc(split, 1)
                    dve.wait_ge(e_step, 4 * b + k + 3)
                    v.scalar_tensor_tensor(out=ee[:, k, :], in0=ee[:, k, :], scalar=INV_SQRT_2PI, in1=un[:, k, :],
                                           op0=ALU.mult, op1=ALU.mult).then_inc(gp_step, 1)
                    dve.wait_ge(gp_step, at + 3)
                    v.tensor_tensor(gp[:, k, :], gp[:, k, :], ee[:, k, :], ALU.add).then_inc(gp_ready, 1)

            def hidden_gradient(ph, b, g):
                dve.wait_ge(gp_ready, 2 * b + 2)
                v.memset(nat[:, :, HI, 2 * HID:2 * HID + 2], 1.0).then_inc(ones_set, 1)
                if ph is body:
                    dve.wait_ge(u1, b * U1_STEPS)
                for k in range(G2):
                    u = use(ph, ("DH", 0), "M", k)
                    dve.wait_ge(u.full, u.before + 1)
                    v.scalar_tensor_tensor(out=gp[:, k, :], in0=psM[:, u.slot, :], scalar=cc[:, :], in1=gp[:, k, :],
                                           op0=ALU.add, op1=ALU.mult).then_inc(u.done, 1)
                    dve.wait_ge(u.done, u.before + 1)
                    v.tensor_copy(dpT[:, k, HI, :], gp[:, k, :]).then_inc(dp_hi, 1)
                    dve.wait_ge(dp_hi, 2 * b + k + 1)
                    v.tensor_tensor(dpT[:, k, LO, :], gp[:, k, :], dpT[:, k, HI, :], ALU.subtract).then_inc(dp_split, 1)

            def sums(ph, b, g):
                u = use(ph, ("S", 0), "M", 0)
                dve.wait_ge(u.full, u.before + 1)
                v.tensor_copy(s3[:, 0:HID + 1], psM[:, u.slot, 0:HID + 1])
                v.tensor_copy(s3[:, HID + 2:HID + 3], psM[:, u.slot, HID + 2:HID + 3]).then_inc(u.done, 1)
                dve.wait_ge(u.done, u.before + 1)
                v.tensor_copy(s4b, s3[:, HID:HID + 1].broadcast_to([P, P])).then_inc(bc_ready, 1)
                for c in range(C):
                    u = use(ph, ("S", 0), "M", 1 + c)
                    dve.wait_ge(u.full, u.before + 1)
                    v.tensor_copy(s12[:, c, 0:2 * HID + 1], psM[:, u.slot, 0:2 * HID + 1]).then_inc(u.done, 1)
                dve.wait_ge(u.done, u.before + 1)
                v.tensor_copy(sxb, s12[:, :, 2 * HID:2 * HID + 1].broadcast_to([P, C, P])).then_inc(bc_ready, 1)

            def update(ph, b, g):
                at = b * U1_STEPS
                m = [use(ph, ("U1", 0), "M", k) for k in range(4)]
                dve.wait_ge(m[0].full, m[0].before + 1)
                v.scalar_tensor_tensor(out=tw, in0=b2b[:, :], scalar=s3[:, HID:HID + 1], in1=psM[:, m[0].slot, :],
                                       op0=ALU.mult, op1=ALU.add).then_inc(m[0].done, 1)
                dve.wait_ge(m[1].full, m[1].before + 1)
                v.scalar_tensor_tensor(out=tb, in0=b2b[:, :], scalar=float(N), in1=psM[:, m[1].slot, :],
                                       op0=ALU.mult, op1=ALU.add).then_inc(m[1].done, 1)
                dve.wait_ge(m[0].done, m[0].before + 1)
                v.scalar_tensor_tensor(out=w2T32[:, :], in0=tw, scalar=-ETA, in1=w2T32[:, :], op0=ALU.mult,
                                       op1=ALU.add).then_inc(u1, 1)
                dve.wait_ge(m[1].done, m[1].before + 1)
                v.scalar_tensor_tensor(out=b2b[:, :], in0=tb, scalar=-ETA, in1=b2b[:, :], op0=ALU.mult,
                                       op1=ALU.add).then_inc(u1, 1)
                v.scalar_tensor_tensor(out=b1c[:, :], in0=s3[:, HID + 2:HID + 3], scalar=-ETA, in1=b1c[:, :],
                                       op0=ALU.mult, op1=ALU.add).then_inc(u1, 1)
                dve.wait_ge(u1, at + 2)
                v.tensor_scalar(w2T16[:, HI], w2T32[:, :], WSCALE, None, ALU.mult).then_inc(u1, 1)
                v.tensor_tensor_reduce(out=tw, in0=w2T32[:, :], in1=b2b[:, :], scale=1.0, scalar=0.0, op0=ALU.mult,
                                       op1=ALU.add, accum_out=cc[:, :]).then_inc(u1, 1)
                dve.wait_ge(u1, at + 4)
                v.scalar_tensor_tensor(out=w2T16[:, LO], in0=w2T32[:, :], scalar=WSCALE, in1=w2T16[:, HI],
                                       op0=ALU.mult, op1=ALU.subtract).then_inc(u1, 1)
                for k, (f32, f16, scale) in enumerate(((A32, A16, 1.0), (Aq32, Aq16, WSCALE))):
                    r = m[2 + k]
                    dve.wait_ge(r.full, r.before + 1)
                    v.scalar_tensor_tensor(out=flat(f32[:, :, :]), in0=psM[:, r.slot, :], scalar=-ETA,
                                           in1=flat(f32[:, :, :]), op0=ALU.mult, op1=ALU.add).then_inc(r.done, 1)
                    dve.wait_ge(r.done, r.before + 1)
                    v.tensor_scalar(f16[:, HI], f32[:, :, :], scale, None, ALU.mult).then_inc(u1, 1)
                    dve.wait_ge(u1, at + 7 + 2 * k)
                    v.scalar_tensor_tensor(out=f16[:, LO], in0=f32[:, :, :], scalar=scale, in1=f16[:, HI],
                                           op0=ALU.mult, op1=ALU.subtract).then_inc(u1, 1)

            def new_hidden(ph, b, g):
                u = use(ph, ("A3P", g), "M", 0)
                dve.wait_ge(u.done, u.before + 1)
                split_stage(use(ph, ("A3P", g), "S", 0), h2[:, HI, :], h2[:, LO, :])

            def add_mlp(name, first_tile):
                def unit(ph, b, g):
                    if ph is first and first_tile == 0:
                        dve.wait_ge(tern_step, 4)
                    for k in range(2):
                        tile = g * T4 + first_tile + k
                        u = use(ph, (name, g), "O", k)
                        dve.wait_ge(u.full, u.before + 1)
                        dve.wait_ge(xa_done, TILES * b + tile + 1)
                        if ph is not first:
                            dve.wait_ge(out_stored[tile], 16 * (b + g))
                        v.scalar_tensor_tensor(out=x1[:, tile, :], in0=psO[:, u.slot, :], scalar=1.0 / WSCALE,
                                               in1=xin[:, tile, :], op0=ALU.mult, op1=ALU.add).then_inc(u.done, 1)
                return unit

            def queries(ph, c_, g):
                for m in range(C):
                    u = use(ph, ("Q", g), "M", m)
                    dve.wait_ge(u.done, u.before + 1)
                    split_stage(use(ph, ("Q", g), "S", m), qs[:, HI, m, :], qs[:, LO, m, :])

            def guard(ph, c_, g):
                for k in range(2 * T4):
                    u = use(ph, ("GUARD", g), "O", k)
                    dve.wait_ge(u.full, u.before + 1)
                    v.tensor_reduce(gm[:, k // 2, (k % 2) * 8:(k % 2) * 8 + 8],
                                    psO[:, u.slot, :].rearrange("p (h k) -> p h k", k=KEYS), AX.X,
                                    ALU.max).then_inc(u.done, 1)

            def exponentials(ph, c_, g):
                for q in range(PAIRS):
                    u = use(ph, ("ST", g), "M", q)
                    dve.wait_ge(u.done, u.before + 1)
                    split_stage(use(ph, ("ST", g), "S", q), es[:, HI, q, :], es[:, LO, q, :])

            def normalize(ph, c_, g):
                for k in range(2 * T4):
                    u = use(ph, ("PV", g), "O", k)
                    i = k % 2
                    dve.wait_ge(u.full, u.before + 1)
                    heads = psO[:, u.slot, 0:8 * (W + 1)].rearrange("p (h w) -> p h w", w=W + 1)
                    v.reciprocal(rden[:, i, :], heads[:, :, W]).then_inc(rd, 1)
                    dve.wait_ge(rd, 16 * c_ + 8 * g + k + 1)
                    if k >= 2:
                        dve.wait_ge(o_done, 16 * c_ + 8 * g + k - 1)
                    v.tensor_tensor(obuf[:, i, :, :], heads[:, :, 0:W],
                                    rden[:, i, :].rearrange("p (h a) -> p h a", a=1).broadcast_to([P, 8, W]),
                                    ALU.mult).then_inc(u.done, 1)

            def ffn_hidden(name, first_chunk):
                def unit(ph, c_, g):
                    for k in range(4):
                        u = use(ph, (name, g), "M", k)
                        f = (first_chunk + k) % (FCH // 2)
                        dve.wait_ge(u.done, u.before + 1)
                        split_stage(use(ph, (name, g), "S", k), hF[:, f, HI, :], hF[:, f, LO, :])
                return unit

            def add_ffn(name, half, first_tile):
                def unit(ph, c_, g):
                    for k in range(2):
                        tile = g * T4 + first_tile + k
                        u = use(ph, (name, g), "O", k)
                        dve.wait_ge(u.full, u.before + 1)
                        if half == 0:
                            dve.wait_ge(xf_done, TILES * c_ + tile + 1)
                        else:
                            before = use(ph, ("F2a" if first_tile == 0 else "F2b", g), "O", k)
                            dve.wait_ge(before.done, before.before + 1)
                        v.tensor_tensor(x1[:, tile, :], psO[:, u.slot, :], x1[:, tile, :], ALU.add).then_inc(u.done, 1)
                return unit

            run(dve, {
                "D": d_and_masks, "TQT": weight_lo("TQT", tqT), "AINIT": a_init, "W2T0": w2_init, "U3": new_pg,
                "WQT": weight_lo("WQT", wqT), "KCTX": keys, "VCTX": values, "MEAN": threshold,
                "TERa": ternary("TERa", 0), "TERb": ternary("TERb", 1),
                "L1a": moments(0, "L1a", xin), "L2a": moments(1, "L2a", x1), "L3a": moments(2, "L3a", x1),
                "L1b": normalized("L1b", lambda g, t, hl: xn1[:, hl, g * T4 + t, :]),
                "L2b": normalized("L2b", lambda g, t, hl: xnX[:, hl, t, :]),
                "L3b": normalized("L3b", lambda g, t, hl: xnX[:, hl, t, :]),
                "PRE": hidden, "PRG": gelu_and_slope, "DH": hidden_gradient, "S": sums, "U1": update,
                "A3P": new_hidden, "A3Oa": add_mlp("A3Oa", 0), "A3Ob": add_mlp("A3Ob", 2),
                "Q": queries, "GUARD": guard, "ST": exponentials, "PV": normalize,
                "F1a": ffn_hidden("F1a", 0), "F1b": ffn_hidden("F1b", 4), "F1c": ffn_hidden("F1c", 8),
                "F1d": ffn_hidden("F1d", 12),
                "F2a": add_ffn("F2a", 0, 0), "F2b": add_ffn("F2b", 0, 2), "F2c": add_ffn("F2c", 1, 0),
                "F2d": add_ffn("F2d", 1, 2),
            })


_INS = ["x", "ctx_1024", "mask_BxS2_ik0", "L0_attn_t_k", "L0_attn_t_v", "L0_attn_t_q", "L0_attn_W1", "L0_attn_b1",
        "L0_attn_W2", "L0_attn_b2", "L0_xattn_Wq", "L0_xattn_bq", "L0_xattn_Wk", "L0_xattn_bk", "L0_xattn_Wv",
        "L0_xattn_bv", "L0_ffn_W1", "L0_ffn_b1", "L0_ffn_W2", "L0_ffn_b2"]


def kernel(**inputs):
    import numpy as _np
    import concourse.bacc as _bacc
    from concourse import mybir as _mybir
    from concourse.bass_utils import run_bass_kernel_spmd as _run

    nc = _bacc.Bacc("TRN2", target_bir_lowering=False, num_devices=1)
    arrays, args = {}, []
    for name in _INS:
        a = _np.ascontiguousarray(inputs[name])
        arrays[f"in_{name}_dram"] = a
        args.append(nc.dram_tensor(f"in_{name}_dram", a.shape, _mybir.dt.from_np(a.dtype), kind="ExternalInput").ap())
    args.append(nc.dram_tensor("out_0_dram", (B, N, D), F32, kind="ExternalOutput").ap())
    build(nc, *args)
    r = _run(nc, [arrays], core_ids=[0])
    return r.results[0]["out_0_dram"]
```

```python
import math
from contextlib import ExitStack

import concourse.bass as bass
from concourse import mybir

F32, F16, BF16, F8, I32 = (mybir.dt.float32, mybir.dt.float16, mybir.dt.bfloat16, mybir.dt.float8e4, mybir.dt.int32)
ALU = mybir.AluOpType
ACT = mybir.ActivationFunctionType
AX = mybir.AxisListType

P = 128
B, N, D = 8, 1024, 512
HID = 128
HEADS, W, KEYS = 16, 32, 64
FF = 4 * D
C = D // P
G2, T4 = 2, 4
GT = T4 * P
TILES = G2 * T4
FCH = FF // P
PAIRS = HEADS // 2
WSCALE = 256.0
LR = 0.001
ETA = LR * 2.0 / (N * D)
EPS = 1e-5
MASKED = 10000.0
TINY = 1e-15
INV_SQRT_2PI = (2.0 * math.pi) ** -0.5
SQW = float(W) ** 0.5
HI, LO = 0, 1
PASSES = ((HI, HI), (HI, LO), (LO, HI))
NAT = 2 * HID + 2
HALF = FF * D // P // 2
HT_AT = TILES * 2 * NAT * 2
DPT_AT = HT_AT + 4096
GP_AT = DPT_AT + 4096
S3_AT = HT_AT + 2560
HF_AT = (GP_AT + C * NAT * 4 + 63) // 64 * 64
ARENA = HF_AT + FCH // 2 * 2 * GT * 2

RINGS = {"M": 4, "O": 2, "T": 2, "S": 3}
USES = {
    "D": {}, "K": {"M": 4}, "KQ": {"M": 4}, "DT": {"M": 4}, "TQT": {"M": 4}, "W1T": {"M": 1}, "AINIT": {"M": 2},
    "W2T0": {"M": 1}, "WQT": {"M": 4}, "WKT": {"M": 4}, "WVT": {"M": 4}, "CTXT": {"M": 4}, "KCTX": {"M": 4},
    "VCTX": {"M": 4}, "FW": {}, "ABS": {}, "MEAN": {"M": 1}, "TERa": {}, "TERb": {},
    "X0": {}, "X1": {}, "KV": {}, "T1": {}, "T2": {}, "T3": {},
    "L1a": {}, "L1b": {"S": 4}, "PRE": {"M": 1}, "PRG": {}, "DHp": {"M": 2}, "DHg": {},
    "S": {"M": 5}, "U1": {"M": 4}, "U2": {"M": 1}, "U3": {"M": 2}, "A3P": {"M": 1, "S": 1},
    "L2a": {}, "L2b": {"S": 4}, "GT": {"T": 1}, "L3a": {}, "L3b": {"S": 4},
}
for k in "ab":
    USES |= {"TT" + k: {"T": 4}, "Q" + k: {"M": 2, "S": 2},
             "GUARD" + k: {"O": 4}, "ST" + k: {"M": 4, "S": 4}, "PV" + k: {"O": 4}}
for k in "abcd":
    USES |= {"HT" + k: {"T": 2}, "A3O" + k: {"O": 1}, "F1" + k: {"M": 4, "S": 4}}
for k in "abcdefgh":
    USES |= {"F2" + k: {"O": 1}}


def schedule(text):
    return [(name, int(g or 0)) for name, _, g in (word.partition(".") for word in text.split())]


SETUP = schedule("D W1T AINIT L1a.0 W2T0 U3 L1b.0 T1.0 CTXT WKT WVT WQT DT L1a.1 L1b.1 T1.1")
FIRST = schedule("KCTX PRE.0 PRE.1 PRG VCTX DHp DHg HTa HTb HTc HTd S FW.0 K ABS.0 KQ MEAN.0 TERa.0 U1 TTa.0 "
                 "TQT U2 U3 A3P.0 TERb.0 A3Oa.0 A3Ob.0 TTb.0 FW.1 KV A3Oc.0 A3Od.0 L2a.0 A3P.1 L2b.0 T2.0 A3Oa.1 A3Ob.1 "
                 "ABS.1 A3Oc.1 A3Od.1 MEAN.1 TERa.1 Qa.0 Qb.0 TTa.1 GUARDa.0 GUARDb.0 GT.0 TERb.1 STa.0 STb.0 "
                 "TTb.1 PVa.0 PVb.0 L3a.0 L3b.0 T3.0")
BODY = schedule("X0 X1 L2a.1 F1a.0 L1a.0 F1b.0 L1b.0 T1.0 F2a.0 F2b.0 L2b.1 F2c.0 F2d.0 L1a.1 F1c.0 L1b.1 T1.1 F1d.0 "
                "T2.1 F2e.0 PRE.0 PRE.1 PRG DHp F2f.0 DHg Qa.1 F2g.0 Qb.1 HTa HTb GUARDa.1 HTc GUARDb.1 "
                "HTd GT.1 S STa.1 U1 STb.1 A3P.0 F2h.0 PVa.1 PVb.1 L3a.1 A3Oa.0 L3b.1 T3.1 KV A3Ob.0 U2 A3Oc.0 U3 A3Od.0 "
                "L2a.0 F1a.1 L2b.0 T2.0 F1b.1 F2a.1 F2b.1 F2c.1 Qa.0 Qb.0 F2d.1 GUARDa.0 GUARDb.0 F1c.1 GT.0 "
                "F1d.1 STa.0 STb.0 F2e.1 F2f.1 PVa.0 PVb.0 L3a.0 A3P.1 F2g.1 F2h.1 L3b.0 T3.0 A3Oa.1 A3Ob.1 A3Oc.1 A3Od.1")
LAST = schedule("L2a.1 F1a.0 L2b.1 F1b.0 T2.1 F2a.0 F2b.0 F2c.0 Qa.1 Qb.1 GUARDa.1 GUARDb.1 F2d.0 GT.1 F1c.0 "
                "STa.1 STb.1 F1d.0 PVa.1 F2e.0 PVb.1 L3a.1 L3b.1 T3.1 F2f.0 F2g.0 F2h.0 F1a.1 F1b.1 F2a.1 F2b.1 F2c.1 "
                "F2d.1 F1c.1 F1d.1 F2e.1 F2f.1 F2g.1 F2h.1")
BEHIND = {u for u in BODY if u[0][:2] in ("F1", "F2")}
BEHIND |= {u for u in BODY if u[1] == 1 and u[0].rstrip("ab") in ("L2", "T2", "Q", "GUARD", "GT", "ST",
                                                                "PV", "L3", "T3")}


class Use:

    def __init__(self, slot, before, full, done):
        self.slot, self.before, self.full, self.done = slot, before, full, done
        self.reused = not (isinstance(before, int) and before == 0)


class Phase:

    def __init__(self, order, base):
        self.order, self.base, self.place = order, base, {}
        self.total = {r: [0] * n for r, n in RINGS.items()}
        count = {r: 0 for r in RINGS}
        for unit in order:
            for ring, n in USES[unit[0]].items():
                for i in range(n):
                    slot = count[ring] % RINGS[ring]
                    self.place[unit, ring, i] = (slot, count[ring] if ring == "S" else self.total[ring][slot])
                    self.total[ring][slot] += 1
                    count[ring] += 1
        self.count = count
        self.turn = 0

    def start(self, ring, slot):
        if ring == "S":
            return self.turn * self.count["S"] + self.base["S"][0]
        return self.turn * self.total[ring][slot] + self.base[ring][slot]

    def after(self, turns):
        base = {r: [b + turns * t for b, t in zip(self.base[r], self.total[r])] for r in RINGS}
        base["S"] = [self.base["S"][0] + turns * self.count["S"]] * RINGS["S"]
        return base


def build(nc, x, ctx_in, mask, t_k, t_v, t_q, w1, b1, w2, b2, wq, bq, wk, bk, wv, bv, fw1, fb1, fw2, fb2, out):
    setup = Phase(SETUP, {r: [0] * n for r, n in RINGS.items()})
    first = Phase(FIRST, setup.after(1))
    body = Phase(BODY, first.after(1))
    last = Phase(LAST, body.after(B - 1))

    with ExitStack() as stack:
        def sb(name, shape, dt):
            return stack.enter_context(nc.sbuf_tensor(name, shape, dt))

        def sem(name):
            return stack.enter_context(nc.semaphore(name))

        k_scr = nc.dram_tensor("k_scr", (B, P, 2, C, KEYS), F16).ap()
        v_scr = nc.dram_tensor("v_scr", (B, KEYS, 2, D), F16).ap()
        mb_scr = nc.dram_tensor("mb_scr", (B, P, 1), F32).ap()
        mr_scr = nc.dram_tensor("mr_scr", (B, 1, KEYS), F16).ap()
        dn_scr = nc.dram_tensor("dn_scr", (P, C, D), F32).ap()
        dt_scr = nc.dram_tensor("dt_scr", (P, C, D), F32).ap()

        psT = stack.enter_context(nc.psum_tensor("psT", [P, 2, 1024], F16))
        psM = stack.enter_context(nc.psum_tensor("psM", [P, 4, 512], F32))
        psO = stack.enter_context(nc.psum_tensor("psO", [P, 2, 512], F32))

        id16, idbf, id32 = sb("id16", [P, P], F16), sb("idbf", [P, P], BF16), sb("id32", [P, P], F32)
        ones_row = sb("ones_row", [1, P], F16)
        neg_ind = sb("neg_ind", [HEADS, PAIRS * P], BF16)
        ones_col = sb("ones_col", [P, 1], F32)
        neghalf, minus1, eps = (sb(n, [P, T4], F32) for n in ("neghalf", "minus1", "eps"))
        fw1T = sb("fw1T", [P, C, FF], F8)
        fw2T = sb("fw2T", [P, FCH, D], F8)
        tqT = sb("tqT", [P, 2, C, D], F16)
        wqT = sb("wqT", [P, 2, C, D], F16)
        kk = sb("kk", [P, C, D], F32)
        kq = sb("kq", [P, C, D], F32)
        dd = sb("dd", [P, C, D], F32)
        b1c = sb("b1c", [P, 1], F32)
        cc = sb("cc", [P, 1], F32)
        bqc, bkc, fb1c = sb("bqc", [P, C], F32), sb("bkc", [P, C], F32), sb("fb1c", [P, FCH], F32)
        b2b, fb2b = sb("b2b", [P, D], F32), sb("fb2b", [P, D], F32)

        A32, Aq32 = sb("A32", [P, C, HID], F32), sb("Aq32", [P, C, HID], F32)
        A16, Aq16 = sb("A16", [P, 2, C, HID], F16), sb("Aq16", [P, 2, C, HID], F16)
        P16, G16 = sb("P16", [P, 2, C, HID], F16), sb("G16", [P, 2, HID], F16)
        w2T32, w2T16 = sb("w2T32", [P, D], F32), sb("w2T16", [P, 2, D], F16)

        kbd = sb("kbd", [P, 2, C, 4 * KEYS], F16)
        vbd = sb("vbd", [P, 2, PAIRS, 2 * (W + 1)], F16)
        mbc = sb("mbc", [P, 1], F32)
        mrow = sb("mrow", [1, KEYS], F16)

        xin = sb("xin", [P, TILES, D], F32)
        x1 = sb("x1", [P, TILES, D], F32)
        xn1 = sb("xn1", [P, 2, TILES, D], F16)
        xT1 = sb("xT1", [P, 2 * C, N], F16)
        xnX = sb("xnX", [P, 2, T4, D], F16)
        xTF = sb("xTF", [P, 2 * C, GT], F16)
        arena = sb("arena", [P, ARENA // 2], F16)
        stage = sb("stage", [P, RINGS["S"], 512], F32)
        rden = sb("rden", [P, 2, 8], F32)
        gm = sb("gm", [P, T4, HEADS], BF16)
        st = sb("st", [P, 3, T4, 6], F32)
        mv = sb("mv", [P, 3, T4, 2], F32)
        ve = sb("ve", [P, 3, T4], F32)
        rs = sb("rs", [P, 3, G2, T4], F32)
        nm = sb("nm", [P, 3, G2, T4], F32)
        mci = sb("mci", [P, B], I32)
        mx = sb("mx", [P, B], F32)
        mcf = sb("mcf", [P, B], F32)
        asum = sb("asum", [P, 2, 2], F32)
        thr = sb("thr", [P, 2, 3], F32)

        def part(buf, start, shape, dt, rows=P):
            size = 1
            for s in shape:
                size *= s
            nbytes = size * (4 if dt in (F32, I32) else 2)
            v = buf[0:rows, start // 2:(start + nbytes) // 2]
            if dt != F16:
                v = v.bitcast(dt)
            if len(shape) == 2:
                v = v.rearrange("p (a c) -> p a c", a=shape[0])
            if len(shape) == 3:
                v = v.rearrange("p (a e c) -> p a e c", a=shape[0], e=shape[1])
            return v

        xn1f = xn1[:, :, :, :].rearrange("p a t d -> p (a t d)")
        xnXf = xnX[:, :, :, :].rearrange("p a t d -> p (a t d)")
        xTFf = xTF[:, :, :].rearrange("p a d -> p (a d)")
        x1f = x1[:, :, :].rearrange("p a d -> p (a d)")
        fw1f = fw1T[:, :, :].rearrange("p a d -> p (a d)").bitcast(F32)
        fw2f = fw2T[:, :, :].rearrange("p a d -> p (a d)").bitcast(F32)

        un, ee = part(arena, 0, [G2, GT], F32), part(arena, 4096, [G2, GT], F32)
        nat = part(arena, 0, [TILES, 2, NAT], F16)
        hT, dpT = part(arena, HT_AT, [G2, 2, GT], F16), part(arena, DPT_AT, [G2, 2, GT], F16)
        sxb, s4b = part(arena, HT_AT, [C, P], F32), part(arena, HT_AT + 2048, [P], F32)
        tb, tw = part(arena, DPT_AT, [D], F32), part(arena, DPT_AT + 2048, [D], F32)
        gp = part(arena, GP_AT, [G2, GT], F32)
        ru = part(arena, DPT_AT, [G2, GT], F32)
        s12 = part(arena, GP_AT, [C, NAT], F32)
        w2n = part(arena, HT_AT, [C, HID], F32)
        h2 = part(arena, GP_AT, [2, GT], F16)
        s3 = part(arena, S3_AT, [132], F32)
        xTQ0, qs0 = part(arena, 0, [2 * C, GT], F16), part(arena, 8192, [2, C, GT], F16)
        gT0 = part(arena, 0, [GT], BF16, rows=HEADS)
        xTQ, qs = [xTQ0, xTF], [qs0, part(xnXf, 0, [2, C, GT], F16)]
        gT = [gT0, part(xTFf, 0, [GT], BF16, rows=HEADS)]
        obuf = part(arena, GP_AT + 2048, [2, 8, W], F32)
        es = part(xn1f, 0, [2, PAIRS, GT], F16)

        def at_side(places, ph, g):
            return places[0 if ph is last else g]

        hF = part(arena, HF_AT, [FCH // 2, 2, GT], F16)

        tk, tq = part(x1f.bitcast(F16), 0, [C, D], F32), part(x1f.bitcast(F16), 8192, [C, D], F32)
        dn = kk[:, :, :]
        w1s, w1T = kq[:, 0, :], kq[:, 1, :].rearrange("p (c h) -> p c h", c=C)
        bvb, v32 = kq[:, 2, :], kq[:, 3, :]
        wqs, wks = part(arena, 0, [C, D], F32), part(arena, 8192, [C, D], F32)
        wvs, ctxs = part(arena, 16384, [C, D], F32), part(arena, 24576, [C, D], F32)
        wkT, wvT = (f.rearrange("p (c d) -> p c d", c=C) for f in (fw1f, fw2f))
        ctxT = part(xTFf, 0, [C, D], F32)
        w2s = part(xnXf, 0, [C, HID], F32)
        cjunk = part(xn1f, 14336, [D], F32)
        mr16 = part(xnXf, 2048, [B, KEYS], F16, rows=1)
        mi, mf = part(xnXf, 4096, [B * KEYS], I32), part(xnXf, 6144, [B * KEYS], F32)
        kTs = part(xnXf, 0, [2, C, D], F16)
        vs = part(arena, 24576, [C, 2, D], F16)
        ffs = [part(arena, HF_AT, [HALF], F32), part(xn1f, 0, [HALF], F32)]
        tern = part(xTFf, 0, [HALF], F16)

        full = {r: [sem(f"{r}{i}_filled") for i in range(n)] for r, n in RINGS.items() if r != "S"}
        done = {r: [sem(f"{r}{i}_emptied") for i in range(n)] for r, n in RINGS.items() if r != "S"}
        staged = sem("xhat_staged")
        hi_done = sem("hi_done")
        split = sem("split_done")
        consts, idents = sem("consts"), sem("idents")
        ld = {n: sem(f"load_{n}") for n in ("tk", "tq", "tv", "w1", "w2", "small", "wq", "wk", "wv", "ctx",
                                            "mask", "fw1_0", "fw1_1", "fw2_0", "fw2_1")}
        x_loaded = [sem(f"x_loaded{g}") for g in range(G2)]
        scr_stored, mr_stored = sem("scratch_stored"), sem("mask_rows_stored")
        ctx_loaded = sem("ctx_loaded")
        dd_loaded = sem("dd_loaded")
        xt1_loaded, xt2_loaded, xt3_loaded = ([sem(f"xT{k}_loaded{g}") for g in range(G2)] for k in (1, 2, 3))
        out_stored = [sem(f"out_stored{t}") for t in range(TILES)]
        d_ready = sem("d_ready")
        wt_hi = sem("weight_hi")
        init = sem("state_init")
        kv_hi = sem("kv_hi")
        v_split = sem("v_split")
        mask_step = sem("mask_step")
        abs_done, thr_step, tern_step = sem("abs_done"), sem("thr_step"), sem("tern_step")
        bn = [sem(f"ln{k}_bn") for k in (1, 2, 3)]
        stats = [sem(f"ln{k}_stats") for k in (1, 2, 3)]
        lnp = [sem(f"ln{k}_steps") for k in (1, 2, 3)]
        u_step = sem("u_step")
        e_step = sem("exp_step")
        h_ready = sem("h_ready")
        h_hi, h_split = sem("h_hi"), sem("h_split")
        ru_step = sem("h_over_u_step")
        gp_step = sem("gp_step")
        gp_ready, dp_hi, dp_split = sem("gp_ready"), sem("dp_hi"), sem("dp_split")
        ones_set = sem("ones_set")
        bc_ready = sem("sums_broadcast")
        u1 = sem("update_step")
        u3 = sem("pg_hi")
        xa_done = sem("x_plus_b2")
        o_done = sem("attn_added")
        xf_done = sem("x_plus_fb2")
        rd = sem("denominators")
        passed = sem("passed")
        TR_STEPS = 16 * T4 * 2
        U1_STEPS, LN_STEPS, CONSTS = 10, 4, 12
        STORED = 16 * (3 + 2 * B)

        def use(ph, unit, ring, i):
            slot, nth = ph.place[unit, ring, i]
            before = ph.start(ring, slot) + nth
            if ring == "S":
                return Use(slot, before, None, split)
            return Use(slot, before, full[ring][slot], done[ring][slot])

        def held(eng, waits):
            for sm, n in waits:
                eng.wait_ge(sm, n)
            eng.sem_inc(passed, 1)

        def run(eng, unit_programs):
            for ph, b in ((setup, 0), (first, 0)):
                for name, g in ph.order:
                    if name in unit_programs:
                        unit_programs[name](ph, b, g)
            with eng.Fori(1, B) as b:
                body.turn = b - 1
                for unit in BODY:
                    if unit[0] in unit_programs:
                        unit_programs[unit[0]](body, b - 1 if unit in BEHIND else b, unit[1])
            for name, g in LAST:
                if name in unit_programs:
                    unit_programs[name](last, B - 1, g)

        block = stack.enter_context(nc.Block())

        @block.sync
        def _(sp):
            rows = "(j p) d -> p j d"
            def load_x(b, g):
                sp.dma_start(xin[:, g * T4:(g + 1) * T4, :],
                             x[b, g * GT:(g + 1) * GT, :].rearrange("(t p) d -> p t d", p=P)).then_inc(x_loaded[g], 16)

            sp.dma_start(w1s, w1).then_inc(ld["w1"], 16)
            sp.dma_start(tk, t_k.rearrange(rows, p=P)).then_inc(ld["tk"], 16)
            load_x(0, 0)
            sp.dma_start(dn, t_v.rearrange(rows, p=P)).then_inc(ld["tv"], 16)
            sp.dma_start(tq, t_q.rearrange(rows, p=P)).then_inc(ld["tq"], 16)
            sp.dma_start(w2s, w2.rearrange("(j p) h -> p j h", p=P)).then_inc(ld["w2"], 16)
            small = [(b1c[:, :], b1.rearrange("(p a) -> p a", a=1)), (b2b[:, :], b2.partition_broadcast(P)),
                     (fb2b[:, :], fb2.partition_broadcast(P)), (bvb, bv.partition_broadcast(P)),
                     (bqc[:, :], bq.rearrange("(m p) -> p m", p=P)), (bkc[:, :], bk.rearrange("(m p) -> p m", p=P)),
                     (fb1c[:, :], fb1.rearrange("(m p) -> p m", p=P))]
            for dst, src in small:
                sp.dma_start(dst, src, allow_slow_non_contiguous=True).then_inc(ld["small"], 16)
            sp.dma_start(ctxs, ctx_in.rearrange("b k d -> (b k) d").rearrange(rows, p=P)).then_inc(ld["ctx"], 16)
            sp.dma_start(wks, wk.rearrange(rows, p=P)).then_inc(ld["wk"], 16)
            load_x(0, 1)
            sp.dma_start(wvs, wv.rearrange(rows, p=P)).then_inc(ld["wv"], 16)
            sp.dma_start(wqs, wq.rearrange(rows, p=P)).then_inc(ld["wq"], 16)
            sp.dma_start(mi, mask.rearrange("b k -> (b k)").partition_broadcast(P)).then_inc(ld["mask"], 16)
            for j in range(2):
                sp.dma_start(mci[j * KEYS:(j + 1) * KEYS, :], mask.rearrange("b k -> k b"),
                             allow_slow_non_contiguous=True).then_inc(ld["mask"], 16)
            def store_d(ph, b, g):
                sp.wait_ge(d_ready, 1)
                sp.dma_start(dn_scr, dn).then_inc(scr_stored, 16)
                sp.wait_ge(mask_step, 7)
                sp.dma_start(mb_scr.rearrange("b p a -> p (b a)"), mcf[:, :],
                             allow_slow_non_contiguous=True).then_inc(scr_stored, 16)
                sp.dma_start(mr_scr.rearrange("b a k -> a b k"), mr16[:, :, :]).then_inc(mr_stored, 16)
                for c in range(C):
                    u = use(ph, ("DT", 0), "M", c)
                    sp.wait_ge(u.done, u.before + 1)
                sp.dma_start(dt_scr, dd[:, :, :]).then_inc(scr_stored, 16)

            def store_keys(ph, b, g):
                for m in range(C):
                    u = use(ph, ("KCTX", 0), "M", m)
                    sp.wait_ge(u.done, u.before + 1)
                for k in range(B):
                    sp.dma_start(k_scr[k], kTs[:, :, :, k * KEYS:(k + 1) * KEYS]).then_inc(scr_stored, 16)

            def store_values(ph, b, g):
                sp.wait_ge(v_split, C)
                for k in range(B):
                    half = (k % 2) * KEYS
                    sp.dma_start(v_scr[k], vs[half:half + KEYS, k // 2, :, :]).then_inc(scr_stored, 16)

            def transposes(ln, sems, src, dst):
                def unit(ph, b, g):
                    if ln == "L1b" and ph is body and g == 0:
                        for s in range(2):
                            held(sp, [(done["O"][s], ph.start("O", s))])
                    if ln == "L2b" and ph is body and g == 1:
                        u = use(ph, ("F1d", 0), "M", 3)
                        held(sp, [(u.full, u.before + 1)])
                    for t in range(T4):
                        s = use(ph, (ln, g), "S", t)
                        held(sp, [(split, s.before + 1)])
                        for hl in range(2):
                            sp.dma_start_transpose(out=dst(ph, g)[:, hl * C:(hl + 1) * C, t * P:(t + 1) * P],
                                                   in_=src(g, t, hl)).then_inc(sems[g], 16)
                return unit

            def load_keys(ph, b, g):
                if ph is first:
                    sp.wait_ge(scr_stored, STORED)
                    sp.wait_ge(mr_stored, 16)
                    sp.wait_ge(consts, CONSTS)
                else:
                    u = use(ph, ("STb", 1), "M", 3)
                    r = use(ph, ("PVb", 1), "O", 3)
                    held(sp, [(u.done, u.before + 1)])
                    held(sp, [(r.full, r.before + 1)])
                for hh in range(4):
                    sp.dma_start(kbd[hh * W:(hh + 1) * W, :, :, hh * KEYS:(hh + 1) * KEYS],
                                 k_scr[b, hh * W:(hh + 1) * W, :, :, :]).then_inc(ctx_loaded, 16)
                for j in range(2):
                    for hl in range(2):
                        src = v_scr[b, :, hl, :].rearrange("k (q e w) -> k q e w", e=2, w=W)[:, :, j, :]
                        sp.dma_start(vbd[j * KEYS:(j + 1) * KEYS, hl, :, j * (W + 1):j * (W + 1) + W],
                                     src).then_inc(ctx_loaded, 16)
                sp.dma_start(mbc[:, :], mb_scr[b]).then_inc(ctx_loaded, 16)
                sp.dma_start(mrow[:, :], mr_scr[b]).then_inc(ctx_loaded, 16)

            def load_ffn(ph, b, g):
                w = (fw1 if g == 0 else fw2).rearrange("(m p) d -> p m d", p=P)
                m, d = (FCH, D) if g == 0 else (C, FF)
                if g == 0:
                    sp.wait_ge(scr_stored, STORED)
                for half in range(2):
                    if g == 1:
                        sp.wait_ge(tern_step, 4)
                    elif half == 1:
                        u = use(ph, ("S", 0), "M", C)
                        sp.wait_ge(u.full, u.before + 1)
                    sp.dma_start(ffs[half ^ g].rearrange("p (m d) -> p m d", d=d),
                                 w[:, half * m // 2:(half + 1) * m // 2, :]).then_inc(ld[f"fw{g + 1}_{half}"], 16)

            def load_group(g):
                def unit(ph, b, _):
                    if g == 0:
                        for s in range(2):
                            sp.wait_ge(done["O"][s], ph.start("O", s))
                    load_x(b, g)
                return unit

            def load_d(ph, b, g):
                u = use(ph, ("U1", 0), "M", 1)
                sp.wait_ge(u.full, u.before + 1)
                sp.dma_start(dd[:, :, :], dn_scr).then_inc(dd_loaded, 16)

            def load_dt(ph, b, g):
                if ph is not setup:
                    u = use(ph, ("U3", 0), "M", 0)
                    sp.wait_ge(u.full, u.before + 1)
                    sp.dma_start(dd[:, :, :], dt_scr).then_inc(dd_loaded, 16)

            def store_out(name, t):
                def unit(ph, c, g):
                    u = use(ph, (name, g), "O", 0)
                    sp.wait_ge(u.done, u.before + 1)
                    sp.dma_start(out[c, g * GT + t * P:g * GT + (t + 1) * P, :],
                                 x1[:, g * T4 + t, :]).then_inc(out_stored[g * T4 + t], 16)
                return unit

            run(sp, {"DT": store_d, "KCTX": store_keys, "VCTX": store_values, "KV": load_keys,
                     "T1": transposes("L1b", xt1_loaded, lambda g, t, hl: xn1[:, hl, g * T4 + t, :],
                                      lambda ph, g: xT1[:, :, g * GT:(g + 1) * GT]),
                     "T2": transposes("L2b", xt2_loaded, lambda g, t, hl: xnX[:, hl, t, :],
                                      lambda ph, g: at_side(xTQ, ph, g)),
                     "T3": transposes("L3b", xt3_loaded, lambda g, t, hl: xnX[:, hl, t, :], lambda ph, g: xTF),
                     "FW": load_ffn, "X0": load_group(0), "X1": load_group(1), "U1": load_d,
                     "U3": load_dt, **{"F2" + k: store_out("F2" + k, t) for t, k in enumerate("efgh")}})
            for t in range(TILES):
                sp.wait_ge(out_stored[t], 16 * B)

        @block.tensor
        def _(pe):
            mm = nc.tensor.matmul

            def acquire(u):
                if u.reused:
                    pe.wait_ge(u.done, u.before)

            def transposed(name, src, ready, ident=None):
                def unit(ph, b, g):
                    pe.wait_ge(idents, 6)
                    pe.wait_ge(*ready)
                    for c in range(C):
                        u = use(ph, (name, 0), "M", c)
                        acquire(u)
                        for j in range(C):
                            i = nc.tensor.transpose(psM[:, u.slot, j * P:(j + 1) * P],
                                                    src[:, j, c * P:(c + 1) * P], id32[:, :])
                        i.then_inc(u.full, 1)
                return unit

            def gram(name, right, ready):
                def unit(ph, b, g):
                    pe.wait_ge(ld["tk"], 16)
                    pe.wait_ge(*ready)
                    for c in range(C):
                        u = use(ph, (name, 0), "M", c)
                        acquire(u)
                        for j in range(C):
                            i = mm(psM[:, u.slot, :], tk[:, j, c * P:(c + 1) * P], right[:, j, :],
                                   start=(j == 0), stop=(j == C - 1))
                        i.then_inc(u.full, 1)
                return unit

            def w1_transposed(ph, b, g):
                pe.wait_ge(idents, 6)
                pe.wait_ge(ld["w1"], 16)
                u = use(ph, ("W1T", 0), "M", 0)
                acquire(u)
                for j in range(C):
                    i = nc.tensor.transpose(psM[:, u.slot, j * P:(j + 1) * P], w1s[:, j * P:(j + 1) * P], id32[:, :])
                i.then_inc(u.full, 1)

            def chunked(u, left, right, parts):
                acquire(u)
                for c in range(C):
                    for j in range(parts):
                        i = mm(psM[:, u.slot, c * P:(c + 1) * P], left[:, j, c * P:(c + 1) * P], right(j),
                               start=(c == 0 and j == 0), stop=(j == parts - 1), skip_group_check=True)
                i.then_inc(u.full, 1)

            def a_init(ph, b, g):
                u = use(ph, ("W1T", 0), "M", 0)
                pe.wait_ge(u.done, u.before + 1)
                pe.wait_ge(ld["tk"], 16)
                chunked(use(ph, ("AINIT", 0), "M", 0), tk, lambda j: w1T[:, j, :], C)
                pe.wait_ge(ld["tq"], 16)
                chunked(use(ph, ("AINIT", 0), "M", 1), tq, lambda j: w1T[:, j, :], C)

            def w2_transposed(ph, b, g):
                pe.wait_ge(idents, 6)
                pe.wait_ge(ld["w2"], 16)
                u = use(ph, ("W2T0", 0), "M", 0)
                acquire(u)
                for j in range(C):
                    i = nc.tensor.transpose(psM[:, u.slot, j * P:(j + 1) * P], w2s[:, j, :], id32[:, :])
                i.then_inc(u.full, 1)

            def keys(ph, b, g):
                for n in ("CTXT", "WKT"):
                    for c in range(C):
                        u = use(setup, (n, 0), "M", c)
                        pe.wait_ge(u.done, u.before + 1)
                for m in range(C):
                    u = use(ph, ("KCTX", 0), "M", m)
                    acquire(u)
                    for c in range(C):
                        i = mm(psM[:, u.slot, :], wkT[:, c, m * P:(m + 1) * P], ctxT[:, c, :],
                               start=(c == 0), stop=(c == C - 1))
                    i.then_inc(u.full, 1)

            def values(ph, b, g):
                for c in range(C):
                    u = use(setup, ("WVT", 0), "M", c)
                    pe.wait_ge(u.done, u.before + 1)
                for r in range(C):
                    u = use(ph, ("VCTX", 0), "M", r)
                    acquire(u)
                    for c in range(C):
                        i = mm(psM[:, u.slot, :], ctxT[:, c, r * P:(r + 1) * P], wvT[:, c, :],
                               start=(c == 0), stop=(c == C - 1))
                    i.then_inc(u.full, 1)

            def mean(ph, b, g):
                u = use(ph, ("MEAN", g), "M", 0)
                acquire(u)
                pe.wait_ge(consts, CONSTS)
                pe.wait_ge(abs_done, 2 * g + 2)
                mm(psM[:, u.slot, 0:1], ones_col[:, :].broadcast_to([P, P]), asum[:, g, 0:1], start=True, stop=False)
                mm(psM[:, u.slot, 0:1], ones_col[:, :].broadcast_to([P, P]), asum[:, g, 1:2], start=False, stop=True).then_inc(u.full, 1)

            def ternary(name, half):
                def unit(ph, b, g):
                    pe.wait_ge(tern_step, 4 * g + 2 * half + 2)
                    for k in range(4):
                        u = use(ph, (name, g), "T", k)
                        acquire(u)
                        for j in range(8):
                            if g == 0:
                                dc, fc = j // 2, 2 * k + j % 2
                                src = tern[:, fc * D + dc * P:fc * D + (dc + 1) * P]
                            else:
                                fc, dc = 4 * k + j // 2, j % 2
                                src = tern[:, dc * FF + fc * P:dc * FF + (fc + 1) * P]
                            i = nc.tensor.transpose(psT[:, u.slot, j * P:(j + 1) * P], src, id16[:, :])
                        i.then_inc(u.full, 1)
                return unit

            def triple(dst, lhs, rhs, chunks, opened=False, closes=True):
                n = 0
                for c in range(chunks):
                    for l, r in PASSES:
                        n += 1
                        i = mm(dst, lhs(l, c), rhs(r, c), start=(n == 1 and not opened),
                               stop=(closes and n == 3 * chunks))
                return i

            def pre(ph, b, g):
                if ph is first:
                    pe.wait_ge(init, 7)
                else:
                    pe.wait_ge(u1, b * U1_STEPS)
                pe.wait_ge(xt1_loaded[g], TR_STEPS * (b + 1))
                u = use(ph, ("PRE", g), "M", 0)
                acquire(u)
                triple(psM[:, u.slot, :], lambda l, c: A16[:, l, c, :],
                       lambda r, c: xT1[:, r * C + c, g * GT:(g + 1) * GT], C).then_inc(u.full, 1)

            def residual(ph, b, g):
                if ph is body:
                    for s in range(4):
                        pe.wait_ge(done["M"][s], ph.start("M", s))
                for k in range(G2):
                    u = use(ph, ("DHp", 0), "M", k)
                    acquire(u)
                    triple(psM[:, u.slot, :], lambda l, c: P16[:, l, c, :],
                           lambda r, c: xT1[:, r * C + c, k * GT:(k + 1) * GT], C, closes=False)

            def residual_h(ph, b, g):
                for k in range(G2):
                    u = use(ph, ("DHp", 0), "M", k)
                    pe.wait_ge(h_split, 2 * b + k + 1)
                    triple(psM[:, u.slot, :], lambda l, c: G16[:, l, :], lambda r, c: hT[:, k, r, :], 1,
                           opened=True).then_inc(u.full, 1)

            def h_transposes(name, first_tile):
                def unit(ph, b, g):
                    for i in range(2):
                        t = first_tile + i
                        if t % T4 == 0:
                            pe.wait_ge(dp_split, 2 * b + t // T4 + 1)
                        u = use(ph, (name, 0), "T", i)
                        acquire(u)
                        for k, (src, hl) in enumerate(((dpT, HI), (hT, HI), (dpT, LO), (hT, LO))):
                            i = nc.tensor.transpose(psT[:, u.slot, k * P:(k + 1) * P],
                                                    src[:, t // T4, hl, t % T4 * P:(t % T4 + 1) * P], id16[:, :])
                        i.then_inc(u.full, 1)
                return unit

            def sums(ph, b, g):
                pe.wait_ge(ones_set, b + 1)
                u = use(ph, ("S", 0), "M", 0)
                acquire(u)
                for t in range(TILES):
                    r = use(ph, ("HT" + "abcd"[t // 2], 0), "T", t % 2)
                    pe.wait_ge(r.done, r.before + 1)
                    h_hi, h_lo = nat[:, t, HI, HID:2 * HID], nat[:, t, LO, HID:2 * HID]
                    h_one = nat[:, t, HI, HID:2 * HID + 1]
                    mm(psM[:, u.slot, 0:HID + 1], h_hi, h_one, start=(t == 0), stop=False, skip_group_check=True)
                    mm(psM[:, u.slot, 0:HID + 1], h_lo, h_one, start=False, stop=False, skip_group_check=True)
                    mm(psM[:, u.slot, 0:HID], h_hi, h_lo, start=False, stop=False, skip_group_check=True)
                for t in range(TILES):
                    for hl in range(2):
                        i = mm(psM[:, u.slot, HID + 2:HID + 3], nat[:, t, hl, 0:HID],
                               nat[:, t, HI, 2 * HID:2 * HID + 1], start=False,
                               stop=(t == TILES - 1 and hl == 1), skip_group_check=True)
                i.then_inc(u.full, 1)
                for c in range(C):
                    u = use(ph, ("S", 0), "M", 1 + c)
                    acquire(u)
                    for t in range(TILES):
                        x_hi, x_lo = (xn1[:, hl, t, c * P:(c + 1) * P] for hl in range(2))
                        mm(psM[:, u.slot, 0:2 * HID + 1], x_hi, nat[:, t, HI, 0:2 * HID + 1], start=(t == 0),
                           stop=False, skip_group_check=True)
                        mm(psM[:, u.slot, 0:2 * HID], x_hi, nat[:, t, LO, 0:2 * HID], start=False, stop=False,
                           skip_group_check=True)
                        i = mm(psM[:, u.slot, 0:2 * HID + 1], x_lo, nat[:, t, HI, 0:2 * HID + 1], start=False,
                               stop=(t == TILES - 1), skip_group_check=True)
                    i.then_inc(u.full, 1)

            def update(ph, b, g):
                if ph is not first:
                    pe.wait_ge(dd_loaded, 32 * b)
                u = use(ph, ("U1", 0), "M", 0)
                acquire(u)
                r = use(ph, ("S", 0), "M", 0)
                if r.slot != u.slot:
                    pe.wait_ge(r.done, r.before + 1)
                for c in range(C):
                    r = use(ph, ("S", 0), "M", 1 + c)
                    if r.slot != u.slot:
                        pe.wait_ge(r.done, r.before + 1)
                    mm(psM[:, u.slot, :], s12[:, c, HID:2 * HID], dd[:, c, :], start=(c == 0), stop=False)
                mm(psM[:, u.slot, :], s3[:, 0:HID], w2T32[:, :], start=False, stop=True).then_inc(u.full, 1)
                pe.wait_ge(bc_ready, 2 * b + 2)
                u = use(ph, ("U1", 0), "M", 1)
                acquire(u)
                for c in range(C):
                    mm(psM[:, u.slot, :], sxb[:, c, :], dd[:, c, :], start=(c == 0), stop=False)
                mm(psM[:, u.slot, :], s4b, w2T32[:, :], start=False, stop=True).then_inc(u.full, 1)
                chunked(use(ph, ("U1", 0), "M", 2), kk, lambda j: s12[:, j, 0:HID], C)
                chunked(use(ph, ("U1", 0), "M", 3), kq, lambda j: s12[:, j, 0:HID], C)

            def new_w2(ph, b, g):
                pe.wait_ge(u1, b * U1_STEPS + 1)
                u = use(ph, ("U2", 0), "M", 0)
                acquire(u)
                for j in range(C):
                    i = nc.tensor.transpose(psM[:, u.slot, j * P:(j + 1) * P], w2T32[:, j * P:(j + 1) * P], id32[:, :])
                i.then_inc(u.full, 1)

            def new_pg(ph, b, g):
                if ph is setup:
                    pe.wait_ge(d_ready, 1)
                    left, new = dn, w2s
                else:
                    left, new = dd, w2n
                    u = use(ph, ("U2", 0), "M", 0)
                    pe.wait_ge(u.done, u.before + 1)
                    pe.wait_ge(dd_loaded, 32 * b + 16)
                chunked(use(ph, ("U3", 0), "M", 0), left, lambda j: new[:, j, :], C)
                u = use(ph, ("U3", 0), "M", 1)
                acquire(u)
                for j in range(C):
                    i = mm(psM[:, u.slot, 0:HID], new[:, j, :], new[:, j, :], start=(j == 0), stop=(j == C - 1))
                i.then_inc(u.full, 1)

            def pre2(ph, b, g):
                pe.wait_ge(u1, (b + 1) * U1_STEPS)
                u = use(ph, ("A3P", g), "M", 0)
                acquire(u)
                triple(psM[:, u.slot, :], lambda l, c: Aq16[:, l, c, :],
                       lambda r, c: xT1[:, r * C + c, g * GT:(g + 1) * GT], C).then_inc(u.full, 1)

            def mlp_out(name, t):
                def unit(ph, b, g):
                    for c in range(C if ph is first and g + t == 0 else 0):
                        u = use(ph, ("TQT", 0), "M", c)
                        pe.wait_ge(u.done, u.before + 1)
                    u = use(ph, (name, g), "O", 0)
                    acquire(u)
                    tok = slice(g * GT + t * P, g * GT + (t + 1) * P)
                    triple(psO[:, u.slot, :], lambda l, c: xT1[:, l * C + c, tok], lambda r, c: tqT[:, r, c, :], C,
                           closes=False)
                    if t == 0:
                        s = use(ph, ("A3P", g), "S", 0)
                        pe.wait_ge(split, s.before + 1)
                    triple(psO[:, u.slot, :], lambda l, c: h2[:, l, t * P:(t + 1) * P],
                           lambda r, c: w2T16[:, r, :], 1, opened=True).then_inc(u.full, 1)
                return unit

            def queries(name, first_chunk):
                def unit(ph, c_, g):
                    if first_chunk == 0:
                        pe.wait_ge(xt2_loaded[g], TR_STEPS * (c_ + 1))
                    for k in range(2):
                        m = first_chunk + k
                        u = use(ph, (name, g), "M", k)
                        acquire(u)
                        triple(psM[:, u.slot, :], lambda l, c: wqT[:, l, c, m * P:(m + 1) * P],
                               lambda r, c: at_side(xTQ, ph, g)[:, r * C + c, :], C).then_inc(u.full, 1)
                return unit

            def guard(name, first_tile):
                def unit(ph, c_, g):
                    if first_tile == 0:
                        if g == 0:
                            pe.wait_ge(ctx_loaded, 160 * c_ + 160)
                        s = use(ph, ("Qb", g), "S", 1)
                        pe.wait_ge(split, s.before + 1)
                    for k in range(4):
                        t, i = first_tile + k // 2, k % 2
                        u = use(ph, (name, g), "O", k)
                        acquire(u)
                        for j in range(2):
                            m = 2 * i + j
                            mm(psO[:, u.slot, j * 256:(j + 1) * 256], at_side(qs, ph, g)[:, HI, m, t * P:(t + 1) * P],
                               kbd[:, HI, m, :], start=(j == 0), stop=False, skip_group_check=True)
                        mm(psO[:, u.slot, :].rearrange("p (h k) -> p h k", k=KEYS), ones_row[:, :],
                           mrow[:, :].rearrange("p (a k) -> p a k", a=1).broadcast_to([1, 8, KEYS]), start=False,
                           stop=True, skip_group_check=True).then_inc(u.full, 1)
                return unit

            def guard_transposes(ph, c_, g):
                for k in range(2, 4):
                    u = use(ph, ("GUARDb", g), "O", k)
                    pe.wait_ge(u.done, u.before + 1)
                u = use(ph, ("GT", g), "T", 0)
                acquire(u)
                for t in range(T4):
                    i = nc.tensor.transpose(psT[0:HEADS, u.slot, t * P:(t + 1) * P].bitcast(BF16), gm[:, t, :], idbf[:, :])
                i.then_inc(u.full, 1)

            def scores(name, first_pair):
                def unit(ph, c_, g):
                    u = use(ph, ("GT", g), "T", 0)
                    pe.wait_ge(u.done, u.before + 1)
                    for k in range(4):
                        q = first_pair + k
                        m, half = q // 2, slice((q % 2) * P, (q % 2 + 1) * P)
                        u = use(ph, (name, g), "M", k)
                        acquire(u)
                        triple(psM[:, u.slot, :], lambda l, c: kbd[:, l, m, half], lambda r, c: at_side(qs, ph, g)[:, r, m, :], 1,
                               closes=False)
                        mm(psM[:, u.slot, :], neg_ind[:, q * P:(q + 1) * P], at_side(gT, ph, g), start=False,
                           stop=True).then_inc(u.full, 1)
                return unit

            def weighted_values(name, first_tile):
                def unit(ph, c_, g):
                    for k in range(4):
                        t, i = first_tile + k // 2, k % 2
                        u = use(ph, (name, g), "O", k)
                        acquire(u)
                        n = 0
                        for j in range(4):
                            q = 4 * i + j
                            if t == 0:
                                s = use(ph, ("STa" if q < 4 else "STb", g), "S", q % 4)
                                pe.wait_ge(split, s.before + 1)
                            for l, r in PASSES:
                                ins = mm(psO[:, u.slot, j * 66:(j + 1) * 66], es[:, l, q, t * P:(t + 1) * P],
                                         vbd[:, r, q, :], start=(n == 0), stop=(n == 11), skip_group_check=True)
                                n += 1
                        ins.then_inc(u.full, 1)
                return unit

            def ffn1(name, first_chunk):
                def unit(ph, c_, g):
                    for k in range(4):
                        f = first_chunk + k
                        u = use(ph, (name, g), "M", k)
                        waits = [(u.done, u.before)]
                        if f == 0:
                            waits.append((xt3_loaded[g], TR_STEPS * (c_ + 1)))
                            if g == 0:
                                waits += [(done["T"][s], ph.start("T", s)) for s in range(2)]
                        held(pe, waits)
                        for c in range(C):
                            for hl in range(2):
                                i = mm(psM[:, u.slot, :], fw1T[:, c, f * P:(f + 1) * P], xTF[:, hl * C + c, :],
                                       start=(c == 0 and hl == 0), stop=(c == C - 1 and hl == 1))
                        i.then_inc(u.full, 1)
                return unit

            def ffn2(name, half, t):
                def unit(ph, c_, g):
                    u = use(ph, (name, g), "O", 0)
                    for f in range(FCH // 2):
                        waits = [(u.done, u.before)] if f == 0 else []
                        if t == 0:
                            chunk = ("F1" + "abcd"[2 * half + f // 4], g)
                            s = use(ph, chunk, "S", f % 4)
                            waits.append((split, s.before + 1))
                        if waits:
                            held(pe, waits)
                        for hl in range(2):
                            i = mm(psO[:, u.slot, :], hF[:, f, hl, t * P:(t + 1) * P],
                                   fw2T[:, half * FCH // 2 + f, :], start=(f == 0 and hl == 0),
                                   stop=(f == FCH // 2 - 1 and hl == 1))
                    i.then_inc(u.full, 1)
                return unit

            run(pe, {
                "K": gram("K", tk, (ld["tk"], 16)), "KQ": gram("KQ", tq, (ld["tq"], 16)),
                "DT": transposed("DT", dn, (d_ready, 1)), "TQT": transposed("TQT", tq, (ld["tq"], 16)),
                "WQT": transposed("WQT", wqs, (ld["wq"], 16)), "WKT": transposed("WKT", wks, (ld["wk"], 16)),
                "WVT": transposed("WVT", wvs, (ld["wv"], 16)), "CTXT": transposed("CTXT", ctxs, (ld["ctx"], 16)),
                "W1T": w1_transposed, "AINIT": a_init, "W2T0": w2_transposed, "KCTX": keys, "VCTX": values,
                "MEAN": mean, "TTa": ternary("TTa", 0), "TTb": ternary("TTb", 1),
                "PRE": pre, "DHp": residual, "DHg": residual_h, "HTa": h_transposes("HTa", 0),
                "HTb": h_transposes("HTb", 2), "HTc": h_transposes("HTc", 4), "HTd": h_transposes("HTd", 6),
                "S": sums, "U1": update, "U2": new_w2, "U3": new_pg, "A3P": pre2, "Qa": queries("Qa", 0), "Qb": queries("Qb", 2),
                "GUARDa": guard("GUARDa", 0), "GUARDb": guard("GUARDb", 2), "GT": guard_transposes,
                "STa": scores("STa", 0), "STb": scores("STb", 4), "PVa": weighted_values("PVa", 0),
                "PVb": weighted_values("PVb", 2),
                "F1a": ffn1("F1a", 0), "F1b": ffn1("F1b", 4), "F1c": ffn1("F1c", 8), "F1d": ffn1("F1d", 12),
                **{"A3O" + k: mlp_out("A3O" + k, t) for t, k in enumerate("abcd")},
                **{"F2" + k: ffn2("F2" + k, i // T4, i % T4) for i, k in enumerate("abcdefgh")},
            })

        @block.scalar
        def _(act):
            activation = nc.scalar.activation

            def copied(name, dst):
                def unit(ph, b, g):
                    if name == "CTXT":
                        act.wait_ge(ld["small"], 112)
                    if name == "K":
                        act.wait_ge(scr_stored, STORED)
                    if name == "KQ":
                        act.wait_ge(v_split, C)
                    for c in range(C):
                        u = use(ph, (name, 0), "M", c)
                        act.wait_ge(u.full, u.before + 1)
                        activation(dst[:, c, :], psM[:, u.slot, :], ACT.Copy).then_inc(u.done, 1)
                return unit

            def weight_hi(name, dst):
                def unit(ph, b, g):
                    for c in range(C):
                        u = use(ph, (name, 0), "M", c)
                        act.wait_ge(u.full, u.before + 1)
                        activation(dst[:, HI, c, :], psM[:, u.slot, :], ACT.Copy, scale=WSCALE).then_inc(wt_hi, 1)
                return unit

            def one_block(name, dst):
                def unit(ph, b, g):
                    u = use(ph, (name, 0), "M", 0)
                    act.wait_ge(u.full, u.before + 1)
                    activation(dst, psM[:, u.slot, :].rearrange("p (j h) -> p j h", j=C), ACT.Copy).then_inc(u.done, 1)
                return unit

            def magnitudes(ph, b, g):
                if g == 0:
                    u = use(ph, ("VCTX", 0), "M", C - 1)
                else:
                    u = use(ph, ("TTb", 0), "T", 3)
                act.wait_ge(u.full, u.before + 1)
                for half in range(2):
                    act.wait_ge(ld[f"fw{g + 1}_{half}"], 16)
                    if g + half:
                        act.wait_ge(abs_done, 2 * g + half)
                    activation(tern, ffs[half ^ g], ACT.Abs, accum_out=asum[:, g, half:half + 1]).then_inc(abs_done, 1)

            def ternary(name, half):
                def unit(ph, b, g):
                    for k in range(4):
                        u = use(ph, (name, g), "T", k)
                        act.wait_ge(u.full, u.before + 1)
                        if g == 0:
                            f = half * FF // 2 + k * 2 * P
                            dst = fw1T[:, :, f:f + 2 * P]
                            src = psT[:, u.slot, :].rearrange("p (c f) -> p c f", c=C)
                        else:
                            dst = fw2T[:, 4 * k:4 * k + 4, half * D // 2:(half + 1) * D // 2]
                            src = psT[:, u.slot, :].rearrange("p (c f) -> p c f", c=4)
                        activation(dst, src, ACT.Copy, saturate=False).then_inc(u.done, 1)
                return unit

            def stage_free(ph, unit, i):
                s = use(ph, unit, "S", i)
                if not (isinstance(s.before, int) and s.before < RINGS["S"]):
                    act.wait_ge(split, s.before - (RINGS["S"] - 1))
                return stage[:, s.slot, :]

            def normalized(k, name, src):
                def unit(ph, b, g):
                    act.wait_ge(lnp[k], LN_STEPS * (2 * b + g + 1))
                    for t in range(T4):
                        dst = stage_free(ph, (name, g), t)
                        activation(dst, src[:, g * T4 + t, :], ACT.Identity, bias=nm[:, k, g, t:t + 1],
                                   scale=rs[:, k, g, t:t + 1]).then_inc(staged, 1)
                return unit

            def hidden(ph, b, g):
                act.wait_ge(u_step, 6 * b + 3 * g + 3)
                activation(gp[:, g, :], un[:, g, :], ACT.Gelu).then_inc(h_ready, 1)

            def gaussian(ph, b, g):
                for k in range(G2):
                    activation(ee[:, k, :], un[:, k, :], ACT.Square).then_inc(e_step, 1)
                for k in range(G2):
                    act.wait_ge(e_step, 4 * b + k + 1)
                    activation(ee[:, k, :], ee[:, k, :], ACT.Exp, scale=-0.5).then_inc(e_step, 1)

            def token_major(name, first_tile):
                def unit(ph, b, g):
                    for k in range(2):
                        u = use(ph, (name, 0), "T", k)
                        act.wait_ge(u.full, u.before + 1)
                        activation(nat[:, first_tile + k, :, 0:2 * HID],
                                   psT[:, u.slot, 0:4 * P].rearrange("p (a d) -> p a d", a=2), ACT.Copy).then_inc(u.done, 1)
                return unit

            def new_hidden(ph, b, g):
                u = use(ph, ("A3P", g), "M", 0)
                act.wait_ge(u.full, u.before + 1)
                dst = stage_free(ph, ("A3P", g), 0)
                activation(dst, psM[:, u.slot, :], ACT.Gelu, bias=b1c[:, :], scale=1.0 / WSCALE).then_inc(u.done, 1)

            def queries(name, first_chunk):
                def unit(ph, c_, g):
                    for k in range(2):
                        m = first_chunk + k
                        u = use(ph, (name, g), "M", k)
                        act.wait_ge(u.full, u.before + 1)
                        dst = stage_free(ph, (name, g), k)
                        activation(dst, psM[:, u.slot, :], ACT.Identity, bias=bqc[:, m:m + 1],
                                   scale=1.0 / WSCALE).then_inc(u.done, 1)
                return unit

            def guard_rows(ph, c_, g):
                u = use(ph, ("GT", g), "T", 0)
                act.wait_ge(u.full, u.before + 1)
                activation(at_side(gT, ph, g), psT[0:HEADS, u.slot, 0:GT].bitcast(BF16), ACT.Copy).then_inc(u.done, 1)

            def exponentials(name):
                def unit(ph, c_, g):
                    for k in range(4):
                        u = use(ph, (name, g), "M", k)
                        act.wait_ge(u.full, u.before + 1)
                        dst = stage_free(ph, (name, g), k)
                        activation(dst, psM[:, u.slot, :], ACT.Exp, bias=mbc[:, :], scale=1.0 / SQW).then_inc(u.done, 1)
                return unit

            def ffn_hidden(name, first_chunk):
                def unit(ph, c_, g):
                    for k in range(4):
                        f = first_chunk + k
                        u = use(ph, (name, g), "M", k)
                        act.wait_ge(u.full, u.before + 1)
                        dst = stage_free(ph, (name, g), k)
                        activation(dst, psM[:, u.slot, :], ACT.Gelu, bias=fb1c[:, f:f + 1]).then_inc(u.done, 1)
                return unit

            run(act, {
                "K": copied("K", kk), "KQ": copied("KQ", kq), "DT": copied("DT", dd), "TQT": weight_hi("TQT", tqT),
                "W1T": one_block("W1T", w1T), "WQT": weight_hi("WQT", wqT), "WKT": copied("WKT", wkT),
                "WVT": copied("WVT", wvT), "CTXT": copied("CTXT", ctxT), "ABS": magnitudes,
                "TTa": ternary("TTa", 0), "TTb": ternary("TTb", 1),
                "L1b": normalized(0, "L1b", xin), "L2b": normalized(1, "L2b", x1), "L3b": normalized(2, "L3b", x1),
                "PRE": hidden, "PRG": gaussian, "HTa": token_major("HTa", 0), "HTb": token_major("HTb", 2), "HTc": token_major("HTc", 4),
                "HTd": token_major("HTd", 6), "U2": one_block("U2", w2n), "A3P": new_hidden, "Qa": queries("Qa", 0),
                "Qb": queries("Qb", 2), "GT": guard_rows, "STa": exponentials("STa"), "STb": exponentials("STb"),
                "F1a": ffn_hidden("F1a", 0), "F1b": ffn_hidden("F1b", 4), "F1c": ffn_hidden("F1c", 8),
                "F1d": ffn_hidden("F1d", 12),
            })

        @block.gpsimd
        def _(pool):
            for m in (id16, idbf, id32):
                nc.gpsimd.memset(m[:, :], 0.0).then_inc(idents, 1)
            pool.wait_ge(idents, 3)
            for m in (id16, idbf, id32):
                nc.gpsimd.affine_select(out=m[:, :], in_=m[:, :], compare_op=ALU.not_equal, fill=1.0, base=0,
                                        pattern=[[-1, P]], channel_multiplier=1).then_inc(idents, 1)
            nc.gpsimd.memset(ones_row[:, :], 1.0).then_inc(consts, 1)
            nc.gpsimd.memset(ones_col[:, :], 1.0).then_inc(consts, 1)
            nc.gpsimd.memset(neghalf[:, :], -0.5).then_inc(consts, 1)
            nc.gpsimd.memset(minus1[:, :], -1.0).then_inc(consts, 1)
            nc.gpsimd.memset(eps[:, :], EPS).then_inc(consts, 1)
            nc.gpsimd.memset(neg_ind[:, :], -1.0).then_inc(consts, 1)
            nc.gpsimd.memset(kbd[:, :, :, :], 0.0).then_inc(consts, 1)
            nc.gpsimd.memset(vbd[:, :, :, :], 0.0).then_inc(consts, 1)
            pool.wait_ge(consts, 8)
            for j in range(2):
                one = j * (W + 1) + W
                nc.gpsimd.memset(vbd[j * KEYS:(j + 1) * KEYS, HI, :, one:one + 1], 1.0).then_inc(consts, 1)
            nc.gpsimd.affine_select(out=neg_ind[:, :], in_=neg_ind[:, :], compare_op=ALU.is_ge, fill=0.0, base=0,
                                    pattern=[[1, PAIRS * P]], channel_multiplier=-KEYS).then_inc(consts, 1)
            pool.wait_ge(consts, 11)
            nc.gpsimd.affine_select(out=neg_ind[:, :], in_=neg_ind[:, :], compare_op=ALU.is_ge, fill=0.0,
                                    base=KEYS - 1, pattern=[[-1, PAIRS * P]], channel_multiplier=KEYS).then_inc(consts, 1)
            pool.wait_ge(ld["small"], 112)
            pool.wait_ge(consts, CONSTS)

            def rsqrt(k):
                def unit(ph, b, g):
                    tt, at = nc.gpsimd.tensor_tensor, LN_STEPS * (2 * b + g)
                    pool.wait_ge(stats[k], 2 * b + g + 1)
                    tt(ve[:, k, :], mv[:, k, :, 1], eps[:, :], ALU.add).then_inc(lnp[k], 1)
                    tt(nm[:, k, g, :], mv[:, k, :, 0], minus1[:, :], ALU.mult).then_inc(lnp[k], 1)
                    pool.wait_ge(lnp[k], at + 1)
                    tt(rs[:, k, g, :], ve[:, k, :], neghalf[:, :], ALU.pow).then_inc(lnp[k], 1)
                    pool.wait_ge(lnp[k], at + 3)
                    tt(nm[:, k, g, :], nm[:, k, g, :], rs[:, k, g, :], ALU.mult).then_inc(lnp[k], 1)
                return unit

            def add_b2(ph, b, g):
                if g == 0:
                    pool.wait_ge(u1, b * U1_STEPS + 2)
                for t in range(T4):
                    xt = xin[:, g * T4 + t, :]
                    nc.gpsimd.tensor_tensor(xt, xt, b2b[:, :], ALU.add).then_inc(xa_done, 1)

            def add_attention(name, first_tile):
                def unit(ph, c_, g):
                    for k in range(4):
                        u = use(ph, (name, g), "O", k)
                        pool.wait_ge(u.done, u.before + 1)
                        xt = x1[:, g * T4 + first_tile + k // 2, k % 2 * 256:(k % 2 + 1) * 256]
                        nc.gpsimd.tensor_tensor(xt, xt, obuf[:, k % 2, :, :].rearrange("p h w -> p (h w)"),
                                                ALU.add).then_inc(o_done, 1)
                return unit

            def add_fb2(ph, c_, g):
                for t in range(T4):
                    s = use(ph, ("L3b", g), "S", t)
                    pool.wait_ge(hi_done, s.before + 1)
                    xt = x1[:, g * T4 + t, :]
                    nc.gpsimd.tensor_tensor(xt, xt, fb2b[:, :], ALU.add).then_inc(xf_done, 1)

            run(pool, {"L1a": rsqrt(0), "L2a": rsqrt(1), "L3a": rsqrt(2), "A3P": add_b2,
                       "PVa": add_attention("PVa", 0), "PVb": add_attention("PVb", 2), "T3": add_fb2})

        @block.vector
        def _(dve):
            v = nc.vector

            def d_matrix(ph, b, g):
                dve.wait_ge(ld["tk"], 16)
                dve.wait_ge(ld["tv"], 16)
                v.tensor_tensor(dn, tk, dn, ALU.subtract).then_inc(d_ready, 1)

            def masks(ph, b, g):
                dve.wait_ge(ld["mask"], 48)
                v.tensor_copy(mf, mi).then_inc(mask_step, 1)
                v.tensor_copy(mcf[:, :], mci[:, :]).then_inc(mask_step, 1)
                dve.wait_ge(mask_step, 2)
                mfb = mf.rearrange("p (b k) -> p b k", b=B)
                v.tensor_reduce(mx[:, :], mfb, AX.X, ALU.max).then_inc(mask_step, 1)
                dve.wait_ge(mask_step, 3)
                v.tensor_tensor(mcf[:, :], mcf[:, :], mx[:, :], ALU.subtract).then_inc(mask_step, 1)
                v.tensor_tensor(mfb[0:1], mfb[0:1], mx[0:1, :].rearrange("p (b a) -> p b a", a=1).broadcast_to([1, B, KEYS]),
                                ALU.subtract).then_inc(mask_step, 1)
                dve.wait_ge(mask_step, 5)
                v.tensor_scalar(mcf[:, :], mcf[:, :], MASKED, None, ALU.mult).then_inc(mask_step, 1)
                v.tensor_scalar(mr16[:, :, :], mfb[0:1], MASKED * SQW, -60000.0, ALU.mult, ALU.max).then_inc(mask_step, 1)

            weights_seen = [0]

            def weight_lo(name, dst):
                def unit(ph, b, g):
                    for c in range(C):
                        u = use(ph, (name, 0), "M", c)
                        weights_seen[0] += 1
                        dve.wait_ge(wt_hi, weights_seen[0])
                        v.scalar_tensor_tensor(out=dst[:, LO, c, :], in0=psM[:, u.slot, :], scalar=WSCALE,
                                               in1=dst[:, HI, c, :], op0=ALU.mult, op1=ALU.subtract).then_inc(u.done, 1)
                return unit

            def flat(ap):
                return ap.rearrange("p c h -> p (c h)")

            def a_init(ph, b, g):
                dve.wait_ge(ld["small"], 112)
                step = 0
                for k, (f32, f16, scale) in enumerate(((A32, A16, 1.0), (Aq32, Aq16, WSCALE))):
                    u = use(ph, ("AINIT", 0), "M", k)
                    dve.wait_ge(u.full, u.before + 1)
                    v.tensor_copy(flat(f32[:, :, :]), psM[:, u.slot, :]).then_inc(u.done, 1)
                    dve.wait_ge(u.done, u.before + 1)
                    v.tensor_scalar(f16[:, HI], f32[:, :, :], scale, None, ALU.mult).then_inc(init, 1)
                    dve.wait_ge(init, step + 1)
                    v.scalar_tensor_tensor(out=f16[:, LO], in0=f32[:, :, :], scalar=scale, in1=f16[:, HI],
                                           op0=ALU.mult, op1=ALU.subtract).then_inc(init, 1)
                    step += 2

            def w2_init(ph, b, g):
                u = use(ph, ("W2T0", 0), "M", 0)
                dve.wait_ge(u.full, u.before + 1)
                v.tensor_copy(w2T32[:, :], psM[:, u.slot, :]).then_inc(u.done, 1)
                dve.wait_ge(u.done, u.before + 1)
                v.tensor_scalar(w2T16[:, HI], w2T32[:, :], WSCALE, None, ALU.mult).then_inc(init, 1)
                dve.wait_ge(init, 5)
                v.scalar_tensor_tensor(out=w2T16[:, LO], in0=w2T32[:, :], scalar=WSCALE, in1=w2T16[:, HI],
                                       op0=ALU.mult, op1=ALU.subtract).then_inc(init, 1)
                v.tensor_tensor_reduce(out=cjunk, in0=w2T32[:, :],
                                       in1=b2b[:, :], scale=1.0, scalar=0.0, op0=ALU.mult, op1=ALU.add,
                                       accum_out=cc[:, :]).then_inc(init, 1)

            def new_pg(ph, b, g):
                at = 0 if ph is setup else 2 * b + 2
                for k, (dst, cols) in enumerate(((P16, C * HID), (G16, HID))):
                    u = use(ph, ("U3", 0), "M", k)
                    dve.wait_ge(u.full, u.before + 1)
                    hi = dst[:, HI] if k else flat(dst[:, HI])
                    lo = dst[:, LO] if k else flat(dst[:, LO])
                    v.tensor_copy(hi, psM[:, u.slot, 0:cols]).then_inc(u3, 1)
                    dve.wait_ge(u3, at + k + 1)
                    v.tensor_tensor(lo, psM[:, u.slot, 0:cols], hi, ALU.subtract).then_inc(u.done, 1)
                if ph is setup:
                    for k in range(2):
                        u = use(ph, ("U3", 0), "M", k)
                        dve.wait_ge(u.done, u.before + 1)

            def keys(ph, b, g):
                dve.wait_ge(mr_stored, 16)
                for m in range(C):
                    u = use(ph, ("KCTX", 0), "M", m)
                    dve.wait_ge(u.full, u.before + 1)
                    v.tensor_scalar(kTs[:, HI, m, :], psM[:, u.slot, :], bkc[:, m:m + 1], None, ALU.add).then_inc(kv_hi, 1)
                    dve.wait_ge(kv_hi, m + 1)
                    v.scalar_tensor_tensor(out=kTs[:, LO, m, :], in0=psM[:, u.slot, :], scalar=bkc[:, m:m + 1],
                                           in1=kTs[:, HI, m, :], op0=ALU.add, op1=ALU.subtract).then_inc(u.done, 1)

            def values(ph, b, g):
                for r in range(C):
                    u = use(ph, ("VCTX", 0), "M", r)
                    dve.wait_ge(u.full, u.before + 1)
                    if r:
                        dve.wait_ge(v_split, r)
                    v.tensor_tensor(v32, psM[:, u.slot, :], bvb, ALU.add).then_inc(u.done, 1)
                    dve.wait_ge(u.done, u.before + 1)
                    v.tensor_copy(vs[:, r, HI, :], v32).then_inc(kv_hi, 1)
                    dve.wait_ge(kv_hi, C + r + 1)
                    v.tensor_tensor(vs[:, r, LO, :], v32, vs[:, r, HI, :], ALU.subtract).then_inc(v_split, 1)

            def threshold(ph, b, g):
                u = use(ph, ("MEAN", g), "M", 0)
                dve.wait_ge(u.full, u.before + 1)
                v.tensor_scalar(thr[:, g, 0:1], psM[:, u.slot, 0:1], 1.0 / (FF * D), 1e-8, ALU.mult,
                                ALU.max).then_inc(u.done, 1)
                dve.wait_ge(u.done, u.before + 1)
                v.tensor_scalar(thr[:, g, 1:2], thr[:, g, 0:1], 0.5, None, ALU.mult).then_inc(thr_step, 1)
                v.tensor_scalar(thr[:, g, 2:3], thr[:, g, 0:1], -0.5, None, ALU.mult).then_inc(thr_step, 1)

            def ternary(name, half):
                def unit(ph, b, g):
                    w, at = ffs[half ^ g], 4 * g + 2 * half
                    dve.wait_ge(thr_step, 2 * g + 2)
                    if half:
                        for k in range(2, 4):
                            u = use(ph, ("TTa", g), "T", k)
                            dve.wait_ge(u.full, u.before + 1)
                    v.tensor_scalar(tern, w, thr[:, g, 2:3], None, ALU.is_lt).then_inc(tern_step, 1)
                    dve.wait_ge(tern_step, at + 1)
                    v.scalar_tensor_tensor(out=tern, in0=w, scalar=thr[:, g, 1:2], in1=tern, op0=ALU.is_gt,
                                           op1=ALU.subtract).then_inc(tern_step, 1)
                return unit

            def split_stage(s, hi, lo):
                src = stage[:, s.slot, :]
                v.tensor_copy(hi, src).then_inc(hi_done, 1)
                dve.wait_ge(hi_done, s.before + 1)
                v.tensor_tensor(lo, src, hi, ALU.subtract).then_inc(split, 1)

            def moments(k, name, src):
                def unit(ph, b, g):
                    if name == "L1a":
                        dve.wait_ge(x_loaded[g], 16 * b + 16)
                    elif name == "L3a":
                        dve.wait_ge(o_done, 16 * b + 8 * g + 8)
                    elif g == 0:
                        for q in "cd":
                            u = use(ph, ("A3O" + q, 0), "O", 0)
                            dve.wait_ge(u.done, u.before + 1)
                    else:
                        for s in range(2):
                            dve.wait_ge(done["O"][s], ph.start("O", s))
                    for t in range(T4):
                        i = v.bn_stats(st[:, k, t, :], src[:, g * T4 + t, :])
                    i.then_inc(bn[k], 1)
                    held(dve, [(bn[k], 2 * b + g + 1)])
                    for t in range(T4):
                        i = v.bn_aggr(mv[:, k, t, :], st[:, k, t, :])
                    i.then_inc(stats[k], 1)
                return unit

            def normalized(name, dst):
                def unit(ph, b, g):
                    if ph is first and name == "L2b":
                        dve.wait_ge(scr_stored, STORED)
                    for t in range(T4):
                        dve.wait_ge(staged, staged_before(ph, (name, g)) + t + 1)
                        split_stage(use(ph, (name, g), "S", t), dst(g, t, HI), dst(g, t, LO))
                return unit

            LN_ORDER = [(ph, [u for u in ph.order if u[0] in ("L1b", "L2b", "L3b")])
                        for ph in (setup, first, body, last)]

            def staged_before(ph, unit):
                n = 0
                for p, order in LN_ORDER:
                    if p is ph:
                        turns = p.turn if p is body else 0
                        return turns * (T4 * len(order)) + n + T4 * order.index(unit)
                    n += T4 * len(order) * (B - 1 if p is body else 1)

            def hidden(ph, b, g):
                u = use(ph, ("PRE", g), "M", 0)
                dve.wait_ge(u.full, u.before + 1)
                v.tensor_scalar(un[:, g, :], psM[:, u.slot, :], b1c[:, :], None, ALU.add).then_inc(u.done, 1)
                dve.wait_ge(u.done, u.before + 1)
                v.tensor_tensor(ee[:, g, :], un[:, g, :], un[:, g, :], ALU.mult).then_inc(u_step, 1)
                dve.wait_ge(u_step, 6 * b + 3 * g + 1)
                v.tensor_scalar(ee[:, g, :], ee[:, g, :], TINY * TINY, 4 * TINY, ALU.is_le, ALU.mult).then_inc(u_step, 1)
                dve.wait_ge(u_step, 6 * b + 3 * g + 2)
                v.tensor_tensor(un[:, g, :], ee[:, g, :], un[:, g, :], ALU.add).then_inc(u_step, 1)
                dve.wait_ge(h_ready, 2 * b + g + 1)
                v.tensor_copy(hT[:, g, HI, :], gp[:, g, :]).then_inc(h_hi, 1)
                dve.wait_ge(u_step, 6 * b + 3 * g + 3)
                dve.wait_ge(h_hi, 2 * b + g + 1)
                v.tensor_tensor(hT[:, g, LO, :], gp[:, g, :], hT[:, g, HI, :], ALU.subtract).then_inc(h_split, 1)
                v.reciprocal(ru[:, g, :], un[:, g, :]).then_inc(ru_step, 1)
                dve.wait_ge(ru_step, 4 * b + 2 * g + 1)
                v.tensor_tensor(ru[:, g, :], gp[:, g, :], ru[:, g, :], ALU.mult).then_inc(ru_step, 1)

            def slope(ph, b, g):
                dve.wait_ge(ru_step, 4 * b + 4)
                for k in range(G2):
                    dve.wait_ge(e_step, 4 * b + k + 3)
                    v.scalar_tensor_tensor(out=ee[:, k, :], in0=ee[:, k, :], scalar=INV_SQRT_2PI, in1=un[:, k, :],
                                           op0=ALU.mult, op1=ALU.mult).then_inc(gp_step, 1)
                    dve.wait_ge(gp_step, 2 * b + k + 1)
                    v.tensor_tensor(gp[:, k, :], ru[:, k, :], ee[:, k, :], ALU.add).then_inc(gp_ready, 1)

            def hidden_gradient(ph, b, g):
                dve.wait_ge(gp_ready, 2 * b + 2)
                v.memset(nat[:, :, HI, 2 * HID:2 * HID + 2], 1.0).then_inc(ones_set, 1)
                if ph is body:
                    dve.wait_ge(u1, b * U1_STEPS)
                for k in range(G2):
                    u = use(ph, ("DHp", 0), "M", k)
                    dve.wait_ge(u.full, u.before + 1)
                    v.scalar_tensor_tensor(out=gp[:, k, :], in0=psM[:, u.slot, :], scalar=cc[:, :], in1=gp[:, k, :],
                                           op0=ALU.add, op1=ALU.mult).then_inc(u.done, 1)
                    dve.wait_ge(u.done, u.before + 1)
                    v.tensor_copy(dpT[:, k, HI, :], gp[:, k, :]).then_inc(dp_hi, 1)
                    dve.wait_ge(dp_hi, 2 * b + k + 1)
                    v.tensor_tensor(dpT[:, k, LO, :], gp[:, k, :], dpT[:, k, HI, :], ALU.subtract).then_inc(dp_split, 1)

            def sums(ph, b, g):
                u = use(ph, ("S", 0), "M", 0)
                dve.wait_ge(u.full, u.before + 1)
                v.tensor_copy(s3[:, 0:HID + 1], psM[:, u.slot, 0:HID + 1])
                v.tensor_copy(s3[:, HID + 2:HID + 3], psM[:, u.slot, HID + 2:HID + 3]).then_inc(u.done, 1)
                dve.wait_ge(u.done, u.before + 1)
                v.tensor_copy(s4b, s3[:, HID:HID + 1].broadcast_to([P, P])).then_inc(bc_ready, 1)
                for c in range(C):
                    u = use(ph, ("S", 0), "M", 1 + c)
                    dve.wait_ge(u.full, u.before + 1)
                    v.tensor_copy(s12[:, c, 0:2 * HID + 1], psM[:, u.slot, 0:2 * HID + 1]).then_inc(u.done, 1)
                dve.wait_ge(u.done, u.before + 1)
                v.tensor_copy(sxb, s12[:, :, 2 * HID:2 * HID + 1].broadcast_to([P, C, P])).then_inc(bc_ready, 1)

            def update(ph, b, g):
                at = b * U1_STEPS
                m = [use(ph, ("U1", 0), "M", k) for k in range(4)]
                dve.wait_ge(m[0].full, m[0].before + 1)
                v.scalar_tensor_tensor(out=tw, in0=b2b[:, :], scalar=s3[:, HID:HID + 1], in1=psM[:, m[0].slot, :],
                                       op0=ALU.mult, op1=ALU.add).then_inc(m[0].done, 1)
                dve.wait_ge(m[1].full, m[1].before + 1)
                v.scalar_tensor_tensor(out=tb, in0=b2b[:, :], scalar=float(N), in1=psM[:, m[1].slot, :],
                                       op0=ALU.mult, op1=ALU.add).then_inc(m[1].done, 1)
                dve.wait_ge(m[0].done, m[0].before + 1)
                v.scalar_tensor_tensor(out=w2T32[:, :], in0=tw, scalar=-ETA, in1=w2T32[:, :], op0=ALU.mult,
                                       op1=ALU.add).then_inc(u1, 1)
                dve.wait_ge(m[1].done, m[1].before + 1)
                v.scalar_tensor_tensor(out=b2b[:, :], in0=tb, scalar=-ETA, in1=b2b[:, :], op0=ALU.mult,
                                       op1=ALU.add).then_inc(u1, 1)
                v.scalar_tensor_tensor(out=b1c[:, :], in0=s3[:, HID + 2:HID + 3], scalar=-ETA, in1=b1c[:, :],
                                       op0=ALU.mult, op1=ALU.add).then_inc(u1, 1)
                dve.wait_ge(u1, at + 2)
                v.tensor_scalar(w2T16[:, HI], w2T32[:, :], WSCALE, None, ALU.mult).then_inc(u1, 1)
                v.tensor_tensor_reduce(out=tw, in0=w2T32[:, :], in1=b2b[:, :], scale=1.0, scalar=0.0, op0=ALU.mult,
                                       op1=ALU.add, accum_out=cc[:, :]).then_inc(u1, 1)
                dve.wait_ge(u1, at + 4)
                v.scalar_tensor_tensor(out=w2T16[:, LO], in0=w2T32[:, :], scalar=WSCALE, in1=w2T16[:, HI],
                                       op0=ALU.mult, op1=ALU.subtract).then_inc(u1, 1)
                for k, (f32, f16, scale) in enumerate(((A32, A16, 1.0), (Aq32, Aq16, WSCALE))):
                    r = m[2 + k]
                    dve.wait_ge(r.full, r.before + 1)
                    v.scalar_tensor_tensor(out=flat(f32[:, :, :]), in0=psM[:, r.slot, :], scalar=-ETA,
                                           in1=flat(f32[:, :, :]), op0=ALU.mult, op1=ALU.add).then_inc(r.done, 1)
                    dve.wait_ge(r.done, r.before + 1)
                    v.tensor_scalar(f16[:, HI], f32[:, :, :], scale, None, ALU.mult).then_inc(u1, 1)
                    dve.wait_ge(u1, at + 7 + 2 * k)
                    v.scalar_tensor_tensor(out=f16[:, LO], in0=f32[:, :, :], scalar=scale, in1=f16[:, HI],
                                           op0=ALU.mult, op1=ALU.subtract).then_inc(u1, 1)

            def new_hidden(ph, b, g):
                u = use(ph, ("A3P", g), "M", 0)
                dve.wait_ge(u.done, u.before + 1)
                split_stage(use(ph, ("A3P", g), "S", 0), h2[:, HI, :], h2[:, LO, :])

            def add_mlp(name, t):
                def unit(ph, b, g):
                    tile = g * T4 + t
                    u = use(ph, (name, g), "O", 0)
                    dve.wait_ge(u.full, u.before + 1)
                    dve.wait_ge(xa_done, TILES * b + tile + 1)
                    if ph is body:
                        dve.wait_ge(out_stored[tile], 16 * b)
                    v.scalar_tensor_tensor(out=x1[:, tile, :], in0=psO[:, u.slot, :], scalar=1.0 / WSCALE,
                                           in1=xin[:, tile, :], op0=ALU.mult, op1=ALU.add).then_inc(u.done, 1)
                return unit

            def queries(name, first_chunk):
                def unit(ph, c_, g):
                    for k in range(2):
                        m = first_chunk + k
                        u = use(ph, (name, g), "M", k)
                        dve.wait_ge(u.done, u.before + 1)
                        split_stage(use(ph, (name, g), "S", k), at_side(qs, ph, g)[:, HI, m, :], at_side(qs, ph, g)[:, LO, m, :])
                return unit

            def guard(name, first_tile):
                def unit(ph, c_, g):
                    for k in range(4):
                        u = use(ph, (name, g), "O", k)
                        dve.wait_ge(u.full, u.before + 1)
                        v.tensor_reduce(gm[:, first_tile + k // 2, (k % 2) * 8:(k % 2) * 8 + 8],
                                        psO[:, u.slot, :].rearrange("p (h k) -> p h k", k=KEYS), AX.X,
                                        ALU.max).then_inc(u.done, 1)
                return unit

            def exponentials(name, first_pair):
                def unit(ph, c_, g):
                    for k in range(4):
                        u = use(ph, (name, g), "M", k)
                        dve.wait_ge(u.done, u.before + 1)
                        split_stage(use(ph, (name, g), "S", k), es[:, HI, first_pair + k, :], es[:, LO, first_pair + k, :])
                return unit

            def normalize(name, first_tile):
                def unit(ph, c_, g):
                    for k in range(4):
                        u = use(ph, (name, g), "O", k)
                        i, nth = k % 2, 2 * first_tile + k
                        dve.wait_ge(u.full, u.before + 1)
                        heads = psO[:, u.slot, 0:8 * (W + 1)].rearrange("p (h w) -> p h w", w=W + 1)
                        v.reciprocal(rden[:, i, :], heads[:, :, W]).then_inc(rd, 1)
                        dve.wait_ge(rd, 16 * c_ + 8 * g + nth + 1)
                        if nth >= 2:
                            dve.wait_ge(o_done, 16 * c_ + 8 * g + nth - 1)
                        v.tensor_tensor(obuf[:, i, :, :], heads[:, :, 0:W],
                                        rden[:, i, :].rearrange("p (h a) -> p h a", a=1).broadcast_to([P, 8, W]),
                                        ALU.mult).then_inc(u.done, 1)
                return unit

            def ffn_hidden(name, first_chunk):
                def unit(ph, c_, g):
                    for k in range(4):
                        u = use(ph, (name, g), "M", k)
                        f = (first_chunk + k) % (FCH // 2)
                        dve.wait_ge(u.done, u.before + 1)
                        split_stage(use(ph, (name, g), "S", k), hF[:, f, HI, :], hF[:, f, LO, :])
                return unit

            def add_ffn(name, half, t):
                def unit(ph, c_, g):
                    tile = g * T4 + t
                    u = use(ph, (name, g), "O", 0)
                    dve.wait_ge(u.full, u.before + 1)
                    if half == 0:
                        dve.wait_ge(xf_done, TILES * c_ + tile + 1)
                    else:
                        before = use(ph, ("F2" + "abcd"[t], g), "O", 0)
                        dve.wait_ge(before.done, before.before + 1)
                    v.tensor_tensor(x1[:, tile, :], psO[:, u.slot, :], x1[:, tile, :], ALU.add).then_inc(u.done, 1)
                return unit

            run(dve, {
                "D": d_matrix, "DT": masks, "TQT": weight_lo("TQT", tqT), "AINIT": a_init, "W2T0": w2_init, "U3": new_pg,
                "WQT": weight_lo("WQT", wqT), "KCTX": keys, "VCTX": values, "MEAN": threshold,
                "TERa": ternary("TERa", 0), "TERb": ternary("TERb", 1),
                "L1a": moments(0, "L1a", xin), "L2a": moments(1, "L2a", x1), "L3a": moments(2, "L3a", x1),
                "L1b": normalized("L1b", lambda g, t, hl: xn1[:, hl, g * T4 + t, :]),
                "L2b": normalized("L2b", lambda g, t, hl: xnX[:, hl, t, :]),
                "L3b": normalized("L3b", lambda g, t, hl: xnX[:, hl, t, :]),
                "PRE": hidden, "PRG": slope, "DHg": hidden_gradient, "S": sums, "U1": update,
                "A3P": new_hidden,
                "Qa": queries("Qa", 0), "Qb": queries("Qb", 2), "GUARDa": guard("GUARDa", 0), "GUARDb": guard("GUARDb", 2),
                "STa": exponentials("STa", 0), "STb": exponentials("STb", 4), "PVa": normalize("PVa", 0),
                "PVb": normalize("PVb", 2),
                "F1a": ffn_hidden("F1a", 0), "F1b": ffn_hidden("F1b", 4), "F1c": ffn_hidden("F1c", 8),
                "F1d": ffn_hidden("F1d", 12),
                **{"A3O" + k: add_mlp("A3O" + k, t) for t, k in enumerate("abcd")},
                **{"F2" + k: add_ffn("F2" + k, i // T4, i % T4) for i, k in enumerate("abcdefgh")},
            })


_INS = ["x", "ctx_1024", "mask_BxS2_ik0", "L0_attn_t_k", "L0_attn_t_v", "L0_attn_t_q", "L0_attn_W1", "L0_attn_b1",
        "L0_attn_W2", "L0_attn_b2", "L0_xattn_Wq", "L0_xattn_bq", "L0_xattn_Wk", "L0_xattn_bk", "L0_xattn_Wv",
        "L0_xattn_bv", "L0_ffn_W1", "L0_ffn_b1", "L0_ffn_W2", "L0_ffn_b2"]


def kernel(**inputs):
    import numpy as _np
    import concourse.bacc as _bacc
    from concourse import mybir as _mybir
    from concourse.bass_utils import run_bass_kernel_spmd as _run

    nc = _bacc.Bacc("TRN2", target_bir_lowering=False, num_devices=1)
    arrays, args = {}, []
    for name in _INS:
        a = _np.ascontiguousarray(inputs[name])
        arrays[f"in_{name}_dram"] = a
        args.append(nc.dram_tensor(f"in_{name}_dram", a.shape, _mybir.dt.from_np(a.dtype), kind="ExternalInput").ap())
    args.append(nc.dram_tensor("out_0_dram", (B, N, D), F32, kind="ExternalOutput").ap())
    build(nc, *args)
    r = _run(nc, [arrays], core_ids=[0])
    return r.results[0]["out_0_dram"]
```
